# Optimizing a Trainium2 kernel written in Bass

```python
import numpy as np
import jax
import jax.numpy as jnp

def _softmax(x, axis=-1):
    return jax.nn.softmax(x, axis=axis)

def _gelu(x):
    return jax.nn.gelu(x, approximate=True)

def _silu(x):
    return jax.nn.silu(x)

def _sigmoid(x):
    return jax.nn.sigmoid(x)

def _layernorm(x, axis=-1, eps=1e-05):
    m = jnp.mean(x, axis=axis, keepdims=True)
    v = jnp.var(x, axis=axis, keepdims=True)
    return (x - m) / jnp.sqrt(v + eps)

def _scatter_add(tgt, idx, src, axis=0):
    return tgt.at[idx].add(src)

def _segment_sum(src, seg, n):
    return jax.ops.segment_sum(src, seg, n)
kernel_name = 'mk_lm_tower_d1_tok_ids256_r4_9adb26'

def setup_inputs(seed: int=0):
    np.random.seed(seed)
    _w = jnp.asarray

    def _rec_inputs():
        import jax
        import jax.numpy as jnp
        _rk = jax.random.key(seed)
        x = jax.random.randint(jax.random.fold_in(_rk, 1), (32, 256), 0, 50226, jnp.int32)
        return x
    x = _rec_inputs()

    def _L0_tok_setup():
        import jax, jax.numpy as jnp
        import numpy as np
        VOCAB = 50257
        EMBED = 64
        NFREQ = 64
        NRULES = 100
        B, S = (4, 256)
        key = jax.random.key(seed)
        ks = jax.random.split(key, 7)
        return {'token_ids': jax.random.randint(ks[0], (B, S), 0, VOCAB), 'a_n': jax.random.normal(ks[1], (VOCAB, NFREQ), dtype=jnp.float32), 'b_n': jax.random.normal(ks[2], (VOCAB, NFREQ), dtype=jnp.float32), 'rule_transform': jax.random.normal(ks[3], (NRULES, EMBED, EMBED), dtype=jnp.float32), 'token_rules': jax.random.randint(ks[4], (VOCAB,), 0, NRULES), 'proj_w': jax.random.normal(ks[5], (EMBED, NFREQ), dtype=jnp.float32) * (1.0 / np.sqrt(NFREQ)), 'proj_b': jax.random.normal(ks[6], (EMBED,), dtype=jnp.float32) * 0.01}
    _L0_tok_all = _L0_tok_setup()
    _L0_tok_in = {k: v for k, v in _L0_tok_all.items() if k in ('a_n', 'b_n', 'rule_transform', 'token_rules', 'proj_w', 'proj_b')}
    del _L0_tok_all

    def _L0_attn_setup():
        import jax, jax.numpy as jnp
        import numpy as np
        HEADS, DIM_HEAD = (8, 64)
        EPS = 1e-05

        def instance_norm(t):
            mu = jnp.mean(t, axis=-1, keepdims=True)
            var = jnp.mean((t - mu) ** 2, axis=-1, keepdims=True)
            return (t - mu) * jax.lax.rsqrt(var + EPS)
        key = jax.random.key(seed)
        k1, k2, k3, k4 = jax.random.split(key, 4)
        B, N, D = (8, 2048, 64)
        inner = HEADS * DIM_HEAD
        x = jax.random.normal(k1, (B, N, D), jnp.float32)
        w_qkv = jax.random.normal(k2, (3 * inner, D), jnp.float32) / np.sqrt(D).astype(np.float32)
        w_out = jax.random.normal(k3, (D, inner), jnp.float32) / np.sqrt(inner).astype(np.float32)
        b_out = 0.01 * jax.random.normal(k4, (D,), jnp.float32)
        return {'x': x, 'w_qkv': w_qkv, 'w_out': w_out, 'b_out': b_out}
    _L0_attn_all = _L0_attn_setup()
    _L0_attn_in = {k: v for k, v in _L0_attn_all.items() if k in ('w_qkv', 'w_out', 'b_out')}
    del _L0_attn_all

    def _L0_ffn_setup():
        import jax, jax.numpy as jnp
        import numpy as np
        B, S, D, E, H, K = (4, 1024, 64, 8, 128, 2)
        key = jax.random.key(seed)
        ks = jax.random.split(key, 6)
        x = jax.random.normal(ks[0], (B, S, D), jnp.float32)
        Wg = jax.random.normal(ks[1], (D, E), jnp.float32) * 0.02
        bg = jnp.zeros((E,), jnp.float32)
        W1 = jax.random.normal(ks[2], (E, D, H), jnp.float32) * 0.02
        b1 = jnp.zeros((E, H), jnp.float32)
        W2 = jax.random.normal(ks[3], (E, H, D), jnp.float32) * 0.02
        b2 = jnp.zeros((E, D), jnp.float32)
        return {'x': x, 'Wg': Wg, 'bg': bg, 'W1': W1, 'b1': b1, 'W2': W2, 'b2': b2}
    _L0_ffn_all = _L0_ffn_setup()
    _L0_ffn_in = {k: v for k, v in _L0_ffn_all.items() if k in ('Wg', 'bg', 'W1', 'b1', 'W2', 'b2')}
    del _L0_ffn_all
    return {'x': x, 'L0_tok_a_n': _L0_tok_in['a_n'], 'L0_tok_b_n': _L0_tok_in['b_n'], 'L0_tok_rule_transform': _L0_tok_in['rule_transform'], 'L0_tok_token_rules': _L0_tok_in['token_rules'], 'L0_tok_proj_w': _L0_tok_in['proj_w'], 'L0_tok_proj_b': _L0_tok_in['proj_b'], 'L0_attn_w_qkv': _L0_attn_in['w_qkv'], 'L0_attn_w_out': _L0_attn_in['w_out'], 'L0_attn_b_out': _L0_attn_in['b_out'], 'L0_ffn_Wg': _L0_ffn_in['Wg'], 'L0_ffn_bg': _L0_ffn_in['bg'], 'L0_ffn_W1': _L0_ffn_in['W1'], 'L0_ffn_b1': _L0_ffn_in['b1'], 'L0_ffn_W2': _L0_ffn_in['W2'], 'L0_ffn_b2': _L0_ffn_in['b2']}

def reference(x, L0_tok_a_n, L0_tok_b_n, L0_tok_rule_transform, L0_tok_token_rules, L0_tok_proj_w, L0_tok_proj_b, L0_attn_w_qkv, L0_attn_w_out, L0_attn_b_out, L0_ffn_Wg, L0_ffn_bg, L0_ffn_W1, L0_ffn_b1, L0_ffn_W2, L0_ffn_b2):
    import jax
    import jax.numpy as jnp

    def _L0_tok_ref(token_ids, a_n, b_n, rule_transform, token_rules, proj_w, proj_b):
        import jax, jax.numpy as jnp
        import numpy as np
        VOCAB = 50257
        EMBED = 64
        NFREQ = 64
        NRULES = 100
        B, S = (4, 256)
        vocab_size, nfreq = a_n.shape
        freqs = jnp.arange(1, nfreq + 1, dtype=jnp.float32)
        x = token_ids.astype(jnp.float32)[..., None] / vocab_size
        ang = 2.0 * jnp.pi * freqs * x
        fourier = a_n[token_ids] * jnp.cos(ang) + b_n[token_ids] * jnp.sin(ang)
        base = jnp.einsum('bsf,df->bsd', fourier, proj_w) + proj_b
        rule_idx = token_rules[token_ids]
        rules = rule_transform[rule_idx]
        return jnp.einsum('bsd,bsde->bse', base, rules)

    def _L0_attn_ref(x, w_qkv, w_out, b_out):
        import jax, jax.numpy as jnp
        import numpy as np
        HEADS, DIM_HEAD = (8, 64)
        EPS = 1e-05

        def instance_norm(t):
            mu = jnp.mean(t, axis=-1, keepdims=True)
            var = jnp.mean((t - mu) ** 2, axis=-1, keepdims=True)
            return (t - mu) * jax.lax.rsqrt(var + EPS)
        B, N, _ = x.shape
        H, Dh = (HEADS, DIM_HEAD)
        qkv = jnp.einsum('bnd,ed->bne', x, w_qkv)
        q, k, v = jnp.split(qkv, 3, axis=-1)

        def to_heads(t):
            return t.reshape(B, N, H, Dh).transpose(0, 2, 1, 3)
        q, k, v = (to_heads(q), to_heads(k), to_heads(v))
        k = instance_norm(k)
        v = instance_norm(v)
        dots = jnp.einsum('bhnd,bhne->bhde', k, v)
        out = jnp.einsum('bhnd,bhde->bhne', q, dots) / N
        out = out.transpose(0, 2, 1, 3).reshape(B, N, H * Dh)
        return jnp.einsum('bne,de->bnd', out, w_out) + b_out

    def _L0_ffn_ref(x, Wg, bg, W1, b1, W2, b2):
        import jax, jax.numpy as jnp
        import numpy as np
        B, S, D, E, H, K = (4, 1024, 64, 8, 128, 2)
        Bv, Sv, Dv = x.shape
        gate_scores = x @ Wg + bg
        _, idx = jax.lax.top_k(gate_scores, K)
        mask = jax.nn.one_hot(idx, E, dtype=x.dtype).sum(axis=-2)
        xf = x.reshape(-1, Dv)
        mf = mask.reshape(-1, E)
        h = jax.nn.gelu(jnp.einsum('td,edh->teh', xf, W1) + b1[None], approximate=False)
        y = jnp.einsum('teh,ehd->ted', h, W2) + b2[None]
        out = jnp.einsum('ted,te->td', y, mf)
        return out.reshape(Bv, Sv, Dv)
    h = _L0_tok_ref(x, L0_tok_a_n, L0_tok_b_n, L0_tok_rule_transform, L0_tok_token_rules, L0_tok_proj_w, L0_tok_proj_b)
    h = h + _L0_attn_ref(_layernorm(h, axis=-1), L0_attn_w_qkv, L0_attn_w_out, L0_attn_b_out)
    h = h + _L0_ffn_ref(_layernorm(h, axis=-1), L0_ffn_Wg, L0_ffn_bg, L0_ffn_W1, L0_ffn_b1, L0_ffn_W2, L0_ffn_b2)
    return h

_drawn_inputs = setup_inputs


def setup_inputs(seed=0):
    import zlib

    import numpy as np

    out = dict(_drawn_inputs(seed))
    spreads = {'L0_ffn_bg': (0.0, 0.673), 'L0_ffn_b1': (0.0, 0.8), 'L0_ffn_b2': (0.0, 0.502)}
    factors = {'L0_tok_proj_b': 4.961,
     'L0_attn_b_out': 8.0,
     'L0_ffn_Wg': 3.965,
     'L0_ffn_W1': 8.0,
     'L0_ffn_W2': 8.0}
    for name, (base, spread) in spreads.items():
        noise = np.random.default_rng([zlib.crc32(name.encode()), seed]).standard_normal(out[name].shape)
        drawn = base * np.exp(spread * noise) if base else spread * noise
        out[name] = jnp.asarray(drawn.astype(out[name].dtype))
    for name, factor in factors.items():
        out[name] = (out[name] * factor).astype(out[name].dtype)
    return out
```

```python
from contextlib import ExitStack

import concourse.bass as bass
from concourse import mybir
from concourse.alu_op_type import AluOpType as ALU

F32, F16, BF16 = mybir.dt.float32, mybir.dt.float16, mybir.dt.bfloat16
I32, U32 = mybir.dt.int32, mybir.dt.uint32
ACT = mybir.ActivationFunctionType
AX = mybir.AxisListType

P = 128
EPS = 1e-5
PI = 3.141592653589793
ROUND = 12582912.0
RSQRT_SEED = 1597463007.0
NEWTON = 3
FAR = -1e30


class Steps:

    def __init__(self, eng, sem, base=0):
        self.eng, self.sem, self.base, self.n = eng, sem, base, 0

    def then(self, ins, alone=None):
        ins.then_inc(self.sem, 1)
        self.n += 1
        self.eng.wait_ge(self.sem, self.base + self.n)
        if alone is not None:
            self.eng.sem_inc(alone, 1)


def wait_past(eng, sem, value):
    if not isinstance(value, int) or value > 0:
        eng.wait_ge(sem, value)


def program(nc, x, tables, rule_transform, token_rules, proj_w, proj_b, w_qkv, w_out, b_out,
            wg, bg, w1, b1, w2, b2, out):
    B, S = x.shape
    V, NR = token_rules.shape[0], rule_transform.shape[0]
    D = proj_w.shape[0]
    H = w_qkv.shape[0] // (3 * D)
    E, _, HID = w1.shape
    T = B * S
    TPS = S // P
    NC = T // P
    W = 32
    SLOTS = T // W + NR
    SPT = P // W
    NG = SLOTS // SPT
    assert SLOTS % SPT == 0
    NPOS = SLOTS * W
    GB = 8
    NB_FULL, NB_REST = NG // GB, NG % GB
    NBATCH = NB_FULL + (NB_REST > 0)
    QB = GB * SPT
    SPG = 2
    TG = SPG * TPS
    NGRP = B // SPG
    GT = TG * P
    RB = 4
    CPB = 5

    with ExitStack() as ctx:
        def sb(name, shape, dt):
            return ctx.enter_context(nc.sbuf_tensor(name, shape, dt))

        def sem(name):
            return ctx.enter_context(nc.semaphore(name))

        bank = [ctx.enter_context(nc.psum_tensor(f"bank{i}", [P, 512], F32)) for i in range(8)]
        by_position = nc.dram_tensor("by_position", (NPOS, D), F32).ap()

        rule_iota = sb("rule_iota", [P, NR], BF16)
        part_iota = sb("part_iota", [P, P], BF16)
        tile_iota = sb("tile_iota", [P, NG], BF16)
        freq = sb("freq", [P, D], F32)
        slot_iota = sb("slot_iota", [P, SLOTS], F32)
        expert_iota = sb("expert_iota", [P, E], F32)
        before = sb("before", [P, P], BF16)
        upto = sb("upto", [P, P], BF16)
        ones_bf = sb("ones_bf", [P, P], BF16)
        ones_f = sb("ones_f", [P, P], F32)
        eye_f = sb("eye_f", [P, P], F32)
        eye_16 = sb("eye_16", [P, P], F16)
        eye_bf = sb("eye_bf", [P, P], BF16)
        center = sb("center", [D, D], F32)
        far = sb("far", [2 * E, E, HID], BF16)
        half_pi = sb("half_pi", [P, 1], F32)
        zeros = sb("zeros", [P, NR], F32)

        ids = sb("ids", [P, NC], I32)
        rules_i = sb("rules_i", [P, NC], I32)
        rules_bf = sb("rules_bf", [P, NC], BF16)
        fold = sb("fold", [P, NR * D], F32)
        pwb = sb("pwb", [D, D + 1], F32)
        rows = sb("rows", [P, NG * 2 * D], F32)
        has = rows[:, 0:NC * NR // 2].bitcast(BF16)
        run = rows[:, NC * NR // 2:(2 * NC + 1) * NR // 2].bitcast(BF16)
        has3 = has.rearrange("p (c r) -> p c r", r=NR)
        run3 = run.rearrange("p (c r) -> p c r", r=NR)
        trig_flat = sb("trig", [P, NG * 2 * D], F32)
        trig = trig_flat[:, :].rearrange("p (t a d) -> p t a d", a=2, d=D)
        tot_i = sb("tot_i", [P, NR], I32)
        tot_j = sb("tot_j", [P, NR], I32)
        slots_f = sb("slots_f", [P, NR], F32)
        slots_end = sb("slots_end", [P, NR], F32)
        start_i = sb("start_i", [P, NR], I32)
        start_a = sb("start_a", [P, NR], BF16)
        start_b = sb("start_b", [P, NR], BF16)
        ranked = sb("ranked", [P, CPB * NR], F32)
        pos_f = sb("pos_f", [P, NC], F32)
        pos_i = sb("pos_i", [P, NC], I32)
        pos_t = sb("pos_t", [P, NC], I32)
        pos_p = sb("pos_p", [P, NC], F32)
        pos_g = sb("pos_g", [P, NC], F32)
        id_t = sb("id_t", [P, NC], I32)
        id_hi = sb("id_hi", [P, NC], F32)
        id_lo = sb("id_lo", [P, NC], F32)
        NH = 4
        is_part = sb("is_part", [P, NH, P], BF16)
        is_tile = sb("is_tile", [P, NH, 2, NG], BF16)
        spos_f = sb("spos_f", [P, NG], F32)
        spos_i = sb("spos_i", [P, NG], I32)
        col_i = sb("col_i", [P, 1], I32)
        col_j = sb("col_j", [P, 1], I32)
        col_n = sb("col_n", [P, 1], BF16)
        col_end = sb("col_end", [P, 1], F32)
        past = sb("past", [P, SLOTS], BF16)
        slot_f = sb("slot_f", [1, NBATCH * QB], F32)
        slot_at = sb("slot_at", [1, NBATCH * QB], I32)
        feats = sb("feats", [P, GB, D + 1], F32)
        feats_t = sb("feats_t", [P, GB * P], F32)
        mapped = sb("mapped", [W, QB * D], F32)
        h_all = sb("h_all", [P, NC, D], F32)

        wn = sb("wn", [D, 3 * H, D], F32)
        wc = sb("wc", [D, 2 * H, D], F32)
        wo = sb("wo", [D, H * D], F32)
        wo_t = sb("wo_t", [D, H, D], F32)
        wtmp = sb("wtmp", [P, 2 * H * D], F32)
        wkv_h = sb("wkv_h", [P, 2 * H * D], F16)
        wkv_l = sb("wkv_l", [P, 2 * H * D], F16)
        p_t = sb("p_t", [P, H // 2, P], F32)
        q_w = sb("q_w", [D, H, D], F32)
        fro = sb("fro", [D, 2 * H + E], F32)
        fro_all = sb("fro_all", [P, 2 * H + E], F32)
        fro_root = sb("fro_root", [P, 2 * H + E], F32)
        scale_up = sb("scale_up", [P, 2 * H + E], F32)
        scale_dn = sb("scale_dn", [P, 2 * H + E], F32)
        inv_c2 = sb("inv_c2", [P, 2 * H], F32)
        w1f = sb("w1f", [P, E, HID], F32)
        w1_h = sb("w1_h", [P, E, HID], F16)
        w1_l = sb("w1_l", [P, E, HID], F16)
        b1t = sb("b1t", [HID, E], F32)
        w2f = sb("w2f", [HID, E, D], F32)
        wgf = sb("wgf", [P, E], F32)
        wg_r = sb("wg_r", [P, E], F32)
        wg_3 = sb("wg_3", [P, 3, E], BF16)
        b2f = sb("b2f", [2 * E, D], F32)
        b2_r = sb("b2_r", [2 * E, D], F32)
        b2_3 = sb("b2_3", [2 * E, 3, D], BF16)
        bg_all = sb("bg_all", [P, E], F32)
        bo_all = sb("bo_all", [P, D], F32)

        taken = [0]

        def later(name, shape, dt):
            n = 1
            for k in shape[1:]:
                n *= k
            words = n * (2 if dt in (F16, BF16) else 4) // 4
            assert words * 4 == n * (2 if dt in (F16, BF16) else 4)
            v = trig_flat[0:shape[0], taken[0]:taken[0] + words]
            taken[0] += words
            assert taken[0] <= NG * 2 * D, name
            v = v if dt == F32 else v.bitcast(dt)
            if len(shape) == 2:
                return v
            names = ["a", "b", "c"][:len(shape) - 1]
            return v.rearrange(f"p ({' '.join(names)}) -> p {' '.join(names)}",
                               **dict(zip(names[1:], shape[2:])))

        cen = later("cen", [P, TG, D], F32)
        lsq = later("lsq", [P, TG, D], F32)
        lsum = later("lsum", [P, TG], F32)
        lssq = later("lssq", [P, TG], F32)
        nt_u = later("nt_u", [P, TG * 2 * H], F32)
        nt_i = later("nt_i", [P, TG * 2 * H], I32)
        nt_y = later("nt_y", [P, TG * 2 * H], F32)
        nt_t = later("nt_t", [P, TG * 2 * H], F32)
        x1 = later("x1", [P, TG, D], F32)
        x1_16 = later("x1_16", [P, TG, 2, D], F16)
        x1_t = later("x1_t", [P, GT], F16)
        x1_ta = later("x1_ta", [P, GT], F16)
        sq = later("sq", [P, 4, 512], F32)
        ssq = later("ssq", [P, TG, 2 * H], F32)
        ksv = later("ksv", [P, TG, H], F32)
        xs = later("xs", [P, TG, H, D], F32)
        g_sb = later("g_sb", [D, SPG, H * D], F32)
        t_sb = later("t_sb", [P, H // 2, SPG, D], F32)
        m_f = later("m_f", [P, SPG * D], F32)
        m_r = later("m_r", [P, SPG * D], F32)
        m_3 = later("m_3", [P, 3, SPG * D], BF16)
        h2 = later("h2", [P, TG, D], F32)
        x2 = later("x2", [P, TG, D], F32)
        x2_16 = later("x2_16", [P, TG, 2, D], F16)
        x2_t = later("x2_t", [P, GT], F16)
        score = later("score", [P, TG, E], F32)
        top = later("top", [P, TG, 8], F32)
        top_at = later("top_at", [P, TG, 8], U32)
        top_f = later("top_f", [P, TG, 2], F32)
        is0 = later("is0", [P, TG, E], F32)
        is1 = later("is1", [P, TG, E], F32)
        mask = later("mask", [P, TG, 2, E], BF16)
        mask_t = later("mask_t", [2 * E, GT], BF16)
        hid = later("hid", [P, 2, GT], F32)
        y_t = later("y_t", [D, GT], F32)
        outb = later("outb", [P, TG, D], F32)

        ids_in, const_made = sem("ids_in"), sem("const_made")
        rules_in = [sem(f"rules_in{i}") for i in range(RB)]
        fold_in, qkv_in, wo_in, w1_in, w2_in, small_in = (
            sem(n) for n in ("fold_in", "qkv_in", "wo_in", "w1_in", "w2_in", "small_in"))
        cleared = sem("cleared")
        folded_done, folded = sem("folded_done"), sem("folded")
        wc_done, wc_ready = sem("wc_done"), sem("wc_ready")
        fro_ready, fro_done, fro_copied, root_ready = (
            sem(n) for n in ("fro_ready", "fro_done", "fro_copied", "root_ready"))
        wt_done, wt_used = sem("wt_done"), sem("wt_used")
        wot_done, wot_ready = sem("wot_done"), sem("wot_ready")
        pq_done, pq_ready = sem("pq_done"), sem("pq_ready")
        weights_ready = sem("weights_ready")
        prep_steps, sort_steps = sem("prep_steps"), sem("sort_steps")
        counts_ready, totals_done, starts_ready = (
            sem(n) for n in ("counts_ready", "totals_done", "starts_ready"))
        ranks_done, ranks_used = sem("ranks_done"), sem("ranks_used")
        cols_ready, cols_used, sorted_done = sem("cols_ready"), sem("cols_used"), sem("sorted_done")
        nslots_ready, ends_done, past_ready, slots_done, slots_ready = (
            sem(n) for n in ("nslots_ready", "ends_done", "past_ready", "slots_done", "slots_ready"))
        sorted_ready, pos_ready = sem("sorted_ready"), sem("pos_ready")
        angles_ready, trig_ready = sem("angles_ready"), sem("trig_ready")
        rows_in = [sem(f"rows_in{i}") for i in range(NBATCH)]
        rows_arrived = sem("rows_arrived")
        feats_steps, feats_ready, feats_turned, feats_t_ready = (
            sem(n) for n in ("feats_steps", "feats_ready", "feats_turned", "feats_t_ready"))
        slots_mapped, mapped_ready, mapped_out = (
            sem(n) for n in ("slots_mapped", "mapped_ready", "mapped_out"))
        h_in = [sem(f"h_in{i}") for i in range(NGRP)]
        h_arrived = sem("h_arrived")

        ln1_steps, kvn_steps, ln2_steps, mask_steps, m_steps, h2_steps = (
            sem(n) for n in ("ln1_steps", "kvn_steps", "ln2_steps", "mask_steps", "m_steps", "h2_steps"))
        x1_turned, x1_t_ready, x1_kept = sem("x1_turned"), sem("x1_t_ready"), sem("x1_kept")
        kv_done, sq_ready, sums_ready = sem("kv_done"), sem("sq_ready"), sem("sums_ready")
        xs_ready, g_done, g_ready = sem("xs_ready"), sem("g_done"), sem("g_ready")
        t_done, t_ready, m_done, attn_done = sem("t_done"), sem("t_ready"), sem("m_done"), sem("attn_done")
        x2_turned, x2_t_ready = sem("x2_turned"), sem("x2_t_ready")
        gate_done, mask_turned, mask_t_ready = sem("gate_done"), sem("mask_turned"), sem("mask_t_ready")
        w1_done, gelu_ready, w2_done = sem("w1_done"), sem("gelu_ready"), sem("w2_done")
        y_t_ready, back_done, out_ready, out_sent = (
            sem(n) for n in ("y_t_ready", "back_done", "out_ready", "out_sent"))

        pe_waited, dve_waited = sem("pe_waited"), sem("dve_waited")

        LN_STEPS = 5 + 2 + 3 * NEWTON + 3
        KVN_STEPS = 2 + 2 + 3 * NEWTON + 1
        MASK_STEPS = 3 + 2 * TG + 3
        M_STEPS = 5
        H2_STEPS = 2
        halves = 2 * TG

        block = ctx.enter_context(nc.Block())

        @block.sync
        def _(sp):
            sp.dma_start(ids[:, :].rearrange("p (b s) -> p b s", s=TPS),
                         x.rearrange("b (p s) -> p b s", s=TPS)).then_inc(ids_in, 16)
            sp.dma_start(fold[0:D, :].rearrange("d (r e) -> d r e", e=D),
                         rule_transform.rearrange("r d e -> d r e")).then_inc(fold_in, 16)
            sp.dma_start(pwb[:, 0:D], proj_w).then_inc(fold_in, 16)
            sp.dma_start(pwb[:, D:D + 1], proj_b.rearrange("(d o) -> d o", o=1)).then_inc(fold_in, 16)
            sp.dma_start(wn[:, :, :], w_qkv.rearrange("(g e) d -> e g d", e=D)).then_inc(qkv_in, 16)
            sp.dma_start(wo[:, :], w_out).then_inc(wo_in, 16)
            for half in range(2):
                sp.dma_start(w1f[half * D:(half + 1) * D, :, :],
                             w1.rearrange("e d h -> d e h")).then_inc(w1_in, 16)
            sp.dma_start(w2f[:, :, :], w2.rearrange("e h d -> h e d")).then_inc(w2_in, 16)
            for half in range(2):
                sp.dma_start(wgf[half * D:(half + 1) * D, :], wg).then_inc(small_in, 16)
            sp.wait_ge(cleared, 3)
            sp.dma_start(b2f[E:2 * E, :], b2).then_inc(small_in, 16)
            sp.dma_start(b1t[:, :], b1).then_inc(small_in, 16)
            sp.dma_start(bg_all[:, :], bg.partition_broadcast(P)).then_inc(small_in, 16)
            sp.dma_start(bo_all[:, :], b_out.partition_broadcast(P)).then_inc(small_in, 16)
            posv = by_position[0:NB_FULL * QB * W, :].rearrange("(k q p) d -> k p q d", p=W, q=QB)
            with sp.Fori(0, NB_FULL) as k:
                sp.wait_ge(mapped_ready, k + 1)
                sp.dma_start(posv[k], mapped[:, :].rearrange("p (q d) -> p q d", d=D)).then_inc(mapped_out, 16)
            if NB_REST:
                sp.wait_ge(mapped_ready, NBATCH)
                sp.dma_start(by_position[NB_FULL * QB * W:NPOS, :].rearrange("(q p) d -> p q d", p=W),
                             mapped[:, 0:NB_REST * SPT * D].rearrange("p (q d) -> p q d", d=D)
                             ).then_inc(mapped_out, 16)
            outv = out.rearrange("(g q) (p s) d -> g p q (s d)", q=SPG, s=TPS)
            with sp.Fori(0, NGRP) as g:
                sp.wait_ge(out_ready, g + 1)
                sp.dma_start(outv[g], outb[:, :, :].rearrange("p (q s) d -> p q (s d)", s=TPS)
                             ).then_inc(out_sent, 16)
            sp.wait_ge(out_sent, 16 * NGRP)

        @block.gpsimd
        def _(pool):
            c = Steps(pool, const_made)
            c.then(pool.memset(before[:, :], 0.0))
            c.then(pool.affine_select(before[:, :], before[:, :], pattern=[[-1, P]], compare_op=ALU.is_ge,
                                      fill=1.0, base=0, channel_multiplier=1))
            c.then(pool.memset(upto[:, :], 0.0))
            c.then(pool.affine_select(upto[:, :], upto[:, :], pattern=[[-1, P]], compare_op=ALU.is_ge,
                                      fill=1.0, base=-1, channel_multiplier=1))
            for eye in (eye_f, eye_16, eye_bf):
                c.then(pool.memset(eye[:, :], 0.0))
                c.then(pool.affine_select(eye[:, :], eye[:, :], pattern=[[-1, P]], compare_op=ALU.not_equal,
                                          fill=1.0, base=0, channel_multiplier=1))
            c.then(pool.memset(center[:, :], -1.0 / D))
            c.then(pool.affine_select(center[:, :], center[:, :], pattern=[[-1, D]], compare_op=ALU.not_equal,
                                      fill=1.0 - 1.0 / D, base=0, channel_multiplier=1))
            c.then(pool.memset(far[:, :, :], 0.0))
            c.then(pool.affine_select(far[:, :, :], far[:, :, :], pattern=[[-1, E], [0, HID]],
                                      compare_op=ALU.not_equal, fill=FAR, base=0, channel_multiplier=1))
            for t, n, first in ((rule_iota, NR, 0), (part_iota, P, 0), (tile_iota, NG, 0), (freq, D, 1),
                                (slot_iota, SLOTS, 0), (expert_iota, E, 0)):
                c.then(pool.iota(t[:, :], pattern=[[1, n]], base=first, channel_multiplier=0,
                                 allow_small_or_imprecise_dtypes=True))
            assert c.n == CONSTS
            pool.wait_ge(ids_in, 16)
            for t in range(NC):
                pool.indirect_dma_start(rules_i[:, t:t + 1], None, token_rules.rearrange("(v o) -> v o", o=1),
                                        bass.IndirectOffsetOnAxis(ap=ids[:, t:t + 1], axis=0)
                                        ).then_inc(rules_in[t * RB // NC], 16)
            pool.wait_ge(sorted_ready, 1)
            pool.wait_ge(ranks_used, RANK_BANKS)
            for k in range(NBATCH):
                for t in range(k * GB, min(k * GB + GB, NG)):
                    pool.indirect_dma_start(rows[:, t * 2 * D:(t + 1) * 2 * D], None, tables,
                                            bass.IndirectOffsetOnAxis(ap=spos_i[:, t:t + 1], axis=0)
                                            ).then_inc(rows_in[k], 16)
                if k:
                    pool.wait_ge(rows_in[k - 1], 16 * GB)
                    pool.sem_inc(rows_arrived, 1)
            pool.wait_ge(rows_in[NBATCH - 1], 16 * (NG - (NBATCH - 1) * GB))
            pool.sem_inc(rows_arrived, 1)
            pool.wait_ge(mapped_out, 16 * NBATCH)
            pool.wait_ge(pos_ready, 1)
            for g in range(NGRP):
                for t in range(g * TG, (g + 1) * TG):
                    pool.indirect_dma_start(h_all[:, t, :], None, by_position,
                                            bass.IndirectOffsetOnAxis(ap=pos_i[:, t:t + 1], axis=0)
                                            ).then_inc(h_in[g], 16)
                if g:
                    pool.wait_ge(h_in[g - 1], 16 * TG)
                    pool.sem_inc(h_arrived, 1)
            pool.wait_ge(h_in[NGRP - 1], 16 * TG)
            pool.sem_inc(h_arrived, 1)

        @block.scalar
        def _(act):
            act.wait_ge(wc_done, 1)
            act.activation(wc[:, 0:H, :], bank[4][0:D, :].rearrange("p (h d) -> p h d", d=D), ACT.Copy).then_inc(wc_ready, 1)
            act.activation(wc[:, H:2 * H, :], bank[5][0:D, :].rearrange("p (h d) -> p h d", d=D), ACT.Copy).then_inc(wc_ready, 1)
            act.wait_ge(wot_done, 1)
            act.activation(wo_t[:, :, :], bank[7][0:D, :].rearrange("p (h d) -> p h d", d=D), ACT.Copy).then_inc(wot_ready, 1)
            act.wait_ge(fro_copied, 1)
            act.activation(fro_root[:, :], fro_all[:, :], ACT.Sqrt).then_inc(root_ready, 1)
            act.wait_ge(pq_done, 1)
            for i in range(2):
                act.activation(p_t[:, :, i * D:(i + 1) * D],
                               bank[2][:, 0:H // 2 * D].rearrange("p (h d) -> p h d", d=D), ACT.Copy).then_inc(pq_ready, 1)
            act.activation(q_w[:, :, :], bank[3][0:D, :].rearrange("p (h d) -> p h d", d=D), ACT.Copy,
                           scale=1.0 / S).then_inc(pq_ready, 1)
            with act.Fori(0, FOLD_LOOPS) as k:
                for j in range(4):
                    act.wait_ge(folded_done, 4 * k + j + 1)
                    act.activation(fold[0:D + 1, bass.ds(FOLD * (4 * k + j), FOLD)], bank[j][0:D + 1, 0:FOLD],
                                   ACT.Copy).then_inc(folded, 1)

            act.wait_ge(angles_ready, 1)
            act.activation(trig[:, :, 0, :], trig[:, :, 1, :], ACT.Abs).then_inc(trig_ready, 1)
            act.wait_ge(trig_ready, 1)
            act.activation(trig[:, :, 1, :], trig[:, :, 1, :], ACT.Sin, scale=2 * PI / V).then_inc(trig_ready, 1)
            act.activation(trig[:, :, 0, :], trig[:, :, 0, :], ACT.Sin, scale=-2 * PI / V,
                           bias=half_pi[:, 0:1]).then_inc(trig_ready, 1)

            def batch_evac(k, tiles):
                wait_past(act, slots_mapped, 4 * k)
                for j in range(2):
                    n = min(max(tiles - 4 * j, 0), 4)
                    if n:
                        act.wait_ge(feats_turned, 2 * k + j + 1)
                        act.activation(feats_t[0:D + 1, 4 * j * P:(4 * j + n) * P], bank[4 + j][0:D + 1, 0:n * P],
                                       ACT.Copy).then_inc(feats_t_ready, 1)
                wait_past(act, mapped_out, 16 * k)
                for j in range(4):
                    n = min(max(tiles * SPT - 8 * j, 0), 8)
                    if n:
                        act.wait_ge(slots_mapped, 4 * k + j + 1)
                        ins = act.activation(mapped[:, 8 * j * D:(8 * j + n) * D], bank[j][0:W, 0:n * D], ACT.Copy)
                ins.then_inc(mapped_ready, 1)

            batch_evac(0, GB)
            with act.Fori(1, NB_FULL) as k:
                batch_evac(k, GB)
            if NB_REST:
                batch_evac(NB_FULL, NB_REST)

            def x1_evac(g):
                act.wait_ge(x1_turned, g + 1)
                wait_past(act, kv_done, halves * g)
                act.activation(x1_t[:, :], bank[1][:, :].bitcast(F16)[:, 0:GT], ACT.Copy).then_inc(x1_t_ready, 1)

            def square(g, j):
                act.wait_ge(kv_done, halves * g + j + 1)
                wait_past(act, sums_ready, halves * g + j - 3)
                act.activation(sq[:, j % 4, :], bank[j % 2][:, :], ACT.Square).then_inc(sq_ready, 1)

            def g_evac(g):
                for s in range(SPG):
                    act.wait_ge(g_done, SPG * g + s + 1)
                    act.activation(g_sb[:, s, :], bank[2 + s][0:D, :], ACT.Copy).then_inc(g_ready, 1)

            def t_evac(g):
                wait_past(act, m_done, g)
                for s in range(SPG):
                    act.wait_ge(t_done, SPG * g + s + 1)
                    act.activation(t_sb[:, :, s, :], bank[2 + s][:, 0:H // 2 * D].rearrange("p (h d) -> p h d", d=D),
                                   ACT.Copy).then_inc(t_ready, 1)

            def x2_evac(g):
                act.wait_ge(x2_turned, g + 1)
                wait_past(act, w1_done, E * g)
                act.activation(x2_t[:, :], bank[7][:, :].bitcast(F16)[:, 0:GT], ACT.Copy).then_inc(x2_t_ready, 1)

            def mask_evac(g):
                act.wait_ge(mask_turned, g + 1)
                wait_past(act, back_done, g)
                act.activation(mask_t[:, :], bank[7][0:2 * E, :].bitcast(BF16)[:, 0:GT], ACT.Copy
                               ).then_inc(mask_t_ready, 1)

            def gelu(g, e):
                act.wait_ge(w1_done, E * g + e + 1)
                wait_past(act, w2_done, E * g + e - 1)
                act.activation(hid[:, e % 2, :], bank[4 + e % 2][:, :], ACT.Gelu, bias=b1t[:, e:e + 1],
                               scale=scale_dn[:, 2 * H + e:2 * H + e + 1]).then_inc(gelu_ready, 1)

            def y_evac(g):
                act.wait_ge(w2_done, E * g + E)
                wait_past(act, back_done, g)
                act.activation(y_t[:, :], bank[6][0:D, :], ACT.Copy).then_inc(y_t_ready, 1)

            def step(i, att, ffn, more):
                for j in range(halves):
                    if att:
                        square(i, j)
                    if ffn and j == 3:
                        x2_evac(i - 1)
                if ffn:
                    mask_evac(i - 1)
                    for e in range(4):
                        gelu(i - 1, e)
                if att:
                    g_evac(i)
                if ffn:
                    gelu(i - 1, 4)
                    gelu(i - 1, 5)
                if att:
                    t_evac(i)
                if ffn:
                    gelu(i - 1, 6)
                    gelu(i - 1, 7)
                if more:
                    x1_evac(i + 1)
                if ffn:
                    y_evac(i - 1)

            x1_evac(0)
            step(0, True, False, True)
            step(1, True, True, True)
            with act.Fori(2, NGRP - 1) as i:
                step(i, True, True, True)
            step(NGRP - 1, True, True, False)
            step(NGRP, False, True, False)

        @block.tensor
        def _(pe):
            pe.wait_ge(const_made, CONSTS)
            pe.wait_ge(cleared, 4)
            pe.wait_ge(qkv_in, 16)
            for i in range(2):
                ins = pe.matmul(bank[4 + i][0:D, :], center[:, :],
                                wn[:, H * (1 + i):H * (2 + i), :].rearrange("p h d -> p (h d)"), start=True, stop=True)
            ins.then_inc(wc_done, 1)
            for half in range(2):
                for g in range(2 * H):
                    ins = pe.matmul(bank[g // H][half * D:(half + 1) * D, g % H * D:(g % H + 1) * D],
                                    wn[:, H + g, :], center[:, :], start=True, stop=True)
            ins.then_inc(wt_done, 1)
            pe.wait_ge(wo_in, 16)
            for h in range(H):
                ins = pe.transpose(bank[7][0:D, h * D:(h + 1) * D], wo[:, h * D:(h + 1) * D], eye_f[0:D, 0:D])
            ins.then_inc(wot_done, 1)
            pe.wait_ge(fro_ready, 1)
            pe.matmul(bank[6][:, 0:2 * H + E], ones_f[0:D, :], fro[:, :], start=True, stop=True).then_inc(fro_done, 1)
            pe.wait_ge(wc_ready, 2)
            pe.wait_ge(wot_ready, 1)
            for h in range(H):
                ins = pe.matmul(bank[2][h % 2 * D:(h % 2 + 1) * D, h // 2 * D:(h // 2 + 1) * D],
                                wc[:, h, :], wn[:, h, :], start=True, stop=True)
            for h in range(H):
                ins = pe.matmul(bank[3][0:D, h * D:(h + 1) * D], wc[:, H + h, :], wo_t[:, h, :],
                                start=True, stop=True)
            ins.then_inc(pq_done, 1)
            pe.wait_ge(fold_in, 48)
            pe.wait_ge(wt_used, 1)
            pe.wait_ge(pq_ready, 3)
            for j in range(4):
                pe.matmul(bank[j][0:D + 1, 0:FOLD], pwb[:, :], fold[0:D, FOLD * j:FOLD * (j + 1)],
                          start=True, stop=True).then_inc(folded_done, 1)
            with pe.Fori(1, FOLD_LOOPS) as k:
                for j in range(4):
                    pe.wait_ge(folded, 4 * k + j - 3)
                    pe.matmul(bank[j][0:D + 1, 0:FOLD], pwb[:, :], fold[0:D, bass.ds(FOLD * (4 * k + j), FOLD)],
                              start=True, stop=True).then_inc(folded_done, 1)

            pe.wait_ge(counts_ready, 1)
            pe.wait_ge(folded, 4 * FOLD_LOOPS)
            pe.matmul(bank[0][:, 0:NR], ones_bf[:, :], run3[:, NC, :], start=True, stop=True)
            pe.matmul(bank[1][0:NR, 0:1], run3[:, NC, :], ones_bf[:, 0:1], start=True, stop=True).then_inc(totals_done, 1)
            pe.wait_ge(nslots_ready, 1)
            pe.matmul(bank[1][0:NR, 4:5], upto[0:NR, 0:NR], col_n[0:NR, :], start=True, stop=True).then_inc(ends_done, 1)
            pe.wait_ge(past_ready, 1)
            pe.matmul(bank[1][0:1, 0:SLOTS], ones_bf[0:NR, 0:1], past[0:NR, :], start=True, stop=True).then_inc(slots_done, 1)
            pe.wait_ge(starts_ready, 1)
            for k in range(RANK_BANKS):
                if k >= 4:
                    pe.wait_ge(ranks_used, k - 3)
                for c in range(k * CPB, min(k * CPB + CPB, NC)):
                    o = bank[2 + k % 4][:, (c % CPB) * NR:(c % CPB + 1) * NR]
                    pe.matmul(o, before[:, :], has3[:, c, :], start=True, stop=False)
                    pe.matmul(o, ones_bf[:, :], run3[:, c, :], start=False, stop=False)
                    pe.matmul(o, ones_bf[:, :], start_a[:, :], start=False, stop=False)
                    ins = pe.matmul(o, ones_bf[:, :], start_b[:, :], start=False, stop=True)
                ins.then_inc(ranks_done, 1)
            for c in range(NC):
                pe.wait_ge(cols_ready, 3 * c + 3)
                pe.matmul(bank[6][:, 0:2 * NG], is_part[:, c % NH, :],
                          is_tile[:, c % NH, :, :].rearrange("p a g -> p (a g)"),
                          start=(c == 0), stop=(c == NC - 1)).then_inc(cols_used, 1)

            def batch(k, tiles):
                pe.wait_ge(feats_ready, k + 1)
                for j in range(2):
                    for t in range(4 * j, min(4 * j + 4, tiles)):
                        ins = pe.transpose(bank[4 + j][0:D + 1, (t - 4 * j) * P:(t - 4 * j + 1) * P], feats[:, t, :],
                                           eye_f[:, :])
                    if 4 * j < tiles:
                        ins.then_inc(feats_turned, 1)
                for j in range(4):
                    n = min(max(tiles * SPT - 8 * j, 0), 8)
                    if j in (0, 2) and 2 * j < tiles:
                        pe.wait_ge(feats_t_ready, 2 * k + j // 2 + 1)
                    if n:
                        _, at = nc.values_load_multi_w_load_instructions(
                            slot_at[0:1, bass.ds(QB * k + 8 * j, 8)], engines=[mybir.EngineType.PE],
                            min_val=0, max_val=(NR - 1) * D,
                            skip_runtime_bounds_check_because="the least of it and the last rule's is stored")
                    for q in range(n):
                        s = 8 * j + q
                        ins = pe.matmul(bank[j][0:W, q * D:(q + 1) * D], feats_t[:, s * W:(s + 1) * W],
                                        fold[:, bass.ds(at[q], D)], start=True, stop=True)
                    if n:
                        ins.then_inc(slots_mapped, 1)

            pe.wait_ge(slots_ready, 1)
            pe.wait_ge(sorted_ready, 1)
            pe.wait_ge(ranks_used, RANK_BANKS)
            pe.wait_ge(cleared, 8)
            batch(0, GB)
            with pe.Fori(1, NB_FULL) as k:
                pe.wait_ge(mapped_ready, k)
                batch(k, GB)
            if NB_REST:
                pe.wait_ge(mapped_ready, NB_FULL)
                batch(NB_FULL, NB_REST)

            def x1_turn(g):
                pe.wait_ge(ln1_steps, LN_STEPS * (g + 1))
                wait_past(pe, sq_ready, halves * g)
                for t in range(TG):
                    ins = pe.transpose(bank[1][:, :].bitcast(F16)[:, t * P:(t + 1) * P],
                                       x1_16[:, t, :, :].rearrange("p a d -> p (a d)"), eye_16[:, :])
                ins.then_inc(x1_turned, 1)

            def kv(g, j):
                if j == 0:
                    pe.wait_ge(x1_t_ready, g + 1)
                wait_past(pe, sq_ready, halves * g + j - 1)
                cols = slice(j % 2 * H * D, (j % 2 + 1) * H * D)
                lhs = x1_t[:, j // 2 * P:(j // 2 + 1) * P]
                pe.matmul(bank[j % 2][:, :], lhs, wkv_h[:, cols], start=True, stop=False)
                pe.matmul(bank[j % 2][:, :], lhs, wkv_l[:, cols], start=False, stop=True).then_inc(kv_done, 1)

            def gram(g):
                wait_past(pe, m_steps, M_STEPS * g)
                wait_past(pe, h2_steps, H2_STEPS * g)
                for s in range(SPG):
                    for t in range(TPS):
                        pe.wait_ge(xs_ready, TG * g + s * TPS + t + 1)
                        ins = pe.matmul(bank[2 + s][0:D, :], x1[:, s * TPS + t, :],
                                        xs[:, s * TPS + t, :, :].rearrange("p h d -> p (h d)"),
                                        start=(t == 0), stop=(t == TPS - 1))
                    ins.then_inc(g_done, 1)

            def times_q(g):
                for s in range(SPG):
                    pe.wait_ge(g_ready, SPG * g + s + 1)
                    pe.sem_inc(pe_waited, 1)
                    for h in range(H):
                        ins = pe.matmul(bank[2 + s][h % 2 * D:(h % 2 + 1) * D, h // 2 * D:(h // 2 + 1) * D],
                                        g_sb[:, s, h * D:(h + 1) * D], q_w[:, h, :], start=True, stop=True)
                    ins.then_inc(t_done, 1)

            def p_times(g):
                pe.wait_ge(t_ready, SPG * (g + 1))
                for h in range(H // 2):
                    ins = pe.matmul(bank[2][:, 0:SPG * D], p_t[:, h, :], t_sb[:, h, :, :].rearrange("p s d -> p (s d)"),
                                    start=(h == 0), stop=(h == H // 2 - 1))
                ins.then_inc(m_done, 1)

            def attend(g):
                pe.wait_ge(m_steps, M_STEPS * (g + 1))
                pe.wait_ge(x1_kept, g + 1)
                for t in range(TG):
                    for part in range(3):
                        ins = pe.matmul(bank[3][:, t * D:(t + 1) * D], x1_ta[:, t * P:(t + 1) * P],
                                        m_3[:, part, t // TPS * D:(t // TPS + 1) * D], start=(part == 0), stop=(part == 2))
                ins.then_inc(attn_done, 1)

            def x2_turn(g):
                pe.wait_ge(ln2_steps, LN_STEPS * (g + 1))
                wait_past(pe, out_ready, g)
                for t in range(TG):
                    ins = pe.transpose(bank[7][:, :].bitcast(F16)[:, t * P:(t + 1) * P],
                                       x2_16[:, t, :, :].rearrange("p a d -> p (a d)"), eye_16[:, :])
                ins.then_inc(x2_turned, 1)

            def gate(g):
                pe.wait_ge(x2_t_ready, g + 1)
                for t in range(TG):
                    for part in range(3):
                        ins = pe.matmul(bank[7][:, t * E:(t + 1) * E], x2_t[:, t * P:(t + 1) * P], wg_3[:, part, :],
                                        start=(part == 0), stop=(part == 2))
                ins.then_inc(gate_done, 1)

            def mask_turn(g):
                pe.wait_ge(mask_steps, MASK_STEPS * (g + 1))
                for t in range(TG):
                    ins = pe.transpose(bank[7][0:2 * E, :].bitcast(BF16)[:, t * P:(t + 1) * P],
                                       mask[:, t, :, :].rearrange("p a e -> p (a e)"), eye_bf[:, :])
                ins.then_inc(mask_turned, 1)

            def up(g, e):
                if e == 0:
                    pe.wait_ge(mask_t_ready, g + 1)
                wait_past(pe, gelu_ready, E * g + e - 1)
                o = bank[4 + e % 2][:, :]
                pe.matmul(o, w1_h[:, e, :], x2_t[:, :], start=True, stop=False)
                pe.matmul(o, w1_l[:, e, :], x2_t[:, :], start=False, stop=False)
                pe.matmul(o, far[:, e, :], mask_t[:, :], start=False, stop=True).then_inc(w1_done, 1)

            def down(g, e):
                pe.wait_ge(gelu_ready, E * g + e + 1)
                if e == 0:
                    wait_past(pe, y_t_ready, g)
                pe.matmul(bank[6][0:D, :], w2f[:, e, :], hid[:, e % 2, :], start=(e == 0), stop=(e == E - 1)
                          ).then_inc(w2_done, 1)

            def back(g):
                pe.wait_ge(y_t_ready, g + 1)
                for t in range(TG):
                    o = bank[7][:, t * D:(t + 1) * D]
                    pe.matmul(o, y_t[:, t * P:(t + 1) * P], eye_f[0:D, 0:D], start=True, stop=False)
                    for part in range(3):
                        ins = pe.matmul(o, mask_t[:, t * P:(t + 1) * P], b2_3[:, part, :], start=False,
                                        stop=(part == 2))
                ins.then_inc(back_done, 1)

            def step(i, att, ffn, more):
                for j in range(halves):
                    if att:
                        kv(i, j)
                    if ffn and j == 3:
                        x2_turn(i - 1)
                    if ffn and j == 5:
                        gate(i - 1)
                if ffn:
                    mask_turn(i - 1)
                    up(i - 1, 0)
                    for e in range(1, 4):
                        up(i - 1, e)
                        down(i - 1, e - 1)
                if att:
                    gram(i)
                if ffn:
                    for e in range(4, 6):
                        up(i - 1, e)
                        down(i - 1, e - 1)
                if att:
                    times_q(i)
                if ffn:
                    for e in range(6, 8):
                        up(i - 1, e)
                        down(i - 1, e - 1)
                if att:
                    p_times(i)
                if more:
                    x1_turn(i + 1)
                if ffn:
                    down(i - 1, 7)
                    back(i - 1)
                if att:
                    attend(i)

            pe.wait_ge(weights_ready, 1)
            pe.wait_ge(mapped_ready, NBATCH)
            x1_turn(0)
            step(0, True, False, True)
            step(1, True, True, True)
            with pe.Fori(2, NGRP - 1) as i:
                step(i, True, True, True)
            step(NGRP - 1, True, True, False)
            step(NGRP, False, True, False)

        @block.vector
        def _(dve):
            dve.memset(ones_bf[:, :], 1.0).then_inc(cleared, 1)
            dve.memset(ones_f[:, :], 1.0).then_inc(cleared, 1)
            dve.memset(b2f[:, :], 0.0).then_inc(cleared, 1)
            dve.memset(run3[:, 0, :], 0.0).then_inc(cleared, 1)
            dve.memset(zeros[:, :], 0.0).then_inc(cleared, 1)
            dve.memset(half_pi[:, :], PI / 2).then_inc(cleared, 1)
            dve.memset(feats[:, :, D:D + 1], 1.0).then_inc(cleared, 1)
            dve.memset(feats_t[D:P, :], 0.0).then_inc(cleared, 1)
            dve.memset(fold[D:P, :], 0.0).then_inc(cleared, 1)
            dve.memset(slot_at[:, :], 0).then_inc(cleared, 1)
            dve.wait_ge(cleared, 10)

            s = Steps(dve, prep_steps)
            dve.wait_ge(wc_ready, 2)
            t3 = wtmp[0:D, :].rearrange("p (g d) -> p g d", d=D)
            s.then(dve.tensor_tensor(t3, wc[:, :, :], wc[:, :, :], ALU.mult))
            s.then(dve.tensor_reduce(fro[:, 0:2 * H], t3, AX.X, ALU.add))
            dve.wait_ge(w1_in, 32)
            t3 = wtmp[0:D, :].rearrange("p (e h) -> p e h", h=HID)
            s.then(dve.tensor_tensor(t3, w1f[0:D, :, :], w1f[0:D, :, :], ALU.mult))
            dve.tensor_reduce(fro[:, 2 * H:2 * H + E], t3, AX.X, ALU.add).then_inc(fro_ready, 1)
            dve.wait_ge(fro_done, 1)
            dve.tensor_scalar(fro_all[:, :], bank[6][:, 0:2 * H + E], 1e-20, None, ALU.add).then_inc(fro_copied, 1)
            dve.wait_ge(root_ready, 1)
            s.then(dve.reciprocal(scale_up[:, :], fro_root[:, :]))
            s.then(dve.tensor_scalar(scale_up[:, :], scale_up[:, :], 1024.0, None, ALU.mult))
            s.then(dve.reciprocal(scale_dn[:, :], scale_up[:, :]))
            s.then(dve.tensor_scalar(inv_c2[:, :], scale_dn[:, 0:2 * H], 1.0 / D, None, ALU.mult))
            s.then(dve.tensor_tensor(inv_c2[:, :], inv_c2[:, :], scale_dn[:, 0:2 * H], ALU.mult))
            dve.wait_ge(wt_done, 1)
            for i in range(2):
                ins = dve.tensor_tensor(wtmp[:, i * H * D:(i + 1) * H * D].rearrange("p (h d) -> p h d", d=D),
                                        bank[i][:, :].rearrange("p (h d) -> p h d", d=D),
                                        scale_up[:, i * H:(i + 1) * H].unsqueeze(2).broadcast_to([P, H, D]), ALU.mult)
                ins.then_inc(wt_used, 1) if i else s.then(ins)
            dve.wait_ge(wt_used, 1)
            s.then(dve.tensor_copy(wkv_h[:, :], wtmp[:, :]))
            s.then(dve.tensor_tensor(wkv_l[:, :], wtmp[:, :], wkv_h[:, :], ALU.subtract))
            s.then(dve.tensor_tensor(w1f[:, :, :], w1f[:, :, :],
                                     scale_up[:, 2 * H:2 * H + E].unsqueeze(2).broadcast_to([P, E, HID]), ALU.mult))
            s.then(dve.tensor_copy(w1_h[:, :, :], w1f[:, :, :]))
            s.then(dve.tensor_tensor(w1_l[:, :, :], w1f[:, :, :], w1_h[:, :, :], ALU.subtract))
            dve.wait_ge(small_in, 16 * 6)
            for full, rest, parts in ((wgf, wg_r, wg_3), (b2f, b2_r, b2_3)):
                s.then(dve.tensor_copy(parts[:, 0, :], full[:, :]))
                s.then(dve.tensor_tensor(rest[:, :], full[:, :], parts[:, 0, :], ALU.subtract))
                s.then(dve.tensor_copy(parts[:, 1, :], rest[:, :]))
                s.then(dve.tensor_tensor(parts[:, 2, :], rest[:, :], parts[:, 1, :], ALU.subtract))
            dve.wait_ge(w2_in, 16)
            dve.wait_ge(pq_ready, 3)
            dve.sem_inc(weights_ready, 1)

            s = Steps(dve, sort_steps)
            dve.wait_ge(const_made, CONSTS)
            s.then(dve.tensor_scalar(id_t[:, :], ids[:, :], 8, None, ALU.logical_shift_right))
            s.then(dve.tensor_copy(id_hi[:, :], id_t[:, :]))
            s.then(dve.tensor_scalar(id_t[:, :], ids[:, :], 255, None, ALU.bitwise_and))
            s.then(dve.tensor_copy(id_lo[:, :], id_t[:, :]))
            n = NC // RB
            for b in range(RB):
                dve.wait_ge(rules_in[b], 16 * n)
                s.then(dve.tensor_copy(rules_bf[:, b * n:(b + 1) * n], rules_i[:, b * n:(b + 1) * n]))
                s.then(dve.tensor_tensor(has3[:, b * n:(b + 1) * n, :],
                                         rules_bf[:, b * n:(b + 1) * n].unsqueeze(2).broadcast_to([P, n, NR]),
                                         rule_iota[:, :].unsqueeze(1).broadcast_to([P, n, NR]), ALU.is_equal))
                for c in range(b * n, (b + 1) * n):
                    ins = dve.tensor_tensor(run3[:, c + 1, :], run3[:, c, :], has3[:, c, :], ALU.add)
                    ins.then_inc(counts_ready, 1) if c == NC - 1 else s.then(ins)
            dve.wait_ge(totals_done, 1)
            s.then(dve.tensor_copy(tot_i[:, :], bank[0][:, 0:NR]))
            s.then(dve.tensor_scalar(tot_j[:, :], tot_i[:, :], float(W - 1), None, ALU.add))
            s.then(dve.tensor_scalar(tot_i[:, :], tot_j[:, :], 5, None, ALU.logical_shift_right))
            s.then(dve.tensor_copy(slots_f[:, :], tot_i[:, :]))
            s.then(dve.tensor_tensor_scan(slots_end[:, :], slots_f[:, :], zeros[:, :], 0.0, ALU.add, ALU.add))
            s.then(dve.tensor_tensor(tot_j[:, :], slots_end[:, :], slots_f[:, :], ALU.subtract))
            s.then(dve.tensor_scalar(start_i[:, :], tot_j[:, :], 1, None, ALU.logical_shift_right))
            s.then(dve.tensor_scalar(start_a[:, :], start_i[:, :], 2.0 * W / P, None, ALU.mult))
            s.then(dve.tensor_scalar(start_i[:, :], tot_j[:, :], 1, None, ALU.bitwise_and))
            dve.tensor_scalar(start_b[:, :], start_i[:, :], float(W) / P, None, ALU.mult).then_inc(starts_ready, 1)
            s.then(dve.tensor_copy(col_i[0:NR, :], bank[1][0:NR, 0:1]))
            s.then(dve.tensor_scalar(col_j[0:NR, :], col_i[0:NR, :], float(W - 1), None, ALU.add))
            s.then(dve.tensor_scalar(col_i[0:NR, :], col_j[0:NR, :], 5, None, ALU.logical_shift_right))
            dve.tensor_copy(col_n[0:NR, :], col_i[0:NR, :]).then_inc(nslots_ready, 1)
            dve.wait_ge(ends_done, 1)
            s.then(dve.tensor_copy(col_end[0:NR, :], bank[1][0:NR, 4:5]))
            dve.tensor_scalar(past[0:NR, :], slot_iota[0:NR, :], col_end[0:NR, 0:1], None, ALU.is_ge
                              ).then_inc(past_ready, 1)
            dve.wait_ge(slots_done, 1)
            s.then(dve.tensor_scalar(slot_f[:, 0:SLOTS], bank[1][0:1, 0:SLOTS], float(NR - 1), float(D),
                                     ALU.min, ALU.mult))
            dve.tensor_copy(slot_at[:, 0:SLOTS], slot_f[:, 0:SLOTS]).then_inc(slots_ready, 1)
            for k in range(RANK_BANKS):
                c0, c1 = k * CPB, min(k * CPB + CPB, NC)
                dve.wait_ge(ranks_done, k + 1)
                s.then(dve.tensor_tensor(ranked[:, 0:(c1 - c0) * NR], bank[2 + k % 4][:, 0:(c1 - c0) * NR],
                                         has[:, c0 * NR:c1 * NR], ALU.mult))
                dve.tensor_reduce(pos_f[:, c0:c1], ranked[:, 0:(c1 - c0) * NR].rearrange("p (c r) -> p c r", r=NR),
                                  AX.X, ALU.add).then_inc(ranks_used, 1)
                dve.wait_ge(ranks_used, k + 1)
            dve.tensor_copy(pos_i[:, :], pos_f[:, :]).then_inc(pos_ready, 1)
            dve.wait_ge(pos_ready, 1)
            s.then(dve.tensor_scalar(pos_t[:, :], pos_i[:, :], P - 1, None, ALU.bitwise_and))
            s.then(dve.tensor_copy(pos_p[:, :], pos_t[:, :]))
            s.then(dve.tensor_scalar(pos_t[:, :], pos_i[:, :], 7, None, ALU.logical_shift_right))
            s.then(dve.tensor_copy(pos_g[:, :], pos_t[:, :]))
            for c in range(NC):
                if c >= NH:
                    dve.wait_ge(cols_used, c - NH + 1)
                dve.tensor_scalar(is_part[:, c % NH, :], part_iota[:, :], pos_p[:, c:c + 1], None,
                                  ALU.is_equal).then_inc(cols_ready, 1)
                dve.tensor_scalar(is_tile[:, c % NH, 0, :], tile_iota[:, :], pos_g[:, c:c + 1], id_hi[:, c:c + 1],
                                  ALU.is_equal, ALU.mult).then_inc(cols_ready, 1)
                dve.tensor_scalar(is_tile[:, c % NH, 1, :], tile_iota[:, :], pos_g[:, c:c + 1], id_lo[:, c:c + 1],
                                  ALU.is_equal, ALU.mult).then_inc(cols_ready, 1)
            dve.wait_ge(cols_used, NC)
            s.then(dve.tensor_copy(spos_f[:, :], bank[6][:, NG:2 * NG]))
            s.then(dve.scalar_tensor_tensor(spos_f[:, :], bank[6][:, 0:NG], 256.0, spos_f[:, :], ALU.mult, ALU.add))
            dve.tensor_copy(spos_i[:, :], spos_f[:, :]).then_inc(sorted_ready, 1)
            lo, hi = trig[:, :, 0, :], trig[:, :, 1, :]
            s.then(dve.tensor_tensor(lo, spos_f[:, :].unsqueeze(2).broadcast_to([P, NG, D]),
                                     freq[:, :].unsqueeze(1).broadcast_to([P, NG, D]), ALU.mult))
            s.then(dve.tensor_scalar(hi, lo, 1.0 / V, ROUND, ALU.mult, ALU.add))
            s.then(dve.tensor_scalar(hi, hi, ROUND, float(V), ALU.subtract, ALU.mult))
            dve.tensor_tensor(hi, lo, hi, ALU.subtract).then_inc(angles_ready, 1)
            dve.wait_ge(trig_ready, 3)

            def features(k, tiles):
                dve.wait_ge(rows_arrived, k + 1)
                wait_past(dve, feats_turned, 2 * k)
                r = rows[:, bass.ds(k * GB * 2 * D, tiles * 2 * D)]
                dve.tensor_tensor(r, r, trig[:, bass.ds(k * GB, tiles), :, :].rearrange("p t a d -> p (t a d)"), ALU.mult
                                  ).then_inc(feats_steps, 1)
                dve.wait_ge(feats_steps, k + 1)
                r4 = r.rearrange("p (t a d) -> p t a d", a=2, d=D)
                dve.tensor_tensor(feats[:, 0:tiles, 0:D], r4[:, :, 0, :], r4[:, :, 1, :], ALU.add
                                  ).then_inc(feats_ready, 1)

            features(0, GB)
            with dve.Fori(1, NB_FULL) as k:
                features(k, GB)
            if NB_REST:
                features(NB_FULL, NB_REST)

            def rsqrt(s, n):
                u, i, y, t = nt_u[:, 0:n], nt_i[:, 0:n], nt_y[:, 0:n], nt_t[:, 0:n]
                s.then(dve.tensor_scalar(i, u.bitcast(I32), 1, None, ALU.logical_shift_right))
                s.then(dve.tensor_scalar(y.bitcast(I32), i, -1.0, RSQRT_SEED, ALU.mult, ALU.add))
                for _ in range(NEWTON):
                    s.then(dve.tensor_tensor(t, y, y, ALU.mult))
                    s.then(dve.scalar_tensor_tensor(t, t, -0.5, u, ALU.mult, ALU.mult))
                    s.then(dve.scalar_tensor_tensor(y, t, 1.5, y, ALU.add, ALU.mult))

            def layernorm(s, h, full, halves16):
                s.then(dve.tensor_reduce(lsum[:, :], h, AX.X, ALU.add))
                s.then(dve.scalar_tensor_tensor(cen[:, :, :], lsum[:, :].unsqueeze(2).broadcast_to([P, TG, D]),
                                                -1.0 / D, h, ALU.mult, ALU.add))
                s.then(dve.tensor_tensor(lsq[:, :, :], cen[:, :, :], cen[:, :, :], ALU.mult))
                s.then(dve.tensor_reduce(lssq[:, :], lsq[:, :, :], AX.X, ALU.add))
                s.then(dve.tensor_scalar(nt_u[:, 0:TG], lssq[:, :], 1.0 / D, EPS, ALU.mult, ALU.add))
                rsqrt(s, TG)
                s.then(dve.tensor_tensor(full, cen[:, :, :], nt_y[:, 0:TG].unsqueeze(2).broadcast_to([P, TG, D]),
                                         ALU.mult))
                s.then(dve.tensor_copy(halves16[:, :, 0, :], full))
                s.then(dve.tensor_tensor(halves16[:, :, 1, :], full, halves16[:, :, 0, :], ALU.subtract))
                assert s.n == LN_STEPS

            def h_of(g):
                return h_all[:, bass.ds(TG * g, TG), :]

            def ln1(g):
                dve.wait_ge(h_arrived, g + 1)
                wait_past(dve, g_done, SPG * g)
                wait_past(dve, x1_turned, g)
                layernorm(Steps(dve, ln1_steps, LN_STEPS * g), h_of(g), x1[:, :, :], x1_16)

            def sums(g, j):
                dve.wait_ge(sq_ready, halves * g + j + 1)
                dve.tensor_reduce(ssq[:, j // 2, j % 2 * H:(j % 2 + 1) * H],
                                  sq[:, j % 4, :].rearrange("p (h d) -> p h d", d=D), AX.X, ALU.add
                                  ).then_inc(sums_ready, 1)

            def scale_x(g):
                s = Steps(dve, kvn_steps, KVN_STEPS * g)
                dve.wait_ge(sums_ready, halves * (g + 1))
                u = nt_u[:, :].rearrange("p (t k) -> p t k", k=2 * H)
                s.then(dve.tensor_tensor(u, ssq[:, :, :], inv_c2[:, :].unsqueeze(1).broadcast_to([P, TG, 2 * H]), ALU.mult))
                s.then(dve.tensor_scalar(nt_u[:, :], nt_u[:, :], EPS, None, ALU.add))
                rsqrt(s, TG * 2 * H)
                y = nt_y[:, :].rearrange("p (t a h) -> p t a h", a=2, h=H)
                s.then(dve.tensor_tensor(ksv[:, :, :], y[:, :, 0, :], y[:, :, 1, :], ALU.mult))
                assert s.n == KVN_STEPS
                wait_past(dve, g_done, SPG * g)
                for t in range(TG):
                    dve.tensor_tensor(xs[:, t, :, :], x1[:, t, :].unsqueeze(1).broadcast_to([P, H, D]),
                                      ksv[:, t, :].unsqueeze(2).broadcast_to([P, H, D]), ALU.mult).then_inc(xs_ready, 1)

            def split_m(g):
                s = Steps(dve, m_steps, M_STEPS * g)
                dve.wait_ge(m_done, g + 1)
                wait_past(dve, attn_done, g)
                s.then(dve.tensor_copy(m_f[:, :], bank[2][:, 0:SPG * D]))
                s.then(dve.tensor_copy(m_3[:, 0, :], m_f[:, :]))
                s.then(dve.tensor_tensor(m_r[:, :], m_f[:, :], m_3[:, 0, :], ALU.subtract))
                s.then(dve.tensor_copy(m_3[:, 1, :], m_r[:, :]))
                s.then(dve.tensor_tensor(m_3[:, 2, :], m_r[:, :], m_3[:, 1, :], ALU.subtract))
                assert s.n == M_STEPS

            def keep_x1(g):
                dve.wait_ge(x1_t_ready, g + 1)
                wait_past(dve, attn_done, g)
                dve.tensor_copy(x1_ta[:, :], x1_t[:, :]).then_inc(x1_kept, 1)

            def add_attention(g):
                s = Steps(dve, h2_steps, H2_STEPS * g)
                wait_past(dve, out_ready, g)
                dve.wait_ge(attn_done, g + 1)
                s.then(dve.tensor_tensor(h2[:, :, :], bank[3][:, 0:TG * D].rearrange("p (t d) -> p t d", d=D), h_of(g),
                                         ALU.add))
                s.then(dve.tensor_tensor(h2[:, :, :], h2[:, :, :], bo_all[:, :].unsqueeze(1).broadcast_to([P, TG, D]),
                                         ALU.add))
                assert s.n == H2_STEPS

            def ln2(g):
                wait_past(dve, x2_turned, g)
                layernorm(Steps(dve, ln2_steps, LN_STEPS * g), h2[:, :, :], x2[:, :, :], x2_16)

            def choose(g):
                s = Steps(dve, mask_steps, MASK_STEPS * g)
                dve.wait_ge(gate_done, g + 1)
                wait_past(dve, mask_turned, g)
                s.then(dve.tensor_tensor(score[:, :, :], bank[7][:, 0:TG * E].rearrange("p (t e) -> p t e", e=E),
                                         bg_all[:, :].unsqueeze(1).broadcast_to([P, TG, E]), ALU.add), alone=dve_waited)
                for t in range(TG):
                    s.then(dve.max(top[:, t, :], score[:, t, :]), alone=dve_waited)
                    s.then(dve.max_index(top_at[:, t, :], top[:, t, :], score[:, t, :]), alone=dve_waited)
                s.then(dve.tensor_copy(top_f[:, :, :], top_at[:, :, 0:2]))
                for n, one in enumerate((is0, is1)):
                    s.then(dve.tensor_tensor(one[:, :, :], expert_iota[:, :].unsqueeze(1).broadcast_to([P, TG, E]),
                                             top_f[:, :, n:n + 1].broadcast_to([P, TG, E]), ALU.is_equal))
                s.then(dve.tensor_tensor(mask[:, :, 1, :], is0[:, :, :], is1[:, :, :], ALU.add))
                s.then(dve.tensor_scalar(mask[:, :, 0, :], mask[:, :, 1, :], -1.0, 1.0, ALU.mult, ALU.add))
                assert s.n == MASK_STEPS

            def finish(g):
                dve.wait_ge(back_done, g + 1)
                wait_past(dve, out_sent, 16 * g)
                dve.tensor_tensor(outb[:, :, :], bank[7][:, 0:TG * D].rearrange("p (t d) -> p t d", d=D), h2[:, :, :],
                                  ALU.add).then_inc(out_ready, 1)

            def step(i, att, ffn, more):
                if att:
                    keep_x1(i)
                if ffn:
                    ln2(i - 1)
                for j in range(halves):
                    if att:
                        sums(i, j)
                    if ffn and j == 5:
                        choose(i - 1)
                if att:
                    scale_x(i)
                if more:
                    ln1(i + 1)
                if att:
                    split_m(i)
                if ffn:
                    finish(i - 1)
                if att:
                    add_attention(i)

            ln1(0)
            step(0, True, False, True)
            step(1, True, True, True)
            with dve.Fori(2, NGRP - 1) as i:
                step(i, True, True, True)
            step(NGRP - 1, True, True, False)
            step(NGRP, False, True, False)


CONSTS = 4 + 6 + 2 + 2 + 6
FOLD = 400
FOLD_LOOPS = 4
RANK_BANKS = 13


def kernel(**inputs):
    import numpy as np
    import concourse.bacc as bacc
    from concourse.bass_utils import run_bass_kernel_spmd

    laid = {"x": inputs["x"],
            "tables": np.concatenate([inputs["L0_tok_a_n"], inputs["L0_tok_b_n"]], axis=1)}
    for name in ("L0_tok_rule_transform", "L0_tok_token_rules", "L0_tok_proj_w", "L0_tok_proj_b", "L0_attn_w_qkv",
                 "L0_attn_w_out", "L0_attn_b_out", "L0_ffn_Wg", "L0_ffn_bg", "L0_ffn_W1", "L0_ffn_b1", "L0_ffn_W2",
                 "L0_ffn_b2"):
        laid[name] = inputs[name].T if name == "L0_ffn_b1" else inputs[name]
    nc = bacc.Bacc("TRN2", target_bir_lowering=False, num_devices=1)
    arrays, args = {}, []
    for name, a in laid.items():
        a = np.ascontiguousarray(a)
        arrays[f"in_{name}"] = a
        args.append(nc.dram_tensor(f"in_{name}", a.shape, mybir.dt.from_np(a.dtype), kind="ExternalInput").ap())
    shape = (*laid["x"].shape, laid["L0_tok_proj_w"].shape[0])
    out = nc.dram_tensor("out_0", shape, F32, kind="ExternalOutput").ap()
    program(nc, *args, out)
    r = run_bass_kernel_spmd(nc, [arrays], core_ids=[0])
    return r.results[0]["out_0"]
```

```python
from contextlib import ExitStack

import concourse.bass as bass
from concourse import mybir
from concourse.alu_op_type import AluOpType as ALU

F32, F16, BF16 = mybir.dt.float32, mybir.dt.float16, mybir.dt.bfloat16
I32, U32 = mybir.dt.int32, mybir.dt.uint32
ACT = mybir.ActivationFunctionType
AX = mybir.AxisListType

P = 128
EPS = 1e-5
PI = 3.141592653589793
ROUND = 12582912.0
RSQRT_SEED = 1597463007.0
NEWTON = 3
FAR = -1e30


class Steps:

    def __init__(self, eng, sem, base=0):
        self.eng, self.sem, self.base, self.n = eng, sem, base, 0

    def go(self, ins):
        ins.then_inc(self.sem, 1)
        self.n += 1

    def sync(self, alone=None):
        self.eng.wait_ge(self.sem, self.base + self.n)
        if alone is not None:
            self.eng.sem_inc(alone, 1)

    def then(self, ins, alone=None):
        self.go(ins)
        self.sync(alone)


def wait_past(eng, sem, value):
    if not isinstance(value, int) or value > 0:
        eng.wait_ge(sem, value)


def program(nc, x, tables, rule_transform, token_rules, proj_w, proj_b, w_qkv, w_out, b_out,
            wg, bg, w1, b1, w2, b2, out):
    B, S = x.shape
    V, NR = token_rules.shape[0], rule_transform.shape[0]
    D = proj_w.shape[0]
    H = w_qkv.shape[0] // (3 * D)
    E, _, HID = w1.shape
    T = B * S
    TPS = S // P
    NC = T // P
    W = 32
    SLOTS = T // W + NR
    SPT = P // W
    NG = SLOTS // SPT
    assert SLOTS % SPT == 0
    NPOS = SLOTS * W
    GB = 8
    NB_FULL, NB_REST = NG // GB, NG % GB
    NBATCH = NB_FULL + (NB_REST > 0)
    QB = GB * SPT
    SPG = 2
    TG = SPG * TPS
    NGRP = B // SPG
    GT = TG * P
    RB = 8
    CPB = 5

    with ExitStack() as ctx:
        def sb(name, shape, dt):
            return ctx.enter_context(nc.sbuf_tensor(name, shape, dt))

        def sem(name):
            return ctx.enter_context(nc.semaphore(name))

        bank = [ctx.enter_context(nc.psum_tensor(f"bank{i}", [P, 512], F32)) for i in range(8)]
        by_position = nc.dram_tensor("by_position", (NPOS, D), F32).ap()

        rule_iota = sb("rule_iota", [P, NR], BF16)
        part_iota = sb("part_iota", [P, P], BF16)
        tile_iota = sb("tile_iota", [P, NG], BF16)
        freq = sb("freq", [P, D], F32)
        slot_iota = sb("slot_iota", [P, SLOTS], F32)
        expert_iota = sb("expert_iota", [P, E], F32)
        before = sb("before", [P, P], BF16)
        upto = sb("upto", [P, P], BF16)
        ones_bf = sb("ones_bf", [P, P], BF16)
        ones_f = sb("ones_f", [P, P], F32)
        eye_f = sb("eye_f", [P, P], F32)
        eye_16 = sb("eye_16", [P, P], F16)
        eye_bf = sb("eye_bf", [P, P], BF16)
        center = sb("center", [D, D], F32)
        far = sb("far", [2 * E, E, HID], BF16)
        half_pi = sb("half_pi", [P, 1], F32)
        zeros = sb("zeros", [P, NR], F32)

        ids = sb("ids", [P, NC], I32)
        rules_i = sb("rules_i", [P, NC], I32)
        rules_bf = sb("rules_bf", [P, NC], BF16)
        fold = sb("fold", [P, NR * D], F32)
        pwb = sb("pwb", [D, D + 1], F32)
        rows = sb("rows", [P, NG * 2 * D], F32)
        has = rows[:, 0:NC * NR // 2].bitcast(BF16)
        run = rows[:, NC * NR // 2:(2 * NC + 1) * NR // 2].bitcast(BF16)
        has3 = has.rearrange("p (c r) -> p c r", r=NR)
        run3 = run.rearrange("p (c r) -> p c r", r=NR)
        trig_flat = sb("trig", [P, NG * 2 * D], F32)
        trig = trig_flat[:, :].rearrange("p (t a d) -> p t a d", a=2, d=D)
        tot_i = sb("tot_i", [P, NR], I32)
        tot_j = sb("tot_j", [P, NR], I32)
        slots_f = sb("slots_f", [P, NR], F32)
        slots_end = sb("slots_end", [P, NR], F32)
        start_i = sb("start_i", [P, NR], I32)
        start_a = sb("start_a", [P, NR], BF16)
        start_b = sb("start_b", [P, NR], BF16)
        ranked = sb("ranked", [P, CPB * NR], F32)
        pos_f = sb("pos_f", [P, NC], F32)
        pos_i = sb("pos_i", [P, NC], I32)
        pos_t = sb("pos_t", [P, NC], I32)
        pos_p = sb("pos_p", [P, NC], F32)
        pos_g = sb("pos_g", [P, NC], F32)
        id_f = sb("id_f", [P, NC], F32)
        NH = 4
        is_part = sb("is_part", [P, NH, P], F32)
        is_tile = sb("is_tile", [P, NH, NG], F32)
        spos_f = sb("spos_f", [P, NG], F32)
        spos_i = sb("spos_i", [P, NG], I32)
        col_i = sb("col_i", [P, 1], I32)
        col_j = sb("col_j", [P, 1], I32)
        col_n = sb("col_n", [P, 1], BF16)
        col_end = sb("col_end", [P, 1], F32)
        past = sb("past", [P, SLOTS], BF16)
        slot_f = sb("slot_f", [1, NBATCH * QB], F32)
        slot_at = sb("slot_at", [1, NBATCH * QB], I32)
        feats = sb("feats", [P, GB, D + 1], F32)
        feats_t = sb("feats_t", [P, GB * P], F32)
        mapped = sb("mapped", [W, QB * D], F32)
        h_all = sb("h_all", [P, NC, D], F32)

        wn = sb("wn", [D, 3 * H, D], F32)
        wc = sb("wc", [D, 2 * H, D], F32)
        wo = sb("wo", [D, H * D], F32)
        wo_t = sb("wo_t", [D, H, D], F32)
        wtmp = sb("wtmp", [P, 2 * H * D], F32)
        wkv_h = sb("wkv_h", [P, 2 * H * D], F16)
        wkv_l = sb("wkv_l", [P, 2 * H * D], F16)
        p_t = sb("p_t", [P, H // 2, P], F32)
        q_w = sb("q_w", [D, H, D], F32)
        fro = sb("fro", [D, 2 * H + E], F32)
        fro_all = sb("fro_all", [P, 2 * H + E], F32)
        fro_root = sb("fro_root", [P, 2 * H + E], F32)
        scale_up = sb("scale_up", [P, 2 * H + E], F32)
        scale_dn = sb("scale_dn", [P, 2 * H + E], F32)
        inv_c2 = sb("inv_c2", [P, 2 * H], F32)
        w1f = sb("w1f", [P, E, HID], F32)
        w1_h = sb("w1_h", [P, E, HID], F16)
        w1_l = sb("w1_l", [P, E, HID], F16)
        b1t = sb("b1t", [HID, E], F32)
        w2f = sb("w2f", [HID, E, D], F32)
        wgf = sb("wgf", [P, E], F32)
        wg_r = sb("wg_r", [P, E], F32)
        wg_3 = sb("wg_3", [P, 3, E], BF16)
        b2f = sb("b2f", [2 * E, D], F32)
        b2_r = sb("b2_r", [2 * E, D], F32)
        b2_3 = sb("b2_3", [2 * E, 3, D], BF16)
        bg_all = sb("bg_all", [P, E], F32)
        bo_all = sb("bo_all", [P, D], F32)

        taken = [0]

        def later(name, shape, dt):
            n = 1
            for k in shape[1:]:
                n *= k
            words = n * (2 if dt in (F16, BF16) else 4) // 4
            assert words * 4 == n * (2 if dt in (F16, BF16) else 4)
            if taken[0] < NG * 2 * D < taken[0] + words:
                taken[0] = NG * 2 * D
            o = taken[0] % (NG * 2 * D)
            v = (trig_flat if taken[0] < NG * 2 * D else rows)[0:shape[0], o:o + words]
            taken[0] += words
            assert taken[0] <= 2 * NG * 2 * D, name
            v = v if dt == F32 else v.bitcast(dt)
            if len(shape) == 2:
                return v
            names = ["a", "b", "c"][:len(shape) - 1]
            return v.rearrange(f"p ({' '.join(names)}) -> p {' '.join(names)}",
                               **dict(zip(names[1:], shape[2:])))

 
        NT = TG * (2 * H + 2)
        NT1, NT2 = TG * 2 * H, TG * (2 * H + 1)
        lsq = later("lsq", [P, 2, TG, D], F32)
        lsum = later("lsum", [P, 2, TG], F32)
        lssq = later("lssq", [P, 2, TG], F32)
        nt_u = later("nt_u", [P, NT], F32)
        nt_i = later("nt_i", [P, NT], I32)
        nt_y = later("nt_y", [P, NT], F32)
        nt_t = later("nt_t", [P, NT], F32)
        x1 = [later(f"x1_{p}", [P, TG, D], F32) for p in range(2)]
        x1_16 = later("x1_16", [P, TG, 2, D], F16)
        x1_t = [later(f"x1_t{p}", [P, GT], F16) for p in range(2)]
        sq = later("sq", [P, 4, 512], F32)
        ssq = later("ssq", [P, TG, 2 * H], F32)
        ksv = later("ksv", [P, TG, H], F32)
        xs = later("xs", [P, TG, H, D], F32)
        g_sb = later("g_sb", [D, SPG, H * D], F32)
        t_sb = later("t_sb", [P, H // 2, SPG, D], F32)
        m_f = later("m_f", [P, SPG * D], F32)
        m_r = later("m_r", [P, SPG * D], F32)
        m_3 = later("m_3", [P, 3, SPG * D], BF16)
        h2 = [later(f"h2_{p}", [P, TG, D], F32) for p in range(2)]
        x2 = later("x2", [P, TG, D], F32)
        x2_16 = later("x2_16", [P, TG, 2, D], F16)
        x2_t = [later(f"x2_t{p}", [P, GT], F16) for p in range(2)]
        score = later("score", [P, TG, E], F32)
        top = later("top", [P, TG, 8], F32)
        top_at = later("top_at", [P, TG, 8], U32)
        top_f = later("top_f", [P, TG, 2], F32)
        is0 = later("is0", [P, TG, E], F32)
        is1 = later("is1", [P, TG, E], F32)
        mask = later("mask", [P, TG, 2, E], BF16)
        mask_t = [later(f"mask_t{p}", [2 * E, GT], BF16) for p in range(2)]
        hid = later("hid", [P, 2, GT], F32)
        y_t = later("y_t", [D, GT], F32)
        outb = later("outb", [P, TG, D], F32)

        ids_in, const_first, const_sort, const_made = (
            sem(n) for n in ("ids_in", "const_first", "const_sort", "const_made"))
        pos_p_ready, parts_ready = sem("pos_p_ready"), sem("parts_ready")
        rules_in = [sem(f"rules_in{i}") for i in range(RB)]
        fold_in, qkv_in, wo_in, w1_in, w2_in, small_in = (
            sem(n) for n in ("fold_in", "qkv_in", "wo_in", "w1_in", "w2_in", "small_in"))
        cleared = sem("cleared")
        folded_done, folded = sem("folded_done"), sem("folded")
        wc_done, wc_ready = sem("wc_done"), sem("wc_ready")
        fro_ready, fro_done, fro_copied, root_ready = (
            sem(n) for n in ("fro_ready", "fro_done", "fro_copied", "root_ready"))
        wt_done, wt_used = sem("wt_done"), sem("wt_used")
        wot_done, wot_ready = sem("wot_done"), sem("wot_ready")
        pq_done, pq_ready = sem("pq_done"), sem("pq_ready")
        weights_ready = sem("weights_ready")
        prep_steps, sort_steps = sem("prep_steps"), sem("sort_steps")
        counts_ready, totals_done, starts_ready = (
            sem(n) for n in ("counts_ready", "totals_done", "starts_ready"))
        ranks_done, ranks_used = sem("ranks_done"), sem("ranks_used")
        cols_ready, cols_used, sorted_done = sem("cols_ready"), sem("cols_used"), sem("sorted_done")
        nslots_ready, ends_done, past_ready, slots_done, slots_ready = (
            sem(n) for n in ("nslots_ready", "ends_done", "past_ready", "slots_done", "slots_ready"))
        sorted_ready, pos_ready = sem("sorted_ready"), sem("pos_ready")
        angle_steps, angles_ready, trig_ready = sem("angle_steps"), sem("angles_ready"), sem("trig_ready")
        rows_in = [sem(f"rows_in{i}") for i in range(NBATCH)]
        rows_arrived = sem("rows_arrived")
        feats_steps, feats_ready, feats_turned, feats_t_ready = (
            sem(n) for n in ("feats_steps", "feats_ready", "feats_turned", "feats_t_ready"))
        slots_mapped, mapped_ready, mapped_out = (
            sem(n) for n in ("slots_mapped", "mapped_ready", "mapped_out"))
        h_in = [sem(f"h_in{i}") for i in range(NGRP)]
        h_arrived = sem("h_arrived")

        ln1_steps, kvn_steps, ln2_steps, mask_steps, m_steps, h2_steps = (
            sem(n) for n in ("ln1_steps", "kvn_steps", "ln2_steps", "mask_steps", "m_steps", "h2_steps"))
        x1_turned, x1_t_ready, rs_steps = sem("x1_turned"), sem("x1_t_ready"), sem("rs_steps")
        kv_done, sq_ready, sums_ready = sem("kv_done"), sem("sq_ready"), sem("sums_ready")
        xs_ready, g_done, g_ready = sem("xs_ready"), sem("g_done"), sem("g_ready")
        t_done, t_ready, m_done, attn_done = sem("t_done"), sem("t_ready"), sem("m_done"), sem("attn_done")
        x2_turned, x2_t_ready = sem("x2_turned"), sem("x2_t_ready")
        gate_done, mask_turned, mask_t_ready = sem("gate_done"), sem("mask_turned"), sem("mask_t_ready")
        w1_done, gelu_ready, w2_done = sem("w1_done"), sem("gelu_ready"), sem("w2_done")
        y_t_ready, back_done, out_ready, out_sent = (
            sem(n) for n in ("y_t_ready", "back_done", "out_ready", "out_sent"))

        pe_waited, dve_waited, act_waited = sem("pe_waited"), sem("dve_waited"), sem("act_waited")

        LN_STEPS = 5 + 3
        KVN_STEPS = 2 + 1
        ANGLE_STEPS = 3
        RS_STEPS = 2 + 3 * NEWTON
        MASK_STEPS = 3 + 2 * TG + 3
        M_STEPS = 5
        H2_STEPS = 2
        halves = 2 * TG

        def cols_by(c):
            return c + 1 + c // 2 + 1

        def at_work(i):
            return tuple(0 <= g < NGRP for g in (i, i - 1, i - 2, i - 3, i + 1, i + 2))

        block = ctx.enter_context(nc.Block())

        @block.sync
        def _(sp):
            sp.dma_start(ids[:, :].rearrange("p (b s) -> p b s", s=TPS),
                         x.rearrange("b (p s) -> p b s", s=TPS)).then_inc(ids_in, 16)
            sp.dma_start(fold[0:D, :].rearrange("d (r e) -> d r e", e=D),
                         rule_transform.rearrange("r d e -> d r e")).then_inc(fold_in, 16)
            sp.dma_start(pwb[:, 0:D], proj_w).then_inc(fold_in, 16)
            sp.dma_start(pwb[:, D:D + 1], proj_b.rearrange("(d o) -> d o", o=1)).then_inc(fold_in, 16)
            sp.dma_start(wn[:, :, :], w_qkv.rearrange("(g e) d -> e g d", e=D)).then_inc(qkv_in, 16)
            sp.dma_start(wo[:, :], w_out).then_inc(wo_in, 16)
            for half in range(2):
                sp.dma_start(w1f[half * D:(half + 1) * D, :, :],
                             w1.rearrange("e d h -> d e h")).then_inc(w1_in, 16)
            sp.dma_start(w2f[:, :, :], w2.rearrange("e h d -> h e d")).then_inc(w2_in, 16)
            for half in range(2):
                sp.dma_start(wgf[half * D:(half + 1) * D, :], wg).then_inc(small_in, 16)
            sp.wait_ge(cleared, 3)
            sp.dma_start(b2f[E:2 * E, :], b2).then_inc(small_in, 16)
            sp.dma_start(b1t[:, :], b1).then_inc(small_in, 16)
            sp.dma_start(bg_all[:, :], bg.partition_broadcast(P)).then_inc(small_in, 16)
            sp.dma_start(bo_all[:, :], b_out.partition_broadcast(P)).then_inc(small_in, 16)
            posv = by_position[0:NB_FULL * QB * W, :].rearrange("(k q p) d -> k p q d", p=W, q=QB)
            with sp.Fori(0, NB_FULL) as k:
                sp.wait_ge(mapped_ready, k + 1)
                sp.dma_start(posv[k], mapped[:, :].rearrange("p (q d) -> p q d", d=D)).then_inc(mapped_out, 16)
            if NB_REST:
                sp.wait_ge(mapped_ready, NBATCH)
                sp.dma_start(by_position[NB_FULL * QB * W:NPOS, :].rearrange("(q p) d -> p q d", p=W),
                             mapped[:, 0:NB_REST * SPT * D].rearrange("p (q d) -> p q d", d=D)
                             ).then_inc(mapped_out, 16)
            outv = out.rearrange("(g q) (p s) d -> g p q (s d)", q=SPG, s=TPS)
            with sp.Fori(0, NGRP) as g:
                sp.wait_ge(out_ready, g + 1)
                sp.dma_start(outv[g], outb[:, :, :].rearrange("p (q s) d -> p q (s d)", s=TPS)
                             ).then_inc(out_sent, 16)
            sp.wait_ge(out_sent, 16 * NGRP)

        @block.gpsimd
        def _(pool):
            def triangle(c, t, base):
                c.then(pool.memset(t[:, :], 0.0))
                c.then(pool.affine_select(t[:, :], t[:, :], pattern=[[-1, P]], compare_op=ALU.is_ge,
                                          fill=1.0, base=base, channel_multiplier=1))

            def identity(c, t, off, diagonal):
                n = t.shape[1]
                c.then(pool.memset(t[:, :], off))
                c.then(pool.affine_select(t[:, :], t[:, :], pattern=[[-1, n]], compare_op=ALU.not_equal,
                                          fill=diagonal, base=0, channel_multiplier=1))

            def count(c, t, first=0):
                c.then(pool.iota(t[:, :], pattern=[[1, t.shape[1]]], base=first, channel_multiplier=0,
                                 allow_small_or_imprecise_dtypes=True))

            c = Steps(pool, const_first)
            identity(c, center, -1.0 / D, 1.0 - 1.0 / D)
            identity(c, eye_f, 0.0, 1.0)
            count(c, rule_iota)
            assert c.n == CONST_FIRST
            pool.wait_ge(ids_in, 16)
            for t in range(NC):
                pool.indirect_dma_start(rules_i[:, t:t + 1], None, token_rules.rearrange("(v o) -> v o", o=1),
                                        bass.IndirectOffsetOnAxis(ap=ids[:, t:t + 1], axis=0)
                                        ).then_inc(rules_in[t * RB // NC], 16)
            c = Steps(pool, const_sort)
            triangle(c, before, 0)
            triangle(c, upto, -1)
            count(c, slot_iota)
            count(c, part_iota)
            count(c, tile_iota)
            count(c, freq, 1)
            assert c.n == CONST_SORT
            c = Steps(pool, const_made)
            identity(c, eye_16, 0.0, 1.0)
            identity(c, eye_bf, 0.0, 1.0)
            count(c, expert_iota)
            c.then(pool.memset(far[:, :, :], 0.0))
            c.then(pool.affine_select(far[:, :, :], far[:, :, :], pattern=[[-1, E], [0, HID]],
                                      compare_op=ALU.not_equal, fill=FAR, base=0, channel_multiplier=1))
            assert c.n == CONSTS
            pool.wait_ge(pos_p_ready, 1)
            for c in range(1, NC, 2):
                if c >= NH:
                    pool.wait_ge(cols_used, c - NH + 1)
                pool.tensor_scalar(is_part[:, c % NH, :], part_iota[:, :], pos_p[:, c:c + 1], None,
                                   ALU.is_equal).then_inc(parts_ready, 1)
            pool.wait_ge(sorted_ready, 1)
            pool.wait_ge(ranks_used, RANK_BANKS)
            for k in range(NBATCH):
                for t in range(k * GB, min(k * GB + GB, NG)):
                    pool.indirect_dma_start(rows[:, t * 2 * D:(t + 1) * 2 * D], None, tables,
                                            bass.IndirectOffsetOnAxis(ap=spos_i[:, t:t + 1], axis=0)
                                            ).then_inc(rows_in[k], 16)
                if k:
                    pool.wait_ge(rows_in[k - 1], 16 * GB)
                    pool.sem_inc(rows_arrived, 1)
            pool.wait_ge(rows_in[NBATCH - 1], 16 * (NG - (NBATCH - 1) * GB))
            pool.sem_inc(rows_arrived, 1)
            pool.wait_ge(mapped_out, 16 * NBATCH)
            pool.wait_ge(pos_ready, 1)
            for g in range(NGRP):
                for t in range(g * TG, (g + 1) * TG):
                    pool.indirect_dma_start(h_all[:, t, :], None, by_position,
                                            bass.IndirectOffsetOnAxis(ap=pos_i[:, t:t + 1], axis=0)
                                            ).then_inc(h_in[g], 16)
                if g:
                    pool.wait_ge(h_in[g - 1], 16 * TG)
                    pool.sem_inc(h_arrived, 1)
            pool.wait_ge(h_in[NGRP - 1], 16 * TG)
            pool.sem_inc(h_arrived, 1)

        @block.scalar
        def _(act):
            act.wait_ge(wc_done, 1)
            act.activation(wc[:, 0:H, :], bank[4][0:D, :].rearrange("p (h d) -> p h d", d=D), ACT.Copy).then_inc(wc_ready, 1)
            act.activation(wc[:, H:2 * H, :], bank[5][0:D, :].rearrange("p (h d) -> p h d", d=D), ACT.Copy).then_inc(wc_ready, 1)
            act.wait_ge(wot_done, 1)
            act.activation(wo_t[:, :, :], bank[7][0:D, :].rearrange("p (h d) -> p h d", d=D), ACT.Copy).then_inc(wot_ready, 1)
            act.wait_ge(fro_copied, 1)
            act.activation(fro_root[:, :], fro_all[:, :], ACT.Sqrt).then_inc(root_ready, 1)
            act.wait_ge(pq_done, 1)
            for i in range(2):
                act.activation(p_t[:, :, i * D:(i + 1) * D],
                               bank[2][:, 0:H // 2 * D].rearrange("p (h d) -> p h d", d=D), ACT.Copy).then_inc(pq_ready, 1)
            act.activation(q_w[:, :, :], bank[3][0:D, :].rearrange("p (h d) -> p h d", d=D), ACT.Copy,
                           scale=1.0 / S).then_inc(pq_ready, 1)
            with act.Fori(0, FOLD_LOOPS) as k:
                for j in range(4):
                    act.wait_ge(folded_done, 4 * k + j + 1)
                    act.activation(fold[0:D + 1, bass.ds(FOLD * (4 * k + j), FOLD)], bank[j][0:D + 1, 0:FOLD],
                                   ACT.Copy).then_inc(folded, 1)

            def trigs(k, tiles):
                lo, hi = trig[:, bass.ds(k * GB, tiles), 0, :], trig[:, bass.ds(k * GB, tiles), 1, :]
                act.wait_ge(angles_ready, k + 1)
                act.sem_inc(act_waited, 1)
                act.activation(lo, hi, ACT.Abs).then_inc(trig_ready, 1)
                act.wait_ge(trig_ready, 3 * k + 1)
                act.sem_inc(act_waited, 1)
                act.activation(hi, hi, ACT.Sin, scale=2 * PI / V).then_inc(trig_ready, 1)
                act.activation(lo, lo, ACT.Sin, scale=-2 * PI / V, bias=half_pi[:, 0:1]).then_inc(trig_ready, 1)

            def batch_evac(k, tiles):
                wait_past(act, slots_mapped, 4 * k)
                for j in range(2):
                    n = min(max(tiles - 4 * j, 0), 4)
                    if n:
                        act.wait_ge(feats_turned, 2 * k + j + 1)
                        act.activation(feats_t[0:D + 1, 4 * j * P:(4 * j + n) * P], bank[4 + j][0:D + 1, 0:n * P],
                                       ACT.Copy).then_inc(feats_t_ready, 1)
                wait_past(act, mapped_out, 16 * k)
                for j in range(4):
                    n = min(max(tiles * SPT - 8 * j, 0), 8)
                    if n:
                        act.wait_ge(slots_mapped, 4 * k + j + 1)
                        ins = act.activation(mapped[:, 8 * j * D:(8 * j + n) * D], bank[j][0:W, 0:n * D], ACT.Copy)
                ins.then_inc(mapped_ready, 1)

            trigs(0, GB)
            trigs(1, GB)
            batch_evac(0, GB)
            with act.Fori(1, NB_FULL - 1) as k:
                trigs(k + 1, GB)
                batch_evac(k, GB)
            if NB_REST:
                trigs(NB_FULL, NB_REST)
            batch_evac(NB_FULL - 1, GB)
            if NB_REST:
                batch_evac(NB_FULL, NB_REST)

            def x1_evac(g, par):
                act.wait_ge(x1_turned, g + 1)
                wait_past(act, attn_done, g - 1)
                act.activation(x1_t[par][:, :], bank[1][:, :].bitcast(F16)[:, 0:GT], ACT.Copy).then_inc(x1_t_ready, 1)

            def square(g, j):
                act.wait_ge(kv_done, halves * g + j + 1)
                wait_past(act, sums_ready, halves * g + j - 3)
                act.activation(sq[:, j % 4, :], bank[j % 2][:, :], ACT.Square).then_inc(sq_ready, 1)

            def g_evac(g):
                for s in range(SPG):
                    act.wait_ge(g_done, SPG * g + s + 1)
                    act.activation(g_sb[:, s, :], bank[2 + s][0:D, :], ACT.Copy).then_inc(g_ready, 1)

            def t_evac(g, s):
                wait_past(act, m_done, g)
                act.wait_ge(t_done, SPG * g + s + 1)
                act.activation(t_sb[:, :, s, :], bank[2 + s][:, 0:H // 2 * D].rearrange("p (h d) -> p h d", d=D),
                               ACT.Copy).then_inc(t_ready, 1)

            def x2_evac(g, par):
                act.wait_ge(x2_turned, g + 1)
                wait_past(act, w1_done, E * (g - 1))
                act.activation(x2_t[par][:, :], bank[7][:, :].bitcast(F16)[:, 0:GT], ACT.Copy).then_inc(x2_t_ready, 1)

            def mask_evac(g, par):
                act.wait_ge(mask_turned, g + 1)
                wait_past(act, back_done, g - 1)
                act.activation(mask_t[par][:, :], bank[7][0:2 * E, :].bitcast(BF16)[:, 0:GT], ACT.Copy
                               ).then_inc(mask_t_ready, 1)

            def gelu(g, e):
                act.wait_ge(w1_done, E * g + e + 1)
                wait_past(act, w2_done, E * g + e - 1)
                act.activation(hid[:, e % 2, :], bank[4 + e % 2][:, :], ACT.Gelu, bias=b1t[:, e:e + 1],
                               scale=scale_dn[:, 2 * H + e:2 * H + e + 1]).then_inc(gelu_ready, 1)

            def y_evac(g):
                act.wait_ge(w2_done, E * g + E)
                wait_past(act, back_done, g)
                act.activation(y_t[:, :], bank[6][0:D, :], ACT.Copy).then_inc(y_t_ready, 1)

            def step(i, par, att, mid, ffn, end, more, _):
                def squares(*js):
                    if att:
                        for j in js:
                            square(i, j)

                def gelus(*es):
                    if ffn:
                        for e in es:
                            gelu(i - 2, e)

                squares(0, 1)
                if ffn:
                    mask_evac(i - 2, par)
                if end:
                    gelu(i - 3, 7)
                squares(2, 3)
                if mid:
                    t_evac(i - 1, 0)
                if end:
                    y_evac(i - 3)
                squares(4)
                if mid:
                    t_evac(i - 1, 1)
                squares(5, 6, 7)
                gelus(0, 1, 2, 3, 4)
                if att:
                    g_evac(i)
                if mid:
                    x2_evac(i - 1, 1 - par)
                gelus(5)
                if more:
                    x1_evac(i + 1, 1 - par)
                gelus(6)

            x1_evac(0, 0)
            for i in range(4):
                step(i, i % 2, *at_work(i))
            with act.Fori(2, NGRP // 2 - 1) as k:
                step(2 * k, 0, *at_work(4))
                step(2 * k + 1, 1, *at_work(4))
            for i in range(NGRP - 2, NGRP + 3):
                step(i, i % 2, *at_work(i))

        @block.tensor
        def _(pe):
            pe.wait_ge(const_first, CONST_FIRST)
            pe.wait_ge(cleared, 4)
            pe.wait_ge(qkv_in, 16)
            for i in range(2):
                ins = pe.matmul(bank[4 + i][0:D, :], center[:, :],
                                wn[:, H * (1 + i):H * (2 + i), :].rearrange("p h d -> p (h d)"), start=True, stop=True)
            ins.then_inc(wc_done, 1)
            for half in range(2):
                for g in range(2 * H):
                    ins = pe.matmul(bank[g // H][half * D:(half + 1) * D, g % H * D:(g % H + 1) * D],
                                    wn[:, H + g, :], center[:, :], start=True, stop=True)
            ins.then_inc(wt_done, 1)
            pe.wait_ge(wo_in, 16)
            for h in range(H):
                ins = pe.transpose(bank[7][0:D, h * D:(h + 1) * D], wo[:, h * D:(h + 1) * D], eye_f[0:D, 0:D])
            ins.then_inc(wot_done, 1)
            pe.wait_ge(fro_ready, 1)
            pe.matmul(bank[6][:, 0:2 * H + E], ones_f[0:D, :], fro[:, :], start=True, stop=True).then_inc(fro_done, 1)
            pe.wait_ge(wc_ready, 2)
            pe.wait_ge(wot_ready, 1)
            for h in range(H):
                ins = pe.matmul(bank[2][h % 2 * D:(h % 2 + 1) * D, h // 2 * D:(h // 2 + 1) * D],
                                wc[:, h, :], wn[:, h, :], start=True, stop=True)
            for h in range(H):
                ins = pe.matmul(bank[3][0:D, h * D:(h + 1) * D], wc[:, H + h, :], wo_t[:, h, :],
                                start=True, stop=True)
            ins.then_inc(pq_done, 1)
            pe.wait_ge(fold_in, 48)
            pe.wait_ge(wt_used, 1)
            pe.wait_ge(pq_ready, 3)
            for j in range(4):
                pe.matmul(bank[j][0:D + 1, 0:FOLD], pwb[:, :], fold[0:D, FOLD * j:FOLD * (j + 1)],
                          start=True, stop=True).then_inc(folded_done, 1)
            with pe.Fori(1, FOLD_LOOPS) as k:
                for j in range(4):
                    pe.wait_ge(folded, 4 * k + j - 3)
                    pe.matmul(bank[j][0:D + 1, 0:FOLD], pwb[:, :], fold[0:D, bass.ds(FOLD * (4 * k + j), FOLD)],
                              start=True, stop=True).then_inc(folded_done, 1)

            pe.wait_ge(counts_ready, 1)
            pe.wait_ge(folded, 4 * FOLD_LOOPS)
            pe.matmul(bank[0][:, 0:NR], ones_bf[:, :], run3[:, NC, :], start=True, stop=True)
            pe.matmul(bank[1][0:NR, 0:1], run3[:, NC, :], ones_bf[:, 0:1], start=True, stop=True).then_inc(totals_done, 1)
            pe.wait_ge(const_sort, CONST_SORT)
            pe.wait_ge(nslots_ready, 1)
            pe.matmul(bank[1][0:NR, 4:5], upto[0:NR, 0:NR], col_n[0:NR, :], start=True, stop=True).then_inc(ends_done, 1)
            pe.wait_ge(past_ready, 1)
            pe.matmul(bank[1][0:1, 0:SLOTS], ones_bf[0:NR, 0:1], past[0:NR, :], start=True, stop=True).then_inc(slots_done, 1)
            pe.wait_ge(starts_ready, 1)
            for k in range(RANK_BANKS):
                if k >= 4:
                    pe.wait_ge(ranks_used, k - 3)
                for c in range(k * CPB, min(k * CPB + CPB, NC)):
                    o = bank[2 + k % 4][:, (c % CPB) * NR:(c % CPB + 1) * NR]
                    pe.matmul(o, before[:, :], has3[:, c, :], start=True, stop=False)
                    pe.matmul(o, ones_bf[:, :], run3[:, c, :], start=False, stop=False)
                    pe.matmul(o, ones_bf[:, :], start_a[:, :], start=False, stop=False)
                    ins = pe.matmul(o, ones_bf[:, :], start_b[:, :], start=False, stop=True)
                ins.then_inc(ranks_done, 1)
            for c in range(NC):
                pe.wait_ge(cols_ready, cols_by(c))
                if c % 2:
                    pe.wait_ge(parts_ready, c // 2 + 1)
                pe.matmul(bank[6][:, 0:NG], is_part[:, c % NH, :], is_tile[:, c % NH, :],
                          start=(c == 0), stop=(c == NC - 1)).then_inc(cols_used, 1)

            def batch(k, tiles):
                pe.wait_ge(feats_ready, k + 1)
                for j in range(2):
                    for t in range(4 * j, min(4 * j + 4, tiles)):
                        ins = pe.transpose(bank[4 + j][0:D + 1, (t - 4 * j) * P:(t - 4 * j + 1) * P], feats[:, t, :],
                                           eye_f[:, :])
                    if 4 * j < tiles:
                        ins.then_inc(feats_turned, 1)
                for j in range(4):
                    n = min(max(tiles * SPT - 8 * j, 0), 8)
                    if j in (0, 2) and 2 * j < tiles:
                        pe.wait_ge(feats_t_ready, 2 * k + j // 2 + 1)
                    if n:
                        _, at = nc.values_load_multi_w_load_instructions(
                            slot_at[0:1, bass.ds(QB * k + 8 * j, 8)], engines=[mybir.EngineType.PE],
                            min_val=0, max_val=(NR - 1) * D,
                            skip_runtime_bounds_check_because="the least of it and the last rule's is stored")
                    for q in range(n):
                        s = 8 * j + q
                        ins = pe.matmul(bank[j][0:W, q * D:(q + 1) * D], feats_t[:, s * W:(s + 1) * W],
                                        fold[:, bass.ds(at[q], D)], start=True, stop=True)
                    if n:
                        ins.then_inc(slots_mapped, 1)

            pe.wait_ge(slots_ready, 1)
            pe.wait_ge(sorted_ready, 1)
            pe.wait_ge(ranks_used, RANK_BANKS)
            pe.wait_ge(cleared, 8)
            batch(0, GB)
            with pe.Fori(1, NB_FULL) as k:
                pe.wait_ge(mapped_ready, k)
                batch(k, GB)
            if NB_REST:
                pe.wait_ge(mapped_ready, NB_FULL)
                batch(NB_FULL, NB_REST)

            def x1_turn(g):
                pe.wait_ge(ln1_steps, LN_STEPS * (g + 1))
                wait_past(pe, sq_ready, halves * g)
                for t in range(TG):
                    ins = pe.transpose(bank[1][:, :].bitcast(F16)[:, t * P:(t + 1) * P],
                                       x1_16[:, t, :, :].rearrange("p a d -> p (a d)"), eye_16[:, :])
                ins.then_inc(x1_turned, 1)

            def kv(g, par, j):
                if j == 0:
                    pe.wait_ge(x1_t_ready, g + 1)
                wait_past(pe, sq_ready, halves * g + j - 1)
                cols = slice(j % 2 * H * D, (j % 2 + 1) * H * D)
                lhs = x1_t[par][:, j // 2 * P:(j // 2 + 1) * P]
                pe.matmul(bank[j % 2][:, :], lhs, wkv_h[:, cols], start=True, stop=False)
                pe.matmul(bank[j % 2][:, :], lhs, wkv_l[:, cols], start=False, stop=True).then_inc(kv_done, 1)

            def gram(g, par):
                wait_past(pe, m_steps, M_STEPS * g)
                wait_past(pe, h2_steps, H2_STEPS * g)
                for s in range(SPG):
                    for t in range(TPS):
                        pe.wait_ge(xs_ready, TG * g + s * TPS + t + 1)
                        ins = pe.matmul(bank[2 + s][0:D, :], x1[par][:, s * TPS + t, :],
                                        xs[:, s * TPS + t, :, :].rearrange("p h d -> p (h d)"),
                                        start=(t == 0), stop=(t == TPS - 1))
                    ins.then_inc(g_done, 1)

            def times_q(g, s):
                pe.wait_ge(g_ready, SPG * g + s + 1)
                pe.sem_inc(pe_waited, 1)
                for h in range(H):
                    ins = pe.matmul(bank[2 + s][h % 2 * D:(h % 2 + 1) * D, h // 2 * D:(h // 2 + 1) * D],
                                    g_sb[:, s, h * D:(h + 1) * D], q_w[:, h, :], start=True, stop=True)
                ins.then_inc(t_done, 1)

            def p_times(g):
                pe.wait_ge(t_ready, SPG * (g + 1))
                for h in range(H // 2):
                    ins = pe.matmul(bank[2][:, 0:SPG * D], p_t[:, h, :], t_sb[:, h, :, :].rearrange("p s d -> p (s d)"),
                                    start=(h == 0), stop=(h == H // 2 - 1))
                ins.then_inc(m_done, 1)

            def attend(g, par):
                pe.wait_ge(m_steps, M_STEPS * (g + 1))
                for t in range(TG):
                    for part in range(3):
                        ins = pe.matmul(bank[3][:, t * D:(t + 1) * D], x1_t[par][:, t * P:(t + 1) * P],
                                        m_3[:, part, t // TPS * D:(t // TPS + 1) * D], start=(part == 0), stop=(part == 2))
                ins.then_inc(attn_done, 1)

            def x2_turn(g):
                pe.wait_ge(ln2_steps, LN_STEPS * (g + 1))
                wait_past(pe, out_ready, g - 1)
                for t in range(TG):
                    ins = pe.transpose(bank[7][:, :].bitcast(F16)[:, t * P:(t + 1) * P],
                                       x2_16[:, t, :, :].rearrange("p a d -> p (a d)"), eye_16[:, :])
                ins.then_inc(x2_turned, 1)

            def gate(g, par):
                pe.wait_ge(x2_t_ready, g + 1)
                for t in range(TG):
                    for part in range(3):
                        ins = pe.matmul(bank[7][:, t * E:(t + 1) * E], x2_t[par][:, t * P:(t + 1) * P], wg_3[:, part, :],
                                        start=(part == 0), stop=(part == 2))
                ins.then_inc(gate_done, 1)

            def mask_turn(g):
                pe.wait_ge(mask_steps, MASK_STEPS * (g + 1))
                for t in range(TG):
                    ins = pe.transpose(bank[7][0:2 * E, :].bitcast(BF16)[:, t * P:(t + 1) * P],
                                       mask[:, t, :, :].rearrange("p a e -> p (a e)"), eye_bf[:, :])
                ins.then_inc(mask_turned, 1)

            def up(g, par, e):
                if e == 0:
                    pe.wait_ge(mask_t_ready, g + 1)
                wait_past(pe, gelu_ready, E * g + e - 1)
                o = bank[4 + e % 2][:, :]
                pe.matmul(o, w1_h[:, e, :], x2_t[par][:, :], start=True, stop=False)
                pe.matmul(o, w1_l[:, e, :], x2_t[par][:, :], start=False, stop=False)
                pe.matmul(o, far[:, e, :], mask_t[par][:, :], start=False, stop=True).then_inc(w1_done, 1)

            def down(g, e):
                pe.wait_ge(gelu_ready, E * g + e + 1)
                if e == 0:
                    wait_past(pe, y_t_ready, g)
                pe.matmul(bank[6][0:D, :], w2f[:, e, :], hid[:, e % 2, :], start=(e == 0), stop=(e == E - 1)
                          ).then_inc(w2_done, 1)

            def back(g, par, masks):
                pe.wait_ge(y_t_ready, g + 1)
                pe.wait_ge(mask_t_ready, masks)
                wait_past(pe, out_ready, g)
                for t in range(TG):
                    o = bank[7][:, t * D:(t + 1) * D]
                    pe.matmul(o, y_t[:, t * P:(t + 1) * P], eye_f[0:D, 0:D], start=True, stop=False)
                    for part in range(3):
                        ins = pe.matmul(o, mask_t[par][:, t * P:(t + 1) * P], b2_3[:, part, :], start=False,
                                        stop=(part == 2))
                ins.then_inc(back_done, 1)

            def step(i, par, att, mid, ffn, end, more, _):
                def kvs(*js):
                    if att:
                        for j in js:
                            kv(i, par, j)

                def expert(e):
                    if ffn:
                        up(i - 2, par, e)
                        if e:
                            down(i - 2, e - 1)

                kvs(0, 1)
                if ffn:
                    mask_turn(i - 2)
                if end:
                    up(i - 3, 1 - par, 7)
                    down(i - 3, 6)
                kvs(2, 3)
                if mid:
                    times_q(i - 1, 0)
                if end:
                    down(i - 3, 7)
                kvs(4)
                if mid:
                    times_q(i - 1, 1)
                kvs(5)
                if end:
                    back(i - 3, 1 - par, i - 1 if mid or ffn else NGRP)
                kvs(6, 7)
                if mid:
                    p_times(i - 1)
                expert(0)
                expert(1)
                if mid:
                    attend(i - 1, 1 - par)
                expert(2)
                expert(3)
                expert(4)
                if att:
                    gram(i, par)
                if mid:
                    x2_turn(i - 1)
                expert(5)
                if more:
                    x1_turn(i + 1)
                if mid:
                    gate(i - 1, 1 - par)
                expert(6)

            pe.wait_ge(const_made, CONSTS)
            pe.wait_ge(weights_ready, 1)
            pe.wait_ge(mapped_ready, NBATCH)
            x1_turn(0)
            for i in range(4):
                step(i, i % 2, *at_work(i))
            with pe.Fori(2, NGRP // 2 - 1) as k:
                step(2 * k, 0, *at_work(4))
                step(2 * k + 1, 1, *at_work(4))
            for i in range(NGRP - 2, NGRP + 3):
                step(i, i % 2, *at_work(i))

        @block.vector
        def _(dve):
            dve.memset(ones_bf[:, :], 1.0).then_inc(cleared, 1)
            dve.memset(ones_f[:, :], 1.0).then_inc(cleared, 1)
            dve.memset(b2f[:, :], 0.0).then_inc(cleared, 1)
            dve.memset(run3[:, 0, :], 0.0).then_inc(cleared, 1)
            dve.memset(zeros[:, :], 0.0).then_inc(cleared, 1)
            dve.memset(half_pi[:, :], PI / 2).then_inc(cleared, 1)
            dve.memset(feats[:, :, D:D + 1], 1.0).then_inc(cleared, 1)
            dve.memset(feats_t[D:P, :], 0.0).then_inc(cleared, 1)
            dve.memset(fold[D:P, :], 0.0).then_inc(cleared, 1)
            dve.memset(slot_at[:, :], 0).then_inc(cleared, 1)
            dve.wait_ge(cleared, 10)

            s = Steps(dve, prep_steps)
            dve.wait_ge(wc_ready, 2)
            t3 = wtmp[0:D, :].rearrange("p (g d) -> p g d", d=D)
            s.then(dve.tensor_tensor(t3, wc[:, :, :], wc[:, :, :], ALU.mult))
            s.then(dve.tensor_reduce(fro[:, 0:2 * H], t3, AX.X, ALU.add))
            dve.wait_ge(w1_in, 32)
            t3 = wtmp[0:D, :].rearrange("p (e h) -> p e h", h=HID)
            s.then(dve.tensor_tensor(t3, w1f[0:D, :, :], w1f[0:D, :, :], ALU.mult))
            dve.tensor_reduce(fro[:, 2 * H:2 * H + E], t3, AX.X, ALU.add).then_inc(fro_ready, 1)
            dve.wait_ge(fro_done, 1)
            dve.tensor_scalar(fro_all[:, :], bank[6][:, 0:2 * H + E], 1e-20, None, ALU.add).then_inc(fro_copied, 1)
            dve.wait_ge(root_ready, 1)
            s.then(dve.reciprocal(scale_up[:, :], fro_root[:, :]))
            s.then(dve.tensor_scalar(scale_up[:, :], scale_up[:, :], 1024.0, None, ALU.mult))
            s.then(dve.reciprocal(scale_dn[:, :], scale_up[:, :]))
            s.then(dve.tensor_scalar(inv_c2[:, :], scale_dn[:, 0:2 * H], 1.0 / D, None, ALU.mult))
            s.then(dve.tensor_tensor(inv_c2[:, :], inv_c2[:, :], scale_dn[:, 0:2 * H], ALU.mult))
            dve.wait_ge(wt_done, 1)
            for i in range(2):
                ins = dve.tensor_tensor(wtmp[:, i * H * D:(i + 1) * H * D].rearrange("p (h d) -> p h d", d=D),
                                        bank[i][:, :].rearrange("p (h d) -> p h d", d=D),
                                        scale_up[:, i * H:(i + 1) * H].unsqueeze(2).broadcast_to([P, H, D]), ALU.mult)
                ins.then_inc(wt_used, 1) if i else s.then(ins)
            dve.wait_ge(wt_used, 1)
            s.then(dve.tensor_copy(wkv_h[:, :], wtmp[:, :]))
            s.then(dve.tensor_tensor(wkv_l[:, :], wtmp[:, :], wkv_h[:, :], ALU.subtract))
            s.then(dve.tensor_tensor(w1f[:, :, :], w1f[:, :, :],
                                     scale_up[:, 2 * H:2 * H + E].unsqueeze(2).broadcast_to([P, E, HID]), ALU.mult))
            s.then(dve.tensor_copy(w1_h[:, :, :], w1f[:, :, :]))
            s.then(dve.tensor_tensor(w1_l[:, :, :], w1f[:, :, :], w1_h[:, :, :], ALU.subtract))
            dve.wait_ge(small_in, 16 * 6)
            for full, rest, parts in ((wgf, wg_r, wg_3), (b2f, b2_r, b2_3)):
                s.then(dve.tensor_copy(parts[:, 0, :], full[:, :]))
                s.then(dve.tensor_tensor(rest[:, :], full[:, :], parts[:, 0, :], ALU.subtract))
                s.then(dve.tensor_copy(parts[:, 1, :], rest[:, :]))
                s.then(dve.tensor_tensor(parts[:, 2, :], rest[:, :], parts[:, 1, :], ALU.subtract))
            dve.wait_ge(w2_in, 16)
            dve.wait_ge(pq_ready, 3)
            dve.sem_inc(weights_ready, 1)

            s = Steps(dve, sort_steps)
            dve.wait_ge(const_first, CONST_FIRST)
            s.then(dve.tensor_copy(id_f[:, :], ids[:, :]))
            n = NC // RB
            for b in range(RB):
                dve.wait_ge(rules_in[b], 16 * n)
                s.then(dve.tensor_copy(rules_bf[:, b * n:(b + 1) * n], rules_i[:, b * n:(b + 1) * n]))
                s.then(dve.tensor_tensor(has3[:, b * n:(b + 1) * n, :],
                                         rules_bf[:, b * n:(b + 1) * n].unsqueeze(2).broadcast_to([P, n, NR]),
                                         rule_iota[:, :].unsqueeze(1).broadcast_to([P, n, NR]), ALU.is_equal))
                for c in range(b * n, (b + 1) * n):
                    ins = dve.tensor_tensor(run3[:, c + 1, :], run3[:, c, :], has3[:, c, :], ALU.add)
                    ins.then_inc(counts_ready, 1) if c == NC - 1 else s.then(ins)
            dve.wait_ge(totals_done, 1)
            s.then(dve.tensor_copy(tot_i[:, :], bank[0][:, 0:NR]))
            s.then(dve.tensor_scalar(tot_j[:, :], tot_i[:, :], float(W - 1), None, ALU.add))
            s.then(dve.tensor_scalar(tot_i[:, :], tot_j[:, :], 5, None, ALU.logical_shift_right))
            s.then(dve.tensor_copy(slots_f[:, :], tot_i[:, :]))
            s.then(dve.tensor_tensor_scan(slots_end[:, :], slots_f[:, :], zeros[:, :], 0.0, ALU.add, ALU.add))
            s.then(dve.tensor_tensor(tot_j[:, :], slots_end[:, :], slots_f[:, :], ALU.subtract))
            s.then(dve.tensor_scalar(start_i[:, :], tot_j[:, :], 1, None, ALU.logical_shift_right))
            s.then(dve.tensor_scalar(start_a[:, :], start_i[:, :], 2.0 * W / P, None, ALU.mult))
            s.then(dve.tensor_scalar(start_i[:, :], tot_j[:, :], 1, None, ALU.bitwise_and))
            dve.tensor_scalar(start_b[:, :], start_i[:, :], float(W) / P, None, ALU.mult).then_inc(starts_ready, 1)
            s.then(dve.tensor_copy(col_i[0:NR, :], bank[1][0:NR, 0:1]))
            s.then(dve.tensor_scalar(col_j[0:NR, :], col_i[0:NR, :], float(W - 1), None, ALU.add))
            s.then(dve.tensor_scalar(col_i[0:NR, :], col_j[0:NR, :], 5, None, ALU.logical_shift_right))
            dve.tensor_copy(col_n[0:NR, :], col_i[0:NR, :]).then_inc(nslots_ready, 1)
            dve.wait_ge(ends_done, 1)
            dve.wait_ge(const_sort, CONST_SORT)
            s.then(dve.tensor_copy(col_end[0:NR, :], bank[1][0:NR, 4:5]))
            dve.tensor_scalar(past[0:NR, :], slot_iota[0:NR, :], col_end[0:NR, 0:1], None, ALU.is_ge
                              ).then_inc(past_ready, 1)
            dve.wait_ge(slots_done, 1)
            s.then(dve.tensor_scalar(slot_f[:, 0:SLOTS], bank[1][0:1, 0:SLOTS], float(NR - 1), float(D),
                                     ALU.min, ALU.mult))
            dve.tensor_copy(slot_at[:, 0:SLOTS], slot_f[:, 0:SLOTS]).then_inc(slots_ready, 1)
            for k in range(RANK_BANKS):
                c0, c1 = k * CPB, min(k * CPB + CPB, NC)
                dve.wait_ge(ranks_done, k + 1)
                s.then(dve.tensor_tensor(ranked[:, 0:(c1 - c0) * NR], bank[2 + k % 4][:, 0:(c1 - c0) * NR],
                                         has[:, c0 * NR:c1 * NR], ALU.mult))
                dve.tensor_reduce(pos_f[:, c0:c1], ranked[:, 0:(c1 - c0) * NR].rearrange("p (c r) -> p c r", r=NR),
                                  AX.X, ALU.add).then_inc(ranks_used, 1)
                dve.wait_ge(ranks_used, k + 1)
            dve.tensor_copy(pos_i[:, :], pos_f[:, :]).then_inc(pos_ready, 1)
            dve.wait_ge(pos_ready, 1)
            s.then(dve.tensor_scalar(pos_t[:, :], pos_i[:, :], P - 1, None, ALU.bitwise_and))
            dve.tensor_copy(pos_p[:, :], pos_t[:, :]).then_inc(pos_p_ready, 1)
            dve.wait_ge(pos_p_ready, 1)
            s.then(dve.tensor_scalar(pos_t[:, :], pos_i[:, :], 7, None, ALU.logical_shift_right))
            s.then(dve.tensor_copy(pos_g[:, :], pos_t[:, :]))
            for c in range(NC):
                if c >= NH:
                    dve.wait_ge(cols_used, c - NH + 1)
                if c % 2 == 0:
                    dve.tensor_scalar(is_part[:, c % NH, :], part_iota[:, :], pos_p[:, c:c + 1], None,
                                      ALU.is_equal).then_inc(cols_ready, 1)
                dve.tensor_scalar(is_tile[:, c % NH, :], tile_iota[:, :], pos_g[:, c:c + 1], id_f[:, c:c + 1],
                                  ALU.is_equal, ALU.mult).then_inc(cols_ready, 1)
            dve.wait_ge(cols_used, NC)
            s.then(dve.tensor_copy(spos_f[:, :], bank[6][:, 0:NG]))
            dve.tensor_copy(spos_i[:, :], spos_f[:, :]).then_inc(sorted_ready, 1)

            def angles(k, tiles):
                s = Steps(dve, angle_steps, ANGLE_STEPS * k)
                lo, hi = trig[:, bass.ds(k * GB, tiles), 0, :], trig[:, bass.ds(k * GB, tiles), 1, :]
                s.then(dve.tensor_tensor(lo, spos_f[:, bass.ds(k * GB, tiles)].unsqueeze(2).broadcast_to([P, tiles, D]),
                                         freq[:, :].unsqueeze(1).broadcast_to([P, tiles, D]), ALU.mult))
                s.then(dve.tensor_scalar(hi, lo, 1.0 / V, ROUND, ALU.mult, ALU.add))
                s.then(dve.tensor_scalar(hi, hi, ROUND, float(V), ALU.subtract, ALU.mult))
                assert s.n == ANGLE_STEPS
                dve.tensor_tensor(hi, lo, hi, ALU.subtract).then_inc(angles_ready, 1)

            def features(k, tiles):
                dve.wait_ge(rows_arrived, k + 1)
                dve.wait_ge(trig_ready, 3 * (k + 1))
                wait_past(dve, feats_turned, 2 * k)
                r = rows[:, bass.ds(k * GB * 2 * D, tiles * 2 * D)]
                dve.tensor_tensor(r, r, trig[:, bass.ds(k * GB, tiles), :, :].rearrange("p t a d -> p (t a d)"), ALU.mult
                                  ).then_inc(feats_steps, 1)
                dve.wait_ge(feats_steps, k + 1)
                r4 = r.rearrange("p (t a d) -> p t a d", a=2, d=D)
                dve.tensor_tensor(feats[:, 0:tiles, 0:D], r4[:, :, 0, :], r4[:, :, 1, :], ALU.add
                                  ).then_inc(feats_ready, 1)

            angles(0, GB)
            angles(1, GB)
            features(0, GB)
            with dve.Fori(1, NB_FULL - 1) as k:
                angles(k + 1, GB)
                features(k, GB)
            if NB_REST:
                angles(NB_FULL, NB_REST)
            features(NB_FULL - 1, GB)
            if NB_REST:
                features(NB_FULL, NB_REST)

            def rsqrt(i):
                s = Steps(dve, rs_steps, RS_STEPS * i)
                u, n, y, t = nt_u[:, :], nt_i[:, :], nt_y[:, :], nt_t[:, :]
                s.then(dve.tensor_scalar(n, u.bitcast(I32), 1, None, ALU.logical_shift_right))
                s.then(dve.tensor_scalar(y.bitcast(I32), n, -1.0, RSQRT_SEED, ALU.mult, ALU.add))
                for _ in range(NEWTON):
                    s.then(dve.tensor_tensor(t, y, y, ALU.mult))
                    s.then(dve.scalar_tensor_tensor(t, t, -0.5, u, ALU.mult, ALU.mult))
                    s.then(dve.scalar_tensor_tensor(y, t, 1.5, y, ALU.add, ALU.mult))
                assert s.n == RS_STEPS

            def center_ops(s, h, which, full, col):
                s.then(dve.tensor_reduce(lsum[:, which, :], h, AX.X, ALU.add))
                s.then(dve.scalar_tensor_tensor(full, lsum[:, which, :].unsqueeze(2).broadcast_to([P, TG, D]),
                                                -1.0 / D, h, ALU.mult, ALU.add))
                s.then(dve.tensor_tensor(lsq[:, which, :, :], full, full, ALU.mult))
                s.then(dve.tensor_reduce(lssq[:, which, :], lsq[:, which, :, :], AX.X, ALU.add))
                s.then(dve.tensor_scalar(nt_u[:, col:col + TG], lssq[:, which, :], 1.0 / D, EPS, ALU.mult, ALU.add))
                assert s.n == 5

            def normal_ops(s, full, halves16, col):
                s.n = 5
                s.then(dve.tensor_tensor(full, full, nt_y[:, col:col + TG].unsqueeze(2).broadcast_to([P, TG, D]),
                                         ALU.mult))
                s.then(dve.tensor_copy(halves16[:, :, 0, :], full))
                s.then(dve.tensor_tensor(halves16[:, :, 1, :], full, halves16[:, :, 0, :], ALU.subtract))
                assert s.n == LN_STEPS

            def h_of(g):
                return h_all[:, bass.ds(TG * g, TG), :]

            def ln1_center(g, par):
                dve.wait_ge(h_arrived, g + 1)
                wait_past(dve, g_done, SPG * (g - 1))
                center_ops(Steps(dve, ln1_steps, LN_STEPS * g), h_of(g), 0, x1[par], NT1)

            def ln1_normal(g, par):
                wait_past(dve, x1_turned, g)
                normal_ops(Steps(dve, ln1_steps, LN_STEPS * g), x1[par], x1_16, NT1)

            def sums(g, j):
                dve.wait_ge(sq_ready, halves * g + j + 1)
                dve.tensor_reduce(ssq[:, j // 2, j % 2 * H:(j % 2 + 1) * H],
                                  sq[:, j % 4, :].rearrange("p (h d) -> p h d", d=D), AX.X, ALU.add
                                  ).then_inc(sums_ready, 1)

            def kv_norms(g):
                s = Steps(dve, kvn_steps, KVN_STEPS * g)
                dve.wait_ge(sums_ready, halves * (g + 1))
                u = nt_u[:, 0:NT1].rearrange("p (t k) -> p t k", k=2 * H)
                s.then(dve.tensor_tensor(u, ssq[:, :, :], inv_c2[:, :].unsqueeze(1).broadcast_to([P, TG, 2 * H]), ALU.mult))
                s.then(dve.tensor_scalar(nt_u[:, 0:NT1], nt_u[:, 0:NT1], EPS, None, ALU.add))

            def scale_x(g, par):
                s = Steps(dve, kvn_steps, KVN_STEPS * g)
                s.n = 2
                y = nt_y[:, 0:NT1].rearrange("p (t a h) -> p t a h", a=2, h=H)
                s.then(dve.tensor_tensor(ksv[:, :, :], y[:, :, 0, :], y[:, :, 1, :], ALU.mult))
                assert s.n == KVN_STEPS
                wait_past(dve, g_done, SPG * g)
                for t in range(TG):
                    dve.tensor_tensor(xs[:, t, :, :], x1[par][:, t, :].unsqueeze(1).broadcast_to([P, H, D]),
                                      ksv[:, t, :].unsqueeze(2).broadcast_to([P, H, D]), ALU.mult).then_inc(xs_ready, 1)

            def split_m(g):
                s = Steps(dve, m_steps, M_STEPS * g)
                dve.wait_ge(m_done, g + 1)
                wait_past(dve, attn_done, g)
                s.then(dve.tensor_copy(m_f[:, :], bank[2][:, 0:SPG * D]))
                s.then(dve.tensor_copy(m_3[:, 0, :], m_f[:, :]))
                s.then(dve.tensor_tensor(m_r[:, :], m_f[:, :], m_3[:, 0, :], ALU.subtract))
                s.then(dve.tensor_copy(m_3[:, 1, :], m_r[:, :]))
                s.then(dve.tensor_tensor(m_3[:, 2, :], m_r[:, :], m_3[:, 1, :], ALU.subtract))
                assert s.n == M_STEPS

            def add_attention(g, par):
                s = Steps(dve, h2_steps, H2_STEPS * g)
                wait_past(dve, out_ready, g - 1)
                dve.wait_ge(attn_done, g + 1)
                s.then(dve.tensor_tensor(h2[par], bank[3][:, 0:TG * D].rearrange("p (t d) -> p t d", d=D), h_of(g),
                                         ALU.add))
                s.then(dve.tensor_tensor(h2[par], h2[par], bo_all[:, :].unsqueeze(1).broadcast_to([P, TG, D]),
                                         ALU.add))
                assert s.n == H2_STEPS

            def ln2_center(g, par):
                center_ops(Steps(dve, ln2_steps, LN_STEPS * g), h2[par], 1, x2[:, :, :], NT2)

            def ln2_normal(g):
                wait_past(dve, x2_turned, g)
                normal_ops(Steps(dve, ln2_steps, LN_STEPS * g), x2[:, :, :], x2_16, NT2)

            def choose(g):
                s = Steps(dve, mask_steps, MASK_STEPS * g)
                dve.wait_ge(gate_done, g + 1)
                wait_past(dve, mask_turned, g)
                s.then(dve.tensor_tensor(score[:, :, :], bank[7][:, 0:TG * E].rearrange("p (t e) -> p t e", e=E),
                                         bg_all[:, :].unsqueeze(1).broadcast_to([P, TG, E]), ALU.add), alone=dve_waited)
                for t in range(TG):
                    s.go(dve.max(top[:, t, :], score[:, t, :]))
                s.sync(alone=dve_waited)
                for t in range(TG):
                    s.go(dve.max_index(top_at[:, t, :], top[:, t, :], score[:, t, :]))
                s.sync()
                s.then(dve.tensor_copy(top_f[:, :, :], top_at[:, :, 0:2]))
                for n, one in enumerate((is0, is1)):
                    s.go(dve.tensor_tensor(one[:, :, :], expert_iota[:, :].unsqueeze(1).broadcast_to([P, TG, E]),
                                             top_f[:, :, n:n + 1].broadcast_to([P, TG, E]), ALU.is_equal))
                s.sync()
                s.then(dve.tensor_tensor(mask[:, :, 1, :], is0[:, :, :], is1[:, :, :], ALU.add))
                s.then(dve.tensor_scalar(mask[:, :, 0, :], mask[:, :, 1, :], -1.0, 1.0, ALU.mult, ALU.add))
                assert s.n == MASK_STEPS

            def finish(g, par):
                dve.wait_ge(back_done, g + 1)
                wait_past(dve, out_sent, 16 * g)
                dve.tensor_tensor(outb[:, :, :], bank[7][:, 0:TG * D].rearrange("p (t d) -> p t d", d=D), h2[par],
                                  ALU.add).then_inc(out_ready, 1)

            def step(i, par, att, mid, ffn, end, more, more2):
                if att:
                    for j in range(5):
                        sums(i, j)
                if end:
                    finish(i - 3, 1 - par)
                if att:
                    for j in range(5, halves):
                        sums(i, j)
                    kv_norms(i)
                if mid:
                    split_m(i - 1)
                    add_attention(i - 1, 1 - par)
                    ln2_center(i - 1, 1 - par)
                if att or mid:
                    rsqrt(i + 1)
                if att:
                    scale_x(i, par)
                if mid:
                    ln2_normal(i - 1)
                if more:
                    ln1_normal(i + 1, 1 - par)
                if more2:
                    ln1_center(i + 2, par)
                if mid:
                    choose(i - 1)

            dve.memset(nt_u[:, :], 1.0).then_inc(cleared, 1)
            dve.wait_ge(cleared, 11)
            ln1_center(0, 0)
            rsqrt(0)
            ln1_normal(0, 0)
            ln1_center(1, 1)
            for i in range(4):
                step(i, i % 2, *at_work(i))
            with dve.Fori(2, NGRP // 2 - 1) as k:
                step(2 * k, 0, *at_work(4))
                step(2 * k + 1, 1, *at_work(4))
            for i in range(NGRP - 2, NGRP + 3):
                step(i, i % 2, *at_work(i))


CONST_FIRST = 2 + 2 + 1
CONST_SORT = 4 + 4
CONSTS = 2 + 2 + 1 + 2
FOLD = 400
FOLD_LOOPS = 4
RANK_BANKS = 13


def kernel(**inputs):
    import numpy as np
    import concourse.bacc as bacc
    from concourse.bass_utils import run_bass_kernel_spmd

    laid = {"x": inputs["x"],
            "tables": np.concatenate([inputs["L0_tok_a_n"], inputs["L0_tok_b_n"]], axis=1)}
    for name in ("L0_tok_rule_transform", "L0_tok_token_rules", "L0_tok_proj_w", "L0_tok_proj_b", "L0_attn_w_qkv",
                 "L0_attn_w_out", "L0_attn_b_out", "L0_ffn_Wg", "L0_ffn_bg", "L0_ffn_W1", "L0_ffn_b1", "L0_ffn_W2",
                 "L0_ffn_b2"):
        laid[name] = inputs[name].T if name == "L0_ffn_b1" else inputs[name]
    nc = bacc.Bacc("TRN2", target_bir_lowering=False, num_devices=1)
    arrays, args = {}, []
    for name, a in laid.items():
        a = np.ascontiguousarray(a)
        arrays[f"in_{name}"] = a
        args.append(nc.dram_tensor(f"in_{name}", a.shape, mybir.dt.from_np(a.dtype), kind="ExternalInput").ap())
    shape = (*laid["x"].shape, laid["L0_tok_proj_w"].shape[0])
    out = nc.dram_tensor("out_0", shape, F32, kind="ExternalOutput").ap()
    program(nc, *args, out)
    r = run_bass_kernel_spmd(nc, [arrays], core_ids=[0])
    return r.results[0]["out_0"]
```

```python
from contextlib import ExitStack

import concourse.bass as bass
from concourse import mybir
from concourse.alu_op_type import AluOpType as ALU

F32, F16, BF16 = mybir.dt.float32, mybir.dt.float16, mybir.dt.bfloat16
I32, U32 = mybir.dt.int32, mybir.dt.uint32
ACT = mybir.ActivationFunctionType
AX = mybir.AxisListType

P = 128
EPS = 1e-5
PI = 3.141592653589793
ROUND = 12582912.0
RSQRT_SEED = 1597463007.0
NEWTON = 3
SPLIT = 16384.0
FAR, MASKED = -60000.0, 32768.0


class Steps:

    def __init__(self, eng, sem, base=0):
        self.eng, self.sem, self.base, self.n = eng, sem, base, 0

    def go(self, ins):
        ins.then_inc(self.sem, 1)
        self.n += 1

    def sync(self, alone=None):
        self.eng.wait_ge(self.sem, self.base + self.n)
        if alone is not None:
            self.eng.sem_inc(alone, 1)

    def then(self, ins, alone=None):
        self.go(ins)
        self.sync(alone)


def wait_past(eng, sem, value):
    if not isinstance(value, int) or value > 0:
        eng.wait_ge(sem, value)


def program(nc, x, tables, rule_transform, token_rules, proj_w, proj_b, w_qkv, w_out, b_out,
            wg, bg, w1, b1, w2, b2, out):
    B, S = x.shape
    V, NR = token_rules.shape[0], rule_transform.shape[0]
    D = proj_w.shape[0]
    H = w_qkv.shape[0] // (3 * D)
    E, _, HID = w1.shape
    T = B * S
    TPS = S // P
    NC = T // P
    W = 32
    SLOTS = T // W + NR
    SPT = P // W
    NG = SLOTS // SPT
    assert SLOTS % SPT == 0
    NPOS = SLOTS * W
    GB = 8
    NB_FULL, NB_REST = NG // GB, NG % GB
    NBATCH = NB_FULL + (NB_REST > 0)
    QB = GB * SPT
    SPG = 2
    TG = SPG * TPS
    NGRP = B // SPG
    GT = TG * P
    RB = 16
    CPB = 5

    with ExitStack() as ctx:
        def sb(name, shape, dt):
            return ctx.enter_context(nc.sbuf_tensor(name, shape, dt))

        def sem(name):
            return ctx.enter_context(nc.semaphore(name))

        bank = [ctx.enter_context(nc.psum_tensor(f"bank{i}", [P, 512], F32)) for i in range(8)]
        by_position = nc.dram_tensor("by_position", (NPOS, D), F32).ap()

        rule_iota = sb("rule_iota", [P, NR], BF16)
        part_iota = sb("part_iota", [P, P], BF16)
        tile_iota = sb("tile_iota", [P, NG], BF16)
        freq = sb("freq", [P, D], F32)
        slot_iota = sb("slot_iota", [P, SLOTS], F32)
        expert_iota = sb("expert_iota", [P, E], F32)
        before = sb("before", [P, P], BF16)
        upto = sb("upto", [P, P], BF16)
        ones_bf = sb("ones_bf", [P, P], BF16)
        ones_f = sb("ones_f", [P, P], F32)
        eye_f = sb("eye_f", [P, P], F32)
        eye_16 = sb("eye_16", [P, P], F16)
        eye_bf = sb("eye_bf", [P, P], BF16)
        center = sb("center", [D, D], F32)
        far = sb("far", [2 * E, E, HID], F16)
        half_pi = sb("half_pi", [P, 1], F32)
        zeros = sb("zeros", [P, NR], F32)

        ids = sb("ids", [P, NC], I32)
        rules_i = sb("rules_i", [P, NC], I32)
        rules_bf = sb("rules_bf", [P, NC], BF16)
        fold = sb("fold", [P, NR * D], F32)
        pwb = sb("pwb", [D, D + 1], F32)
        rows = sb("rows", [P, NG * 2 * D], F32)
        has = rows[:, 0:NC * NR // 2].bitcast(BF16)
        run = rows[:, NC * NR // 2:(2 * NC + 1) * NR // 2].bitcast(BF16)
        has3 = has.rearrange("p (c r) -> p c r", r=NR)
        run3 = run.rearrange("p (c r) -> p c r", r=NR)
        trig_flat = sb("trig", [P, NG * 2 * D], F32)
        trig = trig_flat[:, :].rearrange("p (t a d) -> p t a d", a=2, d=D)
        tot_i = sb("tot_i", [P, NR], I32)
        tot_j = sb("tot_j", [P, NR], I32)
        slots_f = sb("slots_f", [P, NR], F32)
        slots_end = sb("slots_end", [P, NR], F32)
        start_i = sb("start_i", [P, NR], I32)
        start_ab = sb("start_ab", [P, NR], BF16)
        ranked = sb("ranked", [P, CPB * NR], F32)
        pos_f = sb("pos_f", [P, NC], F32)
        pos_i = sb("pos_i", [P, NC], I32)
        pos_t = sb("pos_t", [P, NC], I32)
        pos_p = sb("pos_p", [P, NC], F32)
        pos_g = sb("pos_g", [P, NC], F32)
        id_f = sb("id_f", [P, NC], F32)
        NH = 8
        is_tile = sb("is_tile", [P, NH, NG], F32)
        spos_f = sb("spos_f", [P, NG], F32)
        spos_i = sb("spos_i", [P, NG], I32)
        col_i = sb("col_i", [P, 1], I32)
        col_j = sb("col_j", [P, 1], I32)
        col_n = sb("col_n", [P, 1], BF16)
        col_end = sb("col_end", [P, 1], F32)
        past = sb("past", [P, SLOTS], BF16)
        slot_f = sb("slot_f", [1, NBATCH * QB], F32)
        slot_at = sb("slot_at", [1, NBATCH * QB], I32)
        feats = sb("feats", [P, GB, D + 1], F32)
        feats_t0 = sb("feats_t0", [P, GB * P], F32)
        mapped_all = sb("mapped_all", [2 * W, QB * D], F32)
        mapped = [mapped_all[p * W:(p + 1) * W, :] for p in range(2)]
        h_all = sb("h_all", [P, NC, D], F32)

        wn = sb("wn", [D, 3 * H, D], F32)
        wc = sb("wc", [D, 2 * H, D], F32)
        wo = sb("wo", [D, H * D], F32)
        wo_t = sb("wo_t", [D, H, D], F32)
        wtmp = sb("wtmp", [P, 2 * H * D], F32)
        is_part = wtmp[:, 0:NH * P].rearrange("p (c q) -> p c q", q=P)
        feats_t = [feats_t0, wtmp]
        wkv_h = sb("wkv_h", [P, 2 * H * D], F16)
        wkv_l = sb("wkv_l", [P, 2 * H * D], F16)
        p_t = sb("p_t", [P, H // 2, P], F32)
        q_w = sb("q_w", [D, H, D], F32)
        fro = sb("fro", [D, 2 * H + E], F32)
        fro_all = sb("fro_all", [P, 2 * H + E], F32)
        fro_root = sb("fro_root", [P, 2 * H + E], F32)
        scale_up = sb("scale_up", [P, 2 * H + E], F32)
        scale_dn = sb("scale_dn", [P, 2 * H + E], F32)
        inv_c2 = sb("inv_c2", [P, 2 * H], F32)
        w1f = sb("w1f", [P, E, HID], F32)
        w1_h = sb("w1_h", [P, E, HID], F16)
        w1_m = sb("w1_m", [D + 2 * E, E, HID], F16)
        b1sq = sb("b1sq", [HID, E], F32)
        b1t = sb("b1t", [HID, E], F32)
        w2f = sb("w2f", [HID, E, D], F32)
        wgf = sb("wgf", [P, E], F32)
        wg_r = sb("wg_r", [P, E], F32)
        wg_3 = sb("wg_3", [P, 3, E], BF16)
        back_w = sb("back_w", [D + 2 * E, D], F32)
        bg_all = sb("bg_all", [P, E], F32)
        bo_all = sb("bo_all", [P, D], F32)

        taken = [0]

        def later(name, shape, dt):
            n = 1
            for k in shape[1:]:
                n *= k
            words = n * (2 if dt in (F16, BF16) else 4) // 4
            assert words * 4 == n * (2 if dt in (F16, BF16) else 4)
            if taken[0] < NG * 2 * D < taken[0] + words:
                taken[0] = NG * 2 * D
            o = taken[0] % (NG * 2 * D)
            v = (trig_flat if taken[0] < NG * 2 * D else rows)[0:shape[0], o:o + words]
            taken[0] += words
            assert taken[0] <= 2 * NG * 2 * D, name
            v = v if dt == F32 else v.bitcast(dt)
            if len(shape) == 2:
                return v
            names = ["a", "b", "c"][:len(shape) - 1]
            return v.rearrange(f"p ({' '.join(names)}) -> p {' '.join(names)}",
                               **dict(zip(names[1:], shape[2:])))

 
        NT = TG * (2 * H + 2)
        NT1, NT2 = TG * 2 * H, TG * (2 * H + 1)
        lsq = later("lsq", [P, 2, TG, D], F32)
        lsum = later("lsum", [P, 2, TG], F32)
        lssq = later("lssq", [P, 2, TG], F32)
        nt_u = later("nt_u", [P, NT], F32)
        nt_i = later("nt_i", [P, NT], I32)
        nt_y = later("nt_y", [P, NT], F32)
        nt_t = later("nt_t", [P, NT], F32)
        x1 = [later(f"x1_{p}", [P, TG, D], F32) for p in range(2)]
        x1_16 = later("x1_16", [P, TG, 2, D], F16)
        x1_t = [later(f"x1_t{p}", [P, GT], F16) for p in range(2)]
        sq = later("sq", [P, 4, 512], F32)
        ssq = later("ssq", [P, TG, 2 * H], F32)
        ksv = later("ksv", [P, TG, H], F32)
        xs = later("xs", [P, TG, H, D], F32)
        g_sb = later("g_sb", [D, SPG, H * D], F32)
        t_sb = later("t_sb", [P, H // 2, SPG, D], F32)
        m_r = later("m_r", [P, SPG * D], F32)
        m_3 = later("m_3", [P, 3, SPG * D], BF16)
        h2 = [later(f"h2_{p}", [P, TG, D], F32) for p in range(2)]
        x1_c = [later(f"x1_c{p}", [P, TG, D], F32) for p in range(2)]
        x2 = later("x2", [P, TG, D], F32)
        x2_16 = later("x2_16", [P, TG, 2, D], F16)
        x2_t = [later(f"x2_t{p}", [P, GT], F16) for p in range(2)]
        score = later("score", [P, TG, E], F32)
        top = later("top", [P, TG, 8], F32)
        top_at = later("top_at", [P, TG, 8], U32)
        top_f = later("top_f", [P, TG, 2], F32)
        is0 = later("is0", [P, TG, E], F32)
        is1 = later("is1", [P, TG, E], F32)
        mask = later("mask", [P, TG, 2, E], BF16)
        x2m_t = [later(f"x2m_t{p}", [D + 2 * E, GT], F16) for p in range(2)]
        hid = later("hid", [P, 2, GT], F32)
        y_t = [later(f"y_t{p}", [D + 2 * E, GT], F32) for p in range(2)]
        outb = later("outb", [P, TG, D], F32)
        taken[0] = max(taken[0], NG * 2 * D)
        hb_all = later("hb_all", [P, NC, D], F32)

        ids_in, const_first, const_sort, const_made = (
            sem(n) for n in ("ids_in", "const_first", "const_sort", "const_made"))
        pos_p_ready, parts_ready = sem("pos_p_ready"), sem("parts_ready")
        rules_in = [sem(f"rules_in{i}") for i in range(RB)]
        fold_in, qkv_in, wo_in, w1_in, w2_in, small_in = (
            sem(n) for n in ("fold_in", "qkv_in", "wo_in", "w1_in", "w2_in", "small_in"))
        cleared = sem("cleared")
        folded_done, folded = sem("folded_done"), sem("folded")
        wc_done, wc_ready = sem("wc_done"), sem("wc_ready")
        fro_ready, fro_done, fro_copied, root_ready = (
            sem(n) for n in ("fro_ready", "fro_done", "fro_copied", "root_ready"))
        wt_done, wt_used = sem("wt_done"), sem("wt_used")
        wot_done, wot_ready = sem("wot_done"), sem("wot_ready")
        pq_done, pq_ready = sem("pq_done"), sem("pq_ready")
        weights_ready = sem("weights_ready")
        prep_steps, sort_steps = sem("prep_steps"), sem("sort_steps")
        counts_ready, totals_done, starts_ready = (
            sem(n) for n in ("counts_ready", "totals_done", "starts_ready"))
        ranks_done, ranks_used = sem("ranks_done"), sem("ranks_used")
        cols_ready, cols_used, sorted_done = sem("cols_ready"), sem("cols_used"), sem("sorted_done")
        nslots_ready, ends_done, past_ready, slots_done, slots_ready = (
            sem(n) for n in ("nslots_ready", "ends_done", "past_ready", "slots_done", "slots_ready"))
        sorted_ready, pos_ready = sem("sorted_ready"), sem("pos_ready")
        angle_steps, angles_ready, trig_ready = sem("angle_steps"), sem("angles_ready"), sem("trig_ready")
        rows_in = [sem(f"rows_in{i}") for i in range(4)]
        rows_arrived = sem("rows_arrived")
        feats_steps, feats_ready, feats_turned, feats_t_ready = (
            sem(n) for n in ("feats_steps", "feats_ready", "feats_turned", "feats_t_ready"))
        slots_mapped, mapped_ready, mapped_out = (
            sem("slots_mapped"), sem("mapped_ready"), [sem(f"mapped_out{p}") for p in range(2)])
        h_in = [sem(f"h_in{i}") for i in range(NGRP)]
        h_arrived = sem("h_arrived")

        ln1_steps, kvn_steps, xs_second, ln2_steps, mask_steps, m_steps, h2_ready = (
            sem(n) for n in ("ln1_steps", "kvn_steps", "xs_second", "ln2_steps", "mask_steps", "m_steps", "h2_ready"))
        y_mask_ready = sem("y_mask_ready")
        pool_steps, c1_steps = sem("pool_steps"), sem("c1_steps")
        far_ready, x2m_t_ready = sem("far_ready"), sem("x2m_t_ready")
        hb_ready, h2_kept = sem("hb_ready"), sem("h2_kept")
        x1_turned, x1_t_ready, rs_steps = sem("x1_turned"), sem("x1_t_ready"), sem("rs_steps")
        kv_done, sq_ready, sums_ready = sem("kv_done"), sem("sq_ready"), sem("sums_ready")
        xs_ready, g_done, g_ready = sem("xs_ready"), sem("g_done"), sem("g_ready")
        t_done, t_ready, m_done, attn_done = sem("t_done"), sem("t_ready"), sem("m_done"), sem("attn_done")
        x2_turned, x2_t_ready = sem("x2_turned"), sem("x2_t_ready")
        gate_done, mask_turned, mask_t_ready = sem("gate_done"), sem("mask_turned"), sem("mask_t_ready")
        w1_done, gelu_ready, w2_done = sem("w1_done"), sem("gelu_ready"), sem("w2_done")
        y_t_ready, back_done, out_ready, out_sent = (
            sem(n) for n in ("y_t_ready", "back_done", "out_ready", "out_sent"))

        pe_waited, dve_waited, act_waited, pool_waited = (
            sem(n) for n in ("pe_waited", "dve_waited", "act_waited", "pool_waited"))

        CENTER_STEPS = 6
        NORMAL_STEPS = 3
        LN_STEPS = CENTER_STEPS + NORMAL_STEPS
        HALVES = [D >> k for k in range(1, D.bit_length())]
        POOL_STEPS = 2 * len(HALVES) + 3
        POOL_JOINS = 2
        KVN_STEPS = 2 + 1
        ANGLE_STEPS = 3
        RS_STEPS = 2 + 3 * NEWTON
        MASK_STEPS = 3 + 2 * TG + 3
        M_STEPS = 4
        halves = 2 * TG

        HT = GB // 2
        NHALF = -(-NG // HT)

        def tiles_of(k):
            return GB if k < NB_FULL else NB_REST

        MAPPED = sum(-(-tiles_of(k) * SPT // 8) for k in range(NBATCH))
        FIRST_REST = 2 * (NB_FULL // 2 - 1)

        def cols_by(c):
            return c + 1 + c // 2 + 1

        def at_work(i):
            return tuple(0 <= g < NGRP for g in (i, i - 1, i - 2, i - 3, i + 1, i + 2, i + 3))

        block = ctx.enter_context(nc.Block())

        def h_of(g):
            return h_all[:, bass.ds(TG * g, TG), :]

        def center_ops(s, h, which, full, col):
            e = s.eng
            s.then(e.tensor_reduce(lsum[:, which, :], h, AX.X, ALU.add))
            s.then(e.tensor_scalar(lsum[:, which, :], lsum[:, which, :], 1.0 / D, None, ALU.mult))
            s.then(e.tensor_tensor(full, h, lsum[:, which, :].unsqueeze(2).broadcast_to([P, TG, D]), ALU.subtract))
            s.then(e.tensor_tensor(lsq[:, which, :, :], full, full, ALU.mult))
            s.then(e.tensor_reduce(lssq[:, which, :], lsq[:, which, :, :], AX.X, ALU.add))
            s.then(e.tensor_scalar(nt_u[:, col:col + TG], lssq[:, which, :], 1.0 / D, EPS, ALU.mult, ALU.add))
            assert s.n == CENTER_STEPS

        def scale_tiles(e, done, par, tiles):
            for t in tiles:
                e.tensor_tensor(xs[:, t, :, :], x1[par][:, t, :].unsqueeze(1).broadcast_to([P, H, D]),
                                ksv[:, t, :].unsqueeze(2).broadcast_to([P, H, D]), ALU.mult).then_inc(done, 1)

        @block.sync
        def _(sp):
            sp.dma_start(ids[:, :].rearrange("p (b s) -> p b s", s=TPS),
                         x.rearrange("b (p s) -> p b s", s=TPS)).then_inc(ids_in, 16)
            sp.dma_start(fold[0:D, :].rearrange("d (r e) -> d r e", e=D),
                         rule_transform.rearrange("r d e -> d r e")).then_inc(fold_in, 16)
            sp.dma_start(pwb[:, 0:D], proj_w).then_inc(fold_in, 16)
            sp.dma_start(pwb[:, D:D + 1], proj_b.rearrange("(d o) -> d o", o=1)).then_inc(fold_in, 16)
            sp.dma_start(wn[:, :, :], w_qkv.rearrange("(g e) d -> e g d", e=D)).then_inc(qkv_in, 16)
            sp.dma_start(wo[:, :], w_out).then_inc(wo_in, 16)
            for half in range(2):
                sp.dma_start(w1f[half * D:(half + 1) * D, :, :],
                             w1.rearrange("e d h -> d e h")).then_inc(w1_in, 16)
            sp.dma_start(w2f[:, :, :], w2.rearrange("e h d -> h e d")).then_inc(w2_in, 16)
            for half in range(2):
                sp.dma_start(wgf[half * D:(half + 1) * D, :], wg).then_inc(small_in, 16)
            sp.wait_ge(cleared, 3)
            sp.dma_start(back_w[D + E:D + 2 * E, :], b2).then_inc(small_in, 16)
            sp.dma_start(b1t[:, :], b1).then_inc(small_in, 16)
            sp.dma_start(bg_all[:, :], bg.partition_broadcast(P)).then_inc(small_in, 16)
            sp.dma_start(bo_all[:, :], b_out.partition_broadcast(P)).then_inc(small_in, 16)
            posv = by_position[0:NB_FULL * QB * W, :].rearrange("(k q p) d -> k p q d", p=W, q=QB)

            def store(k, par):
                sp.wait_ge(mapped_ready, 4 * (k + 1))
                sp.dma_start(posv[k], mapped[par].rearrange("p (q d) -> p q d", d=D)
                             ).then_inc(mapped_out[par], 16)

            with sp.Fori(0, NB_FULL // 2) as k:
                store(2 * k, 0)
                store(2 * k + 1, 1)
            if NB_FULL % 2:
                store(NB_FULL - 1, 0)
            if NB_REST:
                sp.wait_ge(mapped_ready, MAPPED)
                sp.dma_start(by_position[NB_FULL * QB * W:NPOS, :].rearrange("(q p) d -> p q d", p=W),
                             mapped[NB_FULL % 2][:, 0:NB_REST * SPT * D].rearrange("p (q d) -> p q d", d=D)
                             ).then_inc(mapped_out[NB_FULL % 2], 16)
            outv = out.rearrange("(g q) (p s) d -> g p q (s d)", q=SPG, s=TPS)
            with sp.Fori(0, NGRP) as g:
                sp.wait_ge(out_ready, g + 1)
                sp.dma_start(outv[g], outb[:, :, :].rearrange("p (q s) d -> p q (s d)", s=TPS)
                             ).then_inc(out_sent, 16)
            sp.wait_ge(out_sent, 16 * NGRP)

        @block.gpsimd
        def _(pool):
            def triangle(c, t, base):
                c.then(pool.memset(t[:, :], 0.0))
                c.then(pool.affine_select(t[:, :], t[:, :], pattern=[[-1, P]], compare_op=ALU.is_ge,
                                          fill=1.0, base=base, channel_multiplier=1))

            def identity(c, t, off, diagonal):
                n = t.shape[1]
                c.then(pool.memset(t[:, :], off))
                c.then(pool.affine_select(t[:, :], t[:, :], pattern=[[-1, n]], compare_op=ALU.not_equal,
                                          fill=diagonal, base=0, channel_multiplier=1))

            def count(c, t, first=0):
                c.then(pool.iota(t[:, :], pattern=[[1, t.shape[1]]], base=first, channel_multiplier=0,
                                 allow_small_or_imprecise_dtypes=True))

            c = Steps(pool, const_first)
            identity(c, center, -1.0 / D, 1.0 - 1.0 / D)
            identity(c, eye_f, 0.0, 1.0)
            count(c, rule_iota)
            assert c.n == CONST_FIRST
            pool.wait_ge(ids_in, 16)
            for t in range(NC):
                pool.indirect_dma_start(rules_i[:, t:t + 1], None, token_rules.rearrange("(v o) -> v o", o=1),
                                        bass.IndirectOffsetOnAxis(ap=ids[:, t:t + 1], axis=0)
                                        ).then_inc(rules_in[t * RB // NC], 16)
            c = Steps(pool, const_sort)
            triangle(c, before, 0)
            triangle(c, upto, -1)
            count(c, slot_iota)
            count(c, part_iota)
            count(c, tile_iota)
            count(c, freq, 1)
            assert c.n == CONST_SORT
            c = Steps(pool, const_made)
            identity(c, eye_16, 0.0, 1.0)
            identity(c, eye_bf, 0.0, 1.0)
            count(c, expert_iota)
            c.then(pool.memset(far[:, :, :], 0.0))
            c.then(pool.affine_select(far[:, :, :], far[:, :, :], pattern=[[-1, E], [0, HID]],
                                      compare_op=ALU.not_equal, fill=FAR, base=0, channel_multiplier=1))
            assert c.n == CONSTS
            pool.wait_ge(pos_p_ready, 1)
            for c in range(1, NC, 2):
                if c >= NH:
                    pool.wait_ge(cols_used, c - NH + 1)
                pool.tensor_scalar(is_part[:, c % NH, :], part_iota[:, :], pos_p[:, c:c + 1], None,
                                   ALU.is_equal).then_inc(parts_ready, 1)
            pool.wait_ge(sorted_ready, 1)
            pool.wait_ge(ranks_used, RANK_BANKS)
            def rows_passed_on(u):
                pool.wait_ge(rows_in[u % 4], 16 * (u // 4 * HT + min(NG - u * HT, HT)))
                pool.sem_inc(rows_arrived, 1)

            for u in range(NHALF):
                for t in range(u * HT, min(u * HT + HT, NG)):
                    pool.indirect_dma_start(rows[:, t * 2 * D:(t + 1) * 2 * D], None, tables,
                                            bass.IndirectOffsetOnAxis(ap=spos_i[:, t:t + 1], axis=0)
                                            ).then_inc(rows_in[u % 4], 16)
                if u:
                    rows_passed_on(u - 1)
            rows_passed_on(NHALF - 1)
            pool.wait_ge(mapped_out[0], 16 * ((NBATCH + 1) // 2))
            pool.wait_ge(mapped_out[1], 16 * (NBATCH // 2))
            pool.wait_ge(pos_ready, 1)
            pool.wait_ge(small_in, 16 * 6)
            pool.wait_ge(feats_ready, NHALF)

            def arrived(g):
                pool.wait_ge(h_in[g], 16 * TG)
                pool.sem_inc(h_arrived, 1)
                pool.tensor_tensor(hb_all[:, g * TG:(g + 1) * TG, :], h_all[:, g * TG:(g + 1) * TG, :],
                                   bo_all[:, :].unsqueeze(1).broadcast_to([P, TG, D]), ALU.add).then_inc(hb_ready, 1)

            for g in range(NGRP):
                for t in range(g * TG, (g + 1) * TG):
                    pool.indirect_dma_start(h_all[:, t, :], None, by_position,
                                            bass.IndirectOffsetOnAxis(ap=pos_i[:, t:t + 1], axis=0)
                                            ).then_inc(h_in[g], 16)
                if g:
                    arrived(g - 1)
            arrived(NGRP - 1)

            def keep_h2(g, par):
                pool.wait_ge(h2_ready, g + 1)
                wait_past(pool, out_sent, 16 * g)
                pool.sem_inc(pool_waited, 1)
                pool.tensor_copy(outb[:, :, :], h2[par]).then_inc(h2_kept, 1)

            def scale_second(g, par):
                pool.wait_ge(kvn_steps, KVN_STEPS * (g + 1))
                wait_past(pool, g_done, SPG * g)
                scale_tiles(pool, xs_second, par, range(TPS, TG))

            def ln1_center(g, par):
                s = Steps(pool, pool_steps, POOL_STEPS * (g - POOL_JOINS - 3))
                pool.wait_ge(ln1_steps, NORMAL_STEPS * (g - 1))
                pool.sem_inc(pool_waited, 1)
                h, part = h_of(g), lsq[:, 0, :, :]

                def halve(of, n):
                    s.then(pool.tensor_tensor(part[:, :, 0:n], of[:, :, 0:n], of[:, :, n:2 * n], ALU.add),
                           alone=pool_waited)

                halve(h, D // 2)
                for n in HALVES[1:]:
                    halve(part, n)
                s.then(pool.tensor_scalar(lsum[:, 0, :], part[:, :, 0:1].rearrange("p t o -> p (t o)"), 1.0 / D, None,
                                          ALU.mult), alone=pool_waited)
                s.then(pool.tensor_tensor(x1_c[par], h, lsum[:, 0, :].unsqueeze(2).broadcast_to([P, TG, D]),
                                          ALU.subtract), alone=pool_waited)
                s.then(pool.tensor_tensor(part, x1_c[par], x1_c[par], ALU.mult), alone=pool_waited)
                for n in HALVES:
                    halve(part, n)
                assert s.n == POOL_STEPS
                pool.wait_ge(rs_steps, RS_STEPS * g)
                pool.sem_inc(pool_waited, 1)
                pool.tensor_scalar(nt_u[:, NT1:NT1 + TG], part[:, :, 0:1].rearrange("p t o -> p (t o)"), 1.0 / D, EPS,
                                   ALU.mult, ALU.add).then_inc(c1_steps, CENTER_STEPS)

            def step(i, par, att, mid, ffn, end, more, more2, more3):
                if end:
                    keep_h2(i - 3, 1 - par)
                if att:
                    scale_second(i, par)
                if more3:
                    ln1_center(i + 3, 1 - par)

            for i in range(POOL_JOINS, 4):
                step(i, i % 2, *at_work(i))
            with pool.Fori(2, NGRP // 2 - 2) as k:
                step(2 * k, 0, *at_work(4))
                step(2 * k + 1, 1, *at_work(4))
            for i in range(NGRP - 4, NGRP + 3):
                step(i, i % 2, *at_work(i))

        @block.scalar
        def _(act):
            act.wait_ge(wc_done, 1)
            act.activation(wc[:, 0:H, :], bank[4][0:D, :].rearrange("p (h d) -> p h d", d=D), ACT.Copy).then_inc(wc_ready, 1)
            act.activation(wc[:, H:2 * H, :], bank[5][0:D, :].rearrange("p (h d) -> p h d", d=D), ACT.Copy).then_inc(wc_ready, 1)
            act.wait_ge(wot_done, 1)
            act.activation(wo_t[:, :, :], bank[7][0:D, :].rearrange("p (h d) -> p h d", d=D), ACT.Copy).then_inc(wot_ready, 1)
            act.wait_ge(fro_copied, 1)
            act.activation(fro_root[:, :], fro_all[:, :], ACT.Sqrt).then_inc(root_ready, 1)
            act.wait_ge(pq_done, 1)
            for i in range(2):
                act.activation(p_t[:, :, i * D:(i + 1) * D],
                               bank[2][:, 0:H // 2 * D].rearrange("p (h d) -> p h d", d=D), ACT.Copy).then_inc(pq_ready, 1)
            act.activation(q_w[:, :, :], bank[3][0:D, :].rearrange("p (h d) -> p h d", d=D), ACT.Copy,
                           scale=1.0 / S).then_inc(pq_ready, 1)
            with act.Fori(0, FOLD_LOOPS) as k:
                for j in range(4):
                    act.wait_ge(folded_done, 4 * k + j + 1)
                    act.activation(fold[0:D + 1, bass.ds(FOLD * (4 * k + j), FOLD)], bank[j][0:D + 1, 0:FOLD],
                                   ACT.Copy).then_inc(folded, 1)

            def trigs(k, tiles):
                lo, hi = trig[:, bass.ds(k * GB, tiles), 0, :], trig[:, bass.ds(k * GB, tiles), 1, :]
                act.wait_ge(angles_ready, k + 1)
                act.sem_inc(act_waited, 1)
                act.activation(lo, hi, ACT.Abs).then_inc(trig_ready, 1)
                act.wait_ge(trig_ready, 3 * k + 1)
                act.sem_inc(act_waited, 1)
                act.activation(hi, hi, ACT.Sin, scale=2 * PI / V).then_inc(trig_ready, 1)
                act.activation(lo, lo, ACT.Sin, scale=-2 * PI / V, bias=half_pi[:, 0:1]).then_inc(trig_ready, 1)

            def turned_evac(k, par, half, tiles):
                n = min(max(tiles - half * HT, 0), HT)
                if n:
                    wait_past(act, slots_mapped, 4 * (k - 1))
                    act.wait_ge(feats_turned, 2 * k + half + 1)
                    act.activation(feats_t[par][0:D + 1, half * HT * P:(half * HT + n) * P],
                                   bank[4 + half][0:D + 1, 0:n * P], ACT.Copy).then_inc(feats_t_ready, 1)

            def mapped_evac(half, par, tiles, js):
                k = 2 * half + par
                if 0 in js:
                    wait_past(act, mapped_out[par], 16 * half)
                for j in js:
                    n = min(max(tiles * SPT - 8 * j, 0), 8)
                    if n:
                        act.wait_ge(slots_mapped, 4 * k + j + 1)
                        act.activation(mapped[par][:, 8 * j * D:(8 * j + n) * D],
                                       bank[j][0:W, 0:n * D], ACT.Copy).then_inc(mapped_ready, 1)

            def batch(half, par, tiles, tiles1, tiles2):
                k = 2 * half + par
                mapped_evac(half, par, tiles, (0,))
                turned_evac(k, par, 1, tiles)
                if tiles2:
                    trigs(k + 2, tiles2)
                mapped_evac(half, par, tiles, (1,))
                turned_evac(k + 1, 1 - par, 0, tiles1)
                mapped_evac(half, par, tiles, (2, 3))

            trigs(0, GB)
            trigs(1, GB)
            turned_evac(0, 0, 0, GB)
            for k in range(2):
                batch(0, k, GB, GB, GB)
            with act.Fori(1, FIRST_REST // 2) as k:
                batch(k, 0, GB, GB, GB)
                batch(k, 1, GB, GB, GB)
            for k in range(FIRST_REST, NBATCH):
                batch(k // 2, k % 2, tiles_of(k), tiles_of(k + 1) if k + 1 < NBATCH else 0,
                      tiles_of(k + 2) if k + 2 < NBATCH else 0)

            def x1_evac(g, par):
                act.wait_ge(x1_turned, g + 1)
                wait_past(act, attn_done, g - 1)
                act.activation(x1_t[par][:, :], bank[1][:, :].bitcast(F16)[:, 0:GT], ACT.Copy).then_inc(x1_t_ready, 1)

            def square(g, j):
                act.wait_ge(kv_done, halves * g + j + 1)
                wait_past(act, sums_ready, halves * g + j - 3)
                act.activation(sq[:, j % 4, :], bank[j % 2][:, :], ACT.Square).then_inc(sq_ready, 1)

            def g_evac(g, s):
                act.wait_ge(g_done, SPG * g + s + 1)
                act.activation(g_sb[:, s, :], bank[2 + s][0:D, :], ACT.Copy).then_inc(g_ready, 1)

            def t_evac(g, s):
                wait_past(act, m_done, g)
                act.wait_ge(t_done, SPG * g + s + 1)
                act.activation(t_sb[:, :, s, :], bank[2 + s][:, 0:H // 2 * D].rearrange("p (h d) -> p h d", d=D),
                               ACT.Copy).then_inc(t_ready, 1)

            act.wait_ge(const_made, CONSTS)
            act.activation(w1_m[D:D + 2 * E, :, :], far[:, :, :], ACT.Copy).then_inc(far_ready, 1)

            def x2_evac(g, par):
                act.wait_ge(x2_turned, g + 1)
                wait_past(act, w1_done, E * (g - 1))
                act.activation(x2_t[par][:, :], bank[7][:, :].bitcast(F16)[:, 0:GT], ACT.Copy).then_inc(x2_t_ready, 1)

            def x2m_copy(g, par):
                act.wait_ge(x2_t_ready, g + 1)
                act.activation(x2m_t[par][0:D, :], x2_t[par][0:D, :], ACT.Copy).then_inc(x2m_t_ready, 1)

            def mask_evac(g, par):
                act.wait_ge(mask_turned, g + 1)
                wait_past(act, back_done, g - 1)
                masks = bank[7][0:2 * E, :].bitcast(BF16)[:, 0:GT]
                act.activation(x2m_t[par][D:D + 2 * E, :], masks, ACT.Copy).then_inc(mask_t_ready, 1)

            def y_mask_copy(g, par):
                act.wait_ge(mask_t_ready, g + 1)
                act.activation(y_t[par][D:D + 2 * E, :], x2m_t[par][D:D + 2 * E, :], ACT.Copy).then_inc(y_mask_ready, 1)

            def gelu(g, e):
                act.wait_ge(w1_done, E * g + e + 1)
                wait_past(act, w2_done, E * g + e - 1)
                act.activation(hid[:, e % 2, :], bank[4 + e % 2][:, :], ACT.Gelu, bias=b1t[:, e:e + 1],
                               scale=scale_dn[:, 2 * H + e:2 * H + e + 1]).then_inc(gelu_ready, 1)

            def y_evac(g, par):
                act.wait_ge(w2_done, E * g + E)
                wait_past(act, back_done, g - 1)
                act.activation(y_t[par][0:D, :], bank[6][0:D, :], ACT.Copy).then_inc(y_t_ready, 1)

            def step(i, par, att, mid, ffn, end, more, *_):
                def squares(*js):
                    if att:
                        for j in js:
                            square(i, j)

                def gelus(*es):
                    if ffn:
                        for e in es:
                            gelu(i - 2, e)

                squares(0, 1)
                if mid:
                    t_evac(i - 1, 0)
                squares(2, 3)
                if mid:
                    t_evac(i - 1, 1)
                squares(4)
                if end:
                    gelu(i - 3, 6)
                squares(5, 6, 7)
                if ffn:
                    x2m_copy(i - 2, par)
                if ffn:
                    mask_evac(i - 2, par)
                if end:
                    gelu(i - 3, 7)
                if ffn:
                    y_mask_copy(i - 2, par)
                gelus(0)
                if end:
                    y_evac(i - 3, 1 - par)
                gelus(1)
                if more:
                    x1_evac(i + 1, 1 - par)
                gelus(2, 3, 4, 5)
                if att:
                    g_evac(i, 0)
                if mid:
                    x2_evac(i - 1, 1 - par)
                if att:
                    g_evac(i, 1)

            x1_evac(0, 0)
            for i in range(4):
                step(i, i % 2, *at_work(i))
            with act.Fori(2, NGRP // 2 - 2) as k:
                step(2 * k, 0, *at_work(4))
                step(2 * k + 1, 1, *at_work(4))
            for i in range(NGRP - 4, NGRP + 3):
                step(i, i % 2, *at_work(i))

        @block.tensor
        def _(pe):
            pe.wait_ge(const_first, CONST_FIRST)
            pe.wait_ge(cleared, 4)
            pe.wait_ge(qkv_in, 16)
            for i in range(2):
                ins = pe.matmul(bank[4 + i][0:D, :], center[:, :],
                                wn[:, H * (1 + i):H * (2 + i), :].rearrange("p h d -> p (h d)"), start=True, stop=True)
            ins.then_inc(wc_done, 1)
            for half in range(2):
                for g in range(2 * H):
                    ins = pe.matmul(bank[g // H][half * D:(half + 1) * D, g % H * D:(g % H + 1) * D],
                                    wn[:, H + g, :], center[:, :], start=True, stop=True)
            ins.then_inc(wt_done, 1)
            pe.wait_ge(wo_in, 16)
            for h in range(H):
                ins = pe.transpose(bank[7][0:D, h * D:(h + 1) * D], wo[:, h * D:(h + 1) * D], eye_f[0:D, 0:D])
            ins.then_inc(wot_done, 1)
            pe.wait_ge(fro_ready, 1)
            pe.matmul(bank[6][:, 0:2 * H], ones_f[0:D, :], fro[:, 0:2 * H], start=True, stop=True)
            pe.matmul(bank[6][:, 2 * H:2 * H + E], ones_f[0:D, :], fro[:, 2 * H:2 * H + E], start=True, stop=False)
            pe.matmul(bank[6][:, 2 * H:2 * H + E], ones_f[:, :], b1sq[:, :], start=False, stop=True).then_inc(fro_done, 1)
            pe.wait_ge(wc_ready, 2)
            pe.wait_ge(wot_ready, 1)
            for h in range(H):
                ins = pe.matmul(bank[2][h % 2 * D:(h % 2 + 1) * D, h // 2 * D:(h // 2 + 1) * D],
                                wc[:, h, :], wn[:, h, :], start=True, stop=True)
            for h in range(H):
                ins = pe.matmul(bank[3][0:D, h * D:(h + 1) * D], wc[:, H + h, :], wo_t[:, h, :],
                                start=True, stop=True)
            ins.then_inc(pq_done, 1)
            pe.wait_ge(fold_in, 48)
            pe.wait_ge(wt_used, 1)
            pe.wait_ge(pq_ready, 3)
            for j in range(4):
                pe.matmul(bank[j][0:D + 1, 0:FOLD], pwb[:, :], fold[0:D, FOLD * j:FOLD * (j + 1)],
                          start=True, stop=True).then_inc(folded_done, 1)
            with pe.Fori(1, FOLD_LOOPS) as k:
                for j in range(4):
                    pe.wait_ge(folded, 4 * k + j - 3)
                    pe.matmul(bank[j][0:D + 1, 0:FOLD], pwb[:, :], fold[0:D, bass.ds(FOLD * (4 * k + j), FOLD)],
                              start=True, stop=True).then_inc(folded_done, 1)

            pe.wait_ge(counts_ready, 1)
            pe.wait_ge(folded, 4 * FOLD_LOOPS)
            pe.matmul(bank[0][:, 0:NR], ones_bf[:, :], run3[:, NC, :], start=True, stop=True)
            pe.matmul(bank[1][0:NR, 0:1], run3[:, NC, :], ones_bf[:, 0:1], start=True, stop=True).then_inc(totals_done, 1)
            pe.wait_ge(const_sort, CONST_SORT)
            pe.wait_ge(nslots_ready, 1)
            pe.matmul(bank[1][0:NR, 4:5], upto[0:NR, 0:NR], col_n[0:NR, :], start=True, stop=True).then_inc(ends_done, 1)
            pe.wait_ge(past_ready, 1)
            pe.matmul(bank[1][0:1, 0:SLOTS], ones_bf[0:NR, 0:1], past[0:NR, :], start=True, stop=True).then_inc(slots_done, 1)
            pe.wait_ge(starts_ready, 1)
            for k in range(RANK_BANKS):
                if k >= 4:
                    pe.wait_ge(ranks_used, k - 3)
                for c in range(k * CPB, min(k * CPB + CPB, NC)):
                    o = bank[2 + k % 4][:, (c % CPB) * NR:(c % CPB + 1) * NR]
                    pe.matmul(o, before[:, :], has3[:, c, :], start=True, stop=False)
                    pe.matmul(o, ones_bf[:, :], run3[:, c, :], start=False, stop=False)
                    ins = pe.matmul(o, ones_bf[:, :], start_ab[:, :], start=False, stop=True)
                ins.then_inc(ranks_done, 1)
            for c in range(NC):
                pe.wait_ge(cols_ready, cols_by(c))
                if c % 2:
                    pe.wait_ge(parts_ready, c // 2 + 1)
                pe.matmul(bank[6][:, 0:NG], is_part[:, c % NH, :], is_tile[:, c % NH, :],
                          start=(c == 0), stop=(c == NC - 1)).then_inc(cols_used, 1)

            def turn(k, half, tiles):
                n = min(max(tiles - half * HT, 0), HT)
                if n:
                    pe.wait_ge(feats_ready, 2 * k + half + 1)
                    wait_past(pe, feats_t_ready, 2 * k + half - 1)
                    for t in range(n):
                        ins = pe.transpose(bank[4 + half][0:D + 1, t * P:(t + 1) * P], feats[:, half * HT + t, :],
                                           eye_f[:, :])
                    ins.then_inc(feats_turned, 1)

            def map_slots(k, par, tiles, js):
                for j in js:
                    n = min(max(tiles * SPT - 8 * j, 0), 8)
                    if n == 0:
                        continue
                    if j in (0, 2):
                        pe.wait_ge(feats_t_ready, 2 * k + j // 2 + 1)
                    wait_past(pe, mapped_ready, 4 * k + j - 3)
                    _, at = nc.values_load_multi_w_load_instructions(
                        slot_at[0:1, bass.ds(QB * k + 8 * j, 8)], engines=[mybir.EngineType.PE],
                        min_val=0, max_val=(NR - 1) * D,
                        skip_runtime_bounds_check_because="the least of it and the last rule's is stored")
                    for q in range(n):
                        s = 8 * j + q
                        ins = pe.matmul(bank[j][0:W, q * D:(q + 1) * D],
                                        feats_t[par][:, s * W:(s + 1) * W], fold[:, bass.ds(at[q], D)],
                                        start=True, stop=True)
                    ins.then_inc(slots_mapped, 1)

            def batch(k, par, tiles, tiles1):
                map_slots(k, par, tiles, (0,))
                turn(k, 1, tiles)
                map_slots(k, par, tiles, (1,))
                turn(k + 1, 0, tiles1)
                map_slots(k, par, tiles, (2, 3))

            pe.wait_ge(slots_ready, 1)
            pe.wait_ge(sorted_ready, 1)
            pe.wait_ge(ranks_used, RANK_BANKS)
            pe.wait_ge(cleared, 11)
            turn(0, 0, GB)
            for k in range(2):
                batch(k, k, GB, GB)
            with pe.Fori(1, FIRST_REST // 2) as k:
                batch(2 * k, 0, GB, GB)
                batch(2 * k + 1, 1, GB, GB)
            for k in range(FIRST_REST, NBATCH):
                batch(k, k % 2, tiles_of(k), tiles_of(k + 1) if k + 1 < NBATCH else 0)

            def x1_turn(g):
                pe.wait_ge(ln1_steps, NORMAL_STEPS * (g + 1))
                wait_past(pe, sq_ready, halves * g)
                for t in range(TG):
                    ins = pe.transpose(bank[1][:, :].bitcast(F16)[:, t * P:(t + 1) * P],
                                       x1_16[:, t, :, :].rearrange("p a d -> p (a d)"), eye_16[:, :])
                ins.then_inc(x1_turned, 1)

            def kv(g, par, j):
                if j == 0:
                    pe.wait_ge(x1_t_ready, g + 1)
                wait_past(pe, sq_ready, halves * g + j - 1)
                cols = slice(j % 2 * H * D, (j % 2 + 1) * H * D)
                lhs = x1_t[par][:, j // 2 * P:(j // 2 + 1) * P]
                pe.matmul(bank[j % 2][:, :], lhs, wkv_h[:, cols], start=True, stop=False)
                pe.matmul(bank[j % 2][:, :], lhs, wkv_l[:, cols], start=False, stop=True).then_inc(kv_done, 1)

            def gram(g, par, in_front, which):
                wait_past(pe, m_steps, M_STEPS * g)
                wait_past(pe, h2_ready, g)
                for s in (which,):
                    for t in range(TPS):
                        if in_front:
                            pe.wait_ge(xs_ready, TG * g + s * TPS + t + 1)
                        elif s == 0:
                            pe.wait_ge(xs_ready, TPS * (g + POOL_JOINS) + t + 1)
                        else:
                            pe.wait_ge(xs_second, TPS * (g - POOL_JOINS) + t + 1)
                        ins = pe.matmul(bank[2 + s][0:D, :], x1[par][:, s * TPS + t, :],
                                        xs[:, s * TPS + t, :, :].rearrange("p h d -> p (h d)"),
                                        start=(t == 0), stop=(t == TPS - 1))
                    ins.then_inc(g_done, 1)

            def times_q(g, s):
                for h in range(H):
                    ins = pe.matmul(bank[2 + s][h % 2 * D:(h % 2 + 1) * D, h // 2 * D:(h // 2 + 1) * D],
                                    g_sb[:, s, h * D:(h + 1) * D], q_w[:, h, :], start=True, stop=True)
                ins.then_inc(t_done, 1)

            def p_times(g):
                pe.wait_ge(t_ready, SPG * (g + 1))
                for h in range(H // 2):
                    ins = pe.matmul(bank[2][:, 0:SPG * D], p_t[:, h, :], t_sb[:, h, :, :].rearrange("p s d -> p (s d)"),
                                    start=(h == 0), stop=(h == H // 2 - 1))
                ins.then_inc(m_done, 1)

            def attend(g, par):
                pe.wait_ge(m_steps, M_STEPS * (g + 1))
                for t in range(TG):
                    for part in range(3):
                        ins = pe.matmul(bank[3][:, t * D:(t + 1) * D], x1_t[par][:, t * P:(t + 1) * P],
                                        m_3[:, part, t // TPS * D:(t // TPS + 1) * D], start=(part == 0), stop=(part == 2))
                ins.then_inc(attn_done, 1)

            def x2_turn(g):
                pe.wait_ge(ln2_steps, LN_STEPS * (g + 1))
                wait_past(pe, out_ready, g - 1)
                for t in range(TG):
                    ins = pe.transpose(bank[7][:, :].bitcast(F16)[:, t * P:(t + 1) * P],
                                       x2_16[:, t, :, :].rearrange("p a d -> p (a d)"), eye_16[:, :])
                ins.then_inc(x2_turned, 1)

            def gate(g, par):
                pe.wait_ge(x2_t_ready, g + 1)
                for t in range(TG):
                    for part in range(3):
                        ins = pe.matmul(bank[7][:, t * E:(t + 1) * E], x2_t[par][:, t * P:(t + 1) * P], wg_3[:, part, :],
                                        start=(part == 0), stop=(part == 2))
                ins.then_inc(gate_done, 1)

            def mask_turn(g):
                pe.wait_ge(mask_steps, MASK_STEPS * (g + 1))
                for t in range(TG):
                    ins = pe.transpose(bank[7][0:2 * E, :].bitcast(BF16)[:, t * P:(t + 1) * P],
                                       mask[:, t, :, :].rearrange("p a e -> p (a e)"), eye_bf[:, :])
                ins.then_inc(mask_turned, 1)

            def up(g, par, e):
                if e == 0:
                    pe.wait_ge(x2m_t_ready, g + 1)
                    pe.wait_ge(mask_t_ready, g + 1)
                wait_past(pe, gelu_ready, E * g + e - 1)
                o = bank[4 + e % 2][:, :]
                pe.matmul(o, w1_h[:, e, :], x2_t[par][:, :], start=True, stop=False)
                pe.matmul(o, w1_m[:, e, :], x2m_t[par][:, :], start=False, stop=True).then_inc(w1_done, 1)

            def down(g, e):
                pe.wait_ge(gelu_ready, E * g + e + 1)
                if e == 0:
                    wait_past(pe, y_t_ready, g)
                pe.matmul(bank[6][0:D, :], w2f[:, e, :], hid[:, e % 2, :], start=(e == 0), stop=(e == E - 1)
                          ).then_inc(w2_done, 1)

            def back(g, par, masks):
                pe.wait_ge(y_t_ready, g + 1)
                pe.wait_ge(y_mask_ready, g + 1)
                pe.wait_ge(mask_t_ready, masks)
                wait_past(pe, out_ready, g)
                for t in range(TG):
                    o = bank[7][:, t * D:(t + 1) * D]
                    ins = pe.matmul(o, y_t[par][:, t * P:(t + 1) * P], back_w[:, :], start=True, stop=True)
                ins.then_inc(back_done, 1)

            def step(i, par, att, mid, ffn, end, more, *_, in_front=False):
                def kvs(*js):
                    if att:
                        for j in js:
                            kv(i, par, j)

                def expert(e):
                    if ffn:
                        up(i - 2, par, e)
                        down(i - 2, e - 1)

                kvs(0)
                if mid:
                    pe.wait_ge(g_ready, SPG * (i - 1) + 1)
                    if not att:
                        pe.sem_inc(pe_waited, 1)
                kvs(1)
                if mid:
                    times_q(i - 1, 0)
                kvs(2)
                if mid:
                    pe.wait_ge(g_ready, SPG * (i - 1) + 2)
                    if not att:
                        pe.sem_inc(pe_waited, 1)
                kvs(3)
                if mid:
                    times_q(i - 1, 1)
                kvs(4, 5)
                if mid:
                    p_times(i - 1)
                kvs(6, 7)
                if ffn:
                    mask_turn(i - 2)
                if end:
                    down(i - 3, 5)
                    up(i - 3, 1 - par, 7)
                    down(i - 3, 6)
                if ffn:
                    up(i - 2, par, 0)
                if end:
                    down(i - 3, 7)
                if mid:
                    attend(i - 1, 1 - par)
                if ffn:
                    up(i - 2, par, 1)
                    down(i - 2, 0)
                if end:
                    back(i - 3, 1 - par, i - 1 if mid or ffn else NGRP)
                if more:
                    x1_turn(i + 1)
                for e in range(2, 6):
                    expert(e)
                if att:
                    gram(i, par, in_front, 0)
                if ffn:
                    up(i - 2, par, 6)
                if mid:
                    x2_turn(i - 1)
                if att:
                    gram(i, par, in_front, 1)
                if mid:
                    gate(i - 1, 1 - par)

            pe.wait_ge(const_made, CONSTS)
            pe.wait_ge(far_ready, 1)
            pe.wait_ge(weights_ready, 1)
            pe.wait_ge(mapped_ready, MAPPED)
            x1_turn(0)
            for i in range(4):
                step(i, i % 2, *at_work(i), in_front=i < POOL_JOINS)
            with pe.Fori(2, NGRP // 2 - 2) as k:
                step(2 * k, 0, *at_work(4))
                step(2 * k + 1, 1, *at_work(4))
            for i in range(NGRP - 4, NGRP + 3):
                step(i, i % 2, *at_work(i))

        @block.vector
        def _(dve):
            dve.memset(ones_bf[:, :], 1.0).then_inc(cleared, 1)
            dve.memset(ones_f[:, :], 1.0).then_inc(cleared, 1)
            dve.memset(back_w[:, :], 0.0).then_inc(cleared, 1)
            dve.memset(run3[:, 0, :], 0.0).then_inc(cleared, 1)
            dve.memset(zeros[:, :], 0.0).then_inc(cleared, 1)
            dve.memset(half_pi[:, :], PI / 2).then_inc(cleared, 1)
            dve.memset(feats[:, :, D:D + 1], 1.0).then_inc(cleared, 1)
            dve.memset(feats_t0[D:P, :], 0.0).then_inc(cleared, 1)
            dve.memset(fold[D:P, :], 0.0).then_inc(cleared, 1)
            dve.memset(slot_at[:, :], 0).then_inc(cleared, 1)
            dve.wait_ge(cleared, 10)

            s = Steps(dve, prep_steps)
            dve.wait_ge(wc_ready, 2)
            t3 = wtmp[0:D, :].rearrange("p (g d) -> p g d", d=D)
            s.then(dve.tensor_tensor(t3, wc[:, :, :], wc[:, :, :], ALU.mult))
            s.then(dve.tensor_reduce(fro[:, 0:2 * H], t3, AX.X, ALU.add))
            dve.wait_ge(w1_in, 32)
            t3 = wtmp[0:D, :].rearrange("p (e h) -> p e h", h=HID)
            s.then(dve.tensor_tensor(t3, w1f[0:D, :, :], w1f[0:D, :, :], ALU.mult))
            dve.wait_ge(small_in, 16 * 6)
            s.then(dve.tensor_tensor(b1sq[:, :], b1t[:, :], b1t[:, :], ALU.mult))
            dve.tensor_reduce(fro[:, 2 * H:2 * H + E], t3, AX.X, ALU.add).then_inc(fro_ready, 1)
            dve.wait_ge(fro_done, 1)
            s.then(dve.tensor_scalar(fro_all[:, 0:2 * H], bank[6][:, 0:2 * H], 1e-20, None, ALU.add))
            dve.tensor_scalar(fro_all[:, 2 * H:2 * H + E], bank[6][:, 2 * H:2 * H + E], 1.0, None, ALU.add
                              ).then_inc(fro_copied, 1)
            dve.wait_ge(root_ready, 1)
            s.then(dve.reciprocal(scale_up[:, :], fro_root[:, :]))
            s.then(dve.tensor_scalar(scale_up[:, :], scale_up[:, :], SPLIT, None, ALU.mult))
            s.then(dve.reciprocal(scale_dn[:, :], scale_up[:, :]))
            s.then(dve.tensor_scalar(inv_c2[:, :], scale_dn[:, 0:2 * H], 1.0 / D, None, ALU.mult))
            s.then(dve.tensor_tensor(inv_c2[:, :], inv_c2[:, :], scale_dn[:, 0:2 * H], ALU.mult))
            dve.wait_ge(wt_done, 1)
            for i in range(2):
                ins = dve.tensor_tensor(wtmp[:, i * H * D:(i + 1) * H * D].rearrange("p (h d) -> p h d", d=D),
                                        bank[i][:, :].rearrange("p (h d) -> p h d", d=D),
                                        scale_up[:, i * H:(i + 1) * H].unsqueeze(2).broadcast_to([P, H, D]), ALU.mult)
                ins.then_inc(wt_used, 1) if i else s.then(ins)
            dve.wait_ge(wt_used, 1)
            s.then(dve.tensor_copy(wkv_h[:, :], wtmp[:, :]))
            s.then(dve.tensor_tensor(wkv_l[:, :], wtmp[:, :], wkv_h[:, :], ALU.subtract))
            s.then(dve.tensor_tensor(w1f[:, :, :], w1f[:, :, :],
                                     scale_up[:, 2 * H:2 * H + E].unsqueeze(2).broadcast_to([P, E, HID]), ALU.mult))
            s.then(dve.tensor_copy(w1_h[:, :, :], w1f[:, :, :]))
            s.then(dve.tensor_tensor(w1_m[0:D, :, :], w1f[0:D, :, :], w1_h[0:D, :, :], ALU.subtract))
            s.then(dve.tensor_copy(wg_3[:, 0, :], wgf[:, :]))
            s.then(dve.tensor_tensor(wg_r[:, :], wgf[:, :], wg_3[:, 0, :], ALU.subtract))
            s.then(dve.tensor_copy(wg_3[:, 1, :], wg_r[:, :]))
            s.then(dve.tensor_tensor(wg_3[:, 2, :], wg_r[:, :], wg_3[:, 1, :], ALU.subtract))
            dve.wait_ge(const_first, CONST_FIRST)
            s.then(dve.tensor_copy(back_w[0:D, :], eye_f[0:D, 0:D]))
            dve.wait_ge(w2_in, 16)
            dve.wait_ge(pq_ready, 3)
            dve.sem_inc(weights_ready, 1)

            s = Steps(dve, sort_steps)
            dve.wait_ge(const_first, CONST_FIRST)
            s.then(dve.tensor_copy(id_f[:, :], ids[:, :]))
            n = NC // RB
            for b in range(RB):
                dve.wait_ge(rules_in[b], 16 * n)
                s.then(dve.tensor_copy(rules_bf[:, b * n:(b + 1) * n], rules_i[:, b * n:(b + 1) * n]))
                s.then(dve.tensor_tensor(has3[:, b * n:(b + 1) * n, :],
                                         rules_bf[:, b * n:(b + 1) * n].unsqueeze(2).broadcast_to([P, n, NR]),
                                         rule_iota[:, :].unsqueeze(1).broadcast_to([P, n, NR]), ALU.is_equal))
                for c in range(b * n, (b + 1) * n):
                    ins = dve.tensor_tensor(run3[:, c + 1, :], run3[:, c, :], has3[:, c, :], ALU.add)
                    ins.then_inc(counts_ready, 1) if c == NC - 1 else s.then(ins)
            dve.wait_ge(totals_done, 1)
            s.then(dve.tensor_copy(tot_i[:, :], bank[0][:, 0:NR]))
            s.then(dve.tensor_scalar(tot_j[:, :], tot_i[:, :], float(W - 1), None, ALU.add))
            s.then(dve.tensor_scalar(tot_i[:, :], tot_j[:, :], 5, None, ALU.logical_shift_right))
            s.then(dve.tensor_copy(slots_f[:, :], tot_i[:, :]))
            s.then(dve.tensor_tensor_scan(slots_end[:, :], slots_f[:, :], zeros[:, :], 0.0, ALU.add, ALU.add))
            s.then(dve.tensor_tensor(tot_j[:, :], slots_end[:, :], slots_f[:, :], ALU.subtract))
            s.then(dve.tensor_scalar(start_i[:, :], tot_j[:, :], 1, None, ALU.logical_shift_right))
            s.then(dve.tensor_scalar(start_ab[0:P // 2, :], start_i[0:P // 2, :], 4.0 * W / P, None, ALU.mult))
            s.then(dve.tensor_scalar(start_i[:, :], tot_j[:, :], 1, None, ALU.bitwise_and))
            dve.tensor_scalar(start_ab[P // 2:P, :], start_i[P // 2:P, :], 2.0 * W / P, None, ALU.mult
                              ).then_inc(starts_ready, 1)
            s.then(dve.tensor_copy(col_i[0:NR, :], bank[1][0:NR, 0:1]))
            s.then(dve.tensor_scalar(col_j[0:NR, :], col_i[0:NR, :], float(W - 1), None, ALU.add))
            s.then(dve.tensor_scalar(col_i[0:NR, :], col_j[0:NR, :], 5, None, ALU.logical_shift_right))
            dve.tensor_copy(col_n[0:NR, :], col_i[0:NR, :]).then_inc(nslots_ready, 1)
            dve.wait_ge(ends_done, 1)
            dve.wait_ge(const_sort, CONST_SORT)
            s.then(dve.tensor_copy(col_end[0:NR, :], bank[1][0:NR, 4:5]))
            dve.tensor_scalar(past[0:NR, :], slot_iota[0:NR, :], col_end[0:NR, 0:1], None, ALU.is_ge
                              ).then_inc(past_ready, 1)
            dve.wait_ge(slots_done, 1)
            s.then(dve.tensor_scalar(slot_f[:, 0:SLOTS], bank[1][0:1, 0:SLOTS], float(NR - 1), float(D),
                                     ALU.min, ALU.mult))
            dve.tensor_copy(slot_at[:, 0:SLOTS], slot_f[:, 0:SLOTS]).then_inc(slots_ready, 1)
            for k in range(RANK_BANKS):
                c0, c1 = k * CPB, min(k * CPB + CPB, NC)
                dve.wait_ge(ranks_done, k + 1)
                for c in range(c0, c1):
                    picked = slice((c - c0) * NR, (c - c0 + 1) * NR)
                    ins = dve.scalar_tensor_tensor(ranked[:, picked], bank[2 + k % 4][:, picked], 1.0, has3[:, c, :],
                                                   ALU.mult, ALU.mult, accum_out=pos_f[:, c:c + 1])
                ins.then_inc(ranks_used, 1)
                dve.wait_ge(ranks_used, k + 1)
            dve.tensor_copy(pos_i[:, :], pos_f[:, :]).then_inc(pos_ready, 1)
            dve.wait_ge(pos_ready, 1)
            s.then(dve.tensor_scalar(pos_t[:, :], pos_i[:, :], P - 1, None, ALU.bitwise_and))
            dve.tensor_copy(pos_p[:, :], pos_t[:, :]).then_inc(pos_p_ready, 1)
            dve.wait_ge(pos_p_ready, 1)
            s.then(dve.tensor_scalar(pos_t[:, :], pos_i[:, :], 7, None, ALU.logical_shift_right))
            s.then(dve.tensor_copy(pos_g[:, :], pos_t[:, :]))
            for c in range(NC):
                if c >= NH:
                    dve.wait_ge(cols_used, c - NH + 1)
                if c % 2 == 0:
                    dve.tensor_scalar(is_part[:, c % NH, :], part_iota[:, :], pos_p[:, c:c + 1], None,
                                      ALU.is_equal).then_inc(cols_ready, 1)
                dve.tensor_scalar(is_tile[:, c % NH, :], tile_iota[:, :], pos_g[:, c:c + 1], id_f[:, c:c + 1],
                                  ALU.is_equal, ALU.mult).then_inc(cols_ready, 1)
            dve.wait_ge(cols_used, NC)
            s.then(dve.tensor_copy(spos_f[:, :], bank[6][:, 0:NG]))
            dve.tensor_copy(spos_i[:, :], spos_f[:, :]).then_inc(sorted_ready, 1)

            def angles(k, tiles):
                s = Steps(dve, angle_steps, ANGLE_STEPS * k)
                lo, hi = trig[:, bass.ds(k * GB, tiles), 0, :], trig[:, bass.ds(k * GB, tiles), 1, :]
                s.then(dve.tensor_tensor(lo, spos_f[:, bass.ds(k * GB, tiles)].unsqueeze(2).broadcast_to([P, tiles, D]),
                                         freq[:, :].unsqueeze(1).broadcast_to([P, tiles, D]), ALU.mult))
                s.then(dve.tensor_scalar(hi, lo, 1.0 / V, ROUND, ALU.mult, ALU.add))
                s.then(dve.tensor_scalar(hi, hi, ROUND, float(V), ALU.subtract, ALU.mult))
                assert s.n == ANGLE_STEPS
                dve.tensor_tensor(hi, lo, hi, ALU.subtract).then_inc(angles_ready, 1)

            def features(k, tiles):
                dve.wait_ge(trig_ready, 3 * (k + 1))
                for half in range(2):
                    n = min(max(tiles - half * HT, 0), HT)
                    if n == 0:
                        continue
                    first = k * GB + half * HT
                    dve.wait_ge(rows_arrived, 2 * k + half + 1)
                    wait_past(dve, feats_turned, 2 * k + half - 1)
                    r = rows[:, bass.ds(first * 2 * D, n * 2 * D)]
                    dve.tensor_tensor(r, r, trig[:, bass.ds(first, n), :, :].rearrange("p t a d -> p (t a d)"),
                                      ALU.mult).then_inc(feats_steps, 1)
                    dve.wait_ge(feats_steps, 2 * k + half + 1)
                    r4 = r.rearrange("p (t a d) -> p t a d", a=2, d=D)
                    dve.tensor_tensor(feats[:, half * HT:half * HT + n, 0:D], r4[:, :, 0, :], r4[:, :, 1, :], ALU.add
                                      ).then_inc(feats_ready, 1)

            dve.memset(feats_t[1][D:P, :], 0.0).then_inc(cleared, 1)
            angles(0, GB)
            angles(1, GB)
            angles(2, GB)
            features(0, GB)
            with dve.Fori(1, NB_FULL - 2) as k:
                angles(k + 2, GB)
                features(k, GB)
            for k in range(NB_FULL - 2, NBATCH):
                if k + 2 < NBATCH:
                    angles(k + 2, tiles_of(k + 2))
                features(k, tiles_of(k))

            def rsqrt(i):
                s = Steps(dve, rs_steps, RS_STEPS * i)
                u, n, y, t = nt_u[:, :], nt_i[:, :], nt_y[:, :], nt_t[:, :]
                s.then(dve.tensor_scalar(n, u.bitcast(I32), 1, None, ALU.logical_shift_right))
                s.then(dve.tensor_scalar(y.bitcast(I32), n, -1.0, RSQRT_SEED, ALU.mult, ALU.add))
                for _ in range(NEWTON):
                    s.then(dve.tensor_tensor(t, y, y, ALU.mult))
                    s.then(dve.scalar_tensor_tensor(t, t, -0.5, u, ALU.mult, ALU.mult))
                    s.then(dve.scalar_tensor_tensor(y, t, 1.5, y, ALU.add, ALU.mult))
                assert s.n == RS_STEPS

            def normal_ops(s, centred, full, halves16, col):
                s.then(dve.tensor_tensor(full, centred, nt_y[:, col:col + TG].unsqueeze(2).broadcast_to([P, TG, D]),
                                         ALU.mult))
                s.then(dve.tensor_copy(halves16[:, :, 0, :], full))
                s.then(dve.tensor_tensor(halves16[:, :, 1, :], full, halves16[:, :, 0, :], ALU.subtract))

            def ln1_center(g, par):
                dve.wait_ge(h_arrived, g + 1)
                center_ops(Steps(dve, c1_steps, CENTER_STEPS * g), h_of(g), 0, x1_c[par], NT1)

            def ln1_normal(g, par):
                wait_past(dve, g_done, SPG * (g - 1))
                wait_past(dve, x1_turned, g)
                normal_ops(Steps(dve, ln1_steps, NORMAL_STEPS * g), x1_c[par], x1[par], x1_16, NT1)

            def sums(g, j):
                dve.wait_ge(sq_ready, halves * g + j + 1)
                dve.tensor_reduce(ssq[:, j // 2, j % 2 * H:(j % 2 + 1) * H],
                                  sq[:, j % 4, :].rearrange("p (h d) -> p h d", d=D), AX.X, ALU.add
                                  ).then_inc(sums_ready, 1)

            def kv_norms(g):
                s = Steps(dve, kvn_steps, KVN_STEPS * g)
                dve.wait_ge(sums_ready, halves * (g + 1))
                u = nt_u[:, 0:NT1].rearrange("p (t k) -> p t k", k=2 * H)
                s.then(dve.tensor_tensor(u, ssq[:, :, :], inv_c2[:, :].unsqueeze(1).broadcast_to([P, TG, 2 * H]), ALU.mult))
                s.then(dve.tensor_scalar(nt_u[:, 0:NT1], nt_u[:, 0:NT1], EPS, None, ALU.add))

            def scale_x(g, par, all_tiles):
                s = Steps(dve, kvn_steps, KVN_STEPS * g)
                s.n = 2
                y = nt_y[:, 0:NT1].rearrange("p (t a h) -> p t a h", a=2, h=H)
                wait_past(dve, g_done, SPG * g)
                s.then(dve.tensor_tensor(ksv[:, :, :], y[:, :, 0, :], y[:, :, 1, :], ALU.mult))
                assert s.n == KVN_STEPS
                scale_tiles(dve, xs_ready, par, range(TG) if all_tiles else range(TPS))

            def split_m(g):
                s = Steps(dve, m_steps, M_STEPS * g)
                dve.wait_ge(m_done, g + 1)
                wait_past(dve, attn_done, g)
                m = bank[2][:, 0:SPG * D]
                s.then(dve.tensor_copy(m_3[:, 0, :], m))
                s.then(dve.tensor_tensor(m_r[:, :], m, m_3[:, 0, :], ALU.subtract))
                s.then(dve.tensor_copy(m_3[:, 1, :], m_r[:, :]))
                s.then(dve.tensor_tensor(m_3[:, 2, :], m_r[:, :], m_3[:, 1, :], ALU.subtract))
                assert s.n == M_STEPS

            def add_attention(g, par):
                dve.wait_ge(hb_ready, g + 1)
                wait_past(dve, h2_kept, g - 1)
                dve.wait_ge(attn_done, g + 1)
                dve.tensor_tensor(h2[par], bank[3][:, 0:TG * D].rearrange("p (t d) -> p t d", d=D),
                                  hb_all[:, bass.ds(TG * g, TG), :], ALU.add).then_inc(h2_ready, 1)

            def ln2_center(g, par):
                dve.wait_ge(h2_ready, g + 1)
                center_ops(Steps(dve, ln2_steps, LN_STEPS * g), h2[par], 1, x2[:, :, :], NT2)

            def ln2_normal(g):
                wait_past(dve, x2_turned, g)
                normal_ops(Steps(dve, ln2_steps, LN_STEPS * g + CENTER_STEPS), x2[:, :, :], x2[:, :, :], x2_16, NT2)

            def choose(g):
                s = Steps(dve, mask_steps, MASK_STEPS * g)
                dve.wait_ge(gate_done, g + 1)
                wait_past(dve, mask_turned, g)
                s.then(dve.tensor_tensor(score[:, :, :], bank[7][:, 0:TG * E].rearrange("p (t e) -> p t e", e=E),
                                         bg_all[:, :].unsqueeze(1).broadcast_to([P, TG, E]), ALU.add), alone=dve_waited)
                for t in range(TG):
                    s.go(dve.max(top[:, t, :], score[:, t, :]))
                s.sync(alone=dve_waited)
                for t in range(TG):
                    s.go(dve.max_index(top_at[:, t, :], top[:, t, :], score[:, t, :]))
                s.sync()
                s.then(dve.tensor_copy(top_f[:, :, :], top_at[:, :, 0:2]))
                for n, one in enumerate((is0, is1)):
                    s.go(dve.tensor_tensor(one[:, :, :], expert_iota[:, :].unsqueeze(1).broadcast_to([P, TG, E]),
                                             top_f[:, :, n:n + 1].broadcast_to([P, TG, E]), ALU.is_equal))
                s.sync()
                s.then(dve.tensor_tensor(mask[:, :, 1, :], is0[:, :, :], is1[:, :, :], ALU.add))
                s.then(dve.tensor_scalar(mask[:, :, 0, :], mask[:, :, 1, :], -MASKED, MASKED, ALU.mult, ALU.add))
                assert s.n == MASK_STEPS

            def finish(g):
                dve.wait_ge(back_done, g + 1)
                dve.wait_ge(h2_kept, g + 1)
                dve.tensor_tensor(outb[:, :, :], bank[7][:, 0:TG * D].rearrange("p (t d) -> p t d", d=D),
                                  outb[:, :, :], ALU.add).then_inc(out_ready, 1)

            def step(i, par, att, mid, ffn, end, more, more2, more3, in_front=False):
                if att:
                    for j in range(halves):
                        sums(i, j)
                if mid:
                    split_m(i - 1)
                if att:
                    kv_norms(i)
                if more:
                    ln1_normal(i + 1, 1 - par)
                if mid:
                    add_attention(i - 1, 1 - par)
                    ln2_center(i - 1, 1 - par)
                if more2:
                    dve.wait_ge(c1_steps, CENTER_STEPS * (i + 3))
                if att or mid:
                    rsqrt(i + 2)
                if att:
                    scale_x(i, par, in_front)
                if end:
                    finish(i - 3)
                if mid:
                    ln2_normal(i - 1)
                if more3 and in_front:
                    ln1_center(i + 3, 1 - par)
                if mid:
                    choose(i - 1)

            dve.memset(nt_u[:, :], 1.0).then_inc(cleared, 1)
            dve.wait_ge(cleared, 12)
            ln1_center(0, 0)
            rsqrt(0)
            ln1_normal(0, 0)
            ln1_center(1, 1)
            rsqrt(1)
            ln1_center(2, 0)
            for i in range(4):
                step(i, i % 2, *at_work(i), in_front=i < POOL_JOINS)
            with dve.Fori(2, NGRP // 2 - 2) as k:
                step(2 * k, 0, *at_work(4))
                step(2 * k + 1, 1, *at_work(4))
            for i in range(NGRP - 4, NGRP + 3):
                step(i, i % 2, *at_work(i))


CONST_FIRST = 2 + 2 + 1
CONST_SORT = 4 + 4
CONSTS = 2 + 2 + 1 + 2
FOLD = 400
FOLD_LOOPS = 4
RANK_BANKS = 13


def kernel(**inputs):
    import numpy as np
    import concourse.bacc as bacc
    from concourse.bass_utils import run_bass_kernel_spmd

    laid = {"x": inputs["x"],
            "tables": np.concatenate([inputs["L0_tok_a_n"], inputs["L0_tok_b_n"]], axis=1)}
    for name in ("L0_tok_rule_transform", "L0_tok_token_rules", "L0_tok_proj_w", "L0_tok_proj_b", "L0_attn_w_qkv",
                 "L0_attn_w_out", "L0_attn_b_out", "L0_ffn_Wg", "L0_ffn_bg", "L0_ffn_W1", "L0_ffn_b1", "L0_ffn_W2",
                 "L0_ffn_b2"):
        laid[name] = inputs[name].T if name == "L0_ffn_b1" else inputs[name]
    nc = bacc.Bacc("TRN2", target_bir_lowering=False, num_devices=1)
    arrays, args = {}, []
    for name, a in laid.items():
        a = np.ascontiguousarray(a)
        arrays[f"in_{name}"] = a
        args.append(nc.dram_tensor(f"in_{name}", a.shape, mybir.dt.from_np(a.dtype), kind="ExternalInput").ap())
    shape = (*laid["x"].shape, laid["L0_tok_proj_w"].shape[0])
    out = nc.dram_tensor("out_0", shape, F32, kind="ExternalOutput").ap()
    program(nc, *args, out)
    r = run_bass_kernel_spmd(nc, [arrays], core_ids=[0])
    return r.results[0]["out_0"]
```
